# Optimizing a Trainium2 kernel written in Bass

```python
import numpy as np
import jax
import jax.numpy as jnp

def _softmax(x, axis=-1):
    return jax.nn.softmax(x, axis=axis)

def _gelu(x):
    return jax.nn.gelu(x, approximate=True)

def _silu(x):
    return jax.nn.silu(x)

def _sigmoid(x):
    return jax.nn.sigmoid(x)

def _layernorm(x, axis=-1, eps=1e-05):
    m = jnp.mean(x, axis=axis, keepdims=True)
    v = jnp.var(x, axis=axis, keepdims=True)
    return (x - m) / jnp.sqrt(v + eps)

def _scatter_add(tgt, idx, src, axis=0):
    return tgt.at[idx].add(src)

def _segment_sum(src, seg, n):
    return jax.ops.segment_sum(src, seg, n)
kernel_name = 'mk_hybrid_d4_jaxref_r8_28152b'

def setup_inputs(seed: int=0):
    np.random.seed(seed)
    _w = jnp.asarray

    def _L0_attn_a_setup():
        import jax, jax.numpy as jnp
        import numpy as np
        NUM_HEADS = 16
        NUM_KV_HEADS = 4
        HEAD_DIM = 64
        ROPE_THETA = 10000.0

        def _rope_tables(seq_len, dtype):
            inv_freq = 1.0 / ROPE_THETA ** (jnp.arange(0, HEAD_DIM, 2, dtype=jnp.float32) / HEAD_DIM)
            freqs = jnp.outer(jnp.arange(seq_len, dtype=jnp.float32), inv_freq)
            emb = jnp.concatenate([freqs, freqs], axis=-1)
            return (jnp.cos(emb).astype(dtype), jnp.sin(emb).astype(dtype))

        def _rotate_half(t):
            t1, t2 = (t[..., :HEAD_DIM // 2], t[..., HEAD_DIM // 2:])
            return jnp.concatenate([-t2, t1], axis=-1)
        key = jax.random.key(seed)
        ks = jax.random.split(key, 5)
        B, S, H = (4, 256, 128)
        scale = 1.0 / np.sqrt(H)
        return {'x': jax.random.normal(ks[0], (B, S, H), dtype=jnp.float32), 'wq': jax.random.normal(ks[1], (H, NUM_HEADS * HEAD_DIM), dtype=jnp.float32) * scale, 'wk': jax.random.normal(ks[2], (H, NUM_KV_HEADS * HEAD_DIM), dtype=jnp.float32) * scale, 'wv': jax.random.normal(ks[3], (H, NUM_KV_HEADS * HEAD_DIM), dtype=jnp.float32) * scale, 'wo': jax.random.normal(ks[4], (NUM_HEADS * HEAD_DIM, H), dtype=jnp.float32) * scale}
    _L0_attn_a_in = _L0_attn_a_setup()

    def _L0_attn_b_setup():
        import jax, jax.numpy as jnp
        import numpy as np
        EMB_DIM = 128
        N_HEADS = 16
        HEAD_DIM = 64
        B, S = (4, 256)
        key = jax.random.key(seed)
        k_x, k_qkv, k_out = jax.random.split(key, 3)
        hd = N_HEADS * HEAD_DIM
        x = jax.random.normal(k_x, (B, S, EMB_DIM), dtype=jnp.float32)
        W_qkv = jax.random.normal(k_qkv, (EMB_DIM, 3 * hd), dtype=jnp.float32) * EMB_DIM ** (-0.5)
        W_out = jax.random.normal(k_out, (hd, EMB_DIM), dtype=jnp.float32) * hd ** (-0.5)
        return {'x': x, 'W_qkv': W_qkv, 'W_out': W_out}
    _L0_attn_b_in = _L0_attn_b_setup()

    def _L0_ffn_setup():
        import jax, jax.numpy as jnp
        import numpy as np
        DIM = 128
        DEPTH = 2
        HEADS = 8
        DIM_HEAD = 64
        WINDOW = 64
        INNER = HEADS * DIM_HEAD
        HID = int(DIM * 4 * 2 / 3)
        B, N = (2, 1024)
        QK_SCALE = 8.0

        def shift_token(t):
            t1, t2 = jnp.split(t, 2, axis=-1)
            t2 = jnp.pad(t2, ((0, 0), (1, 0), (0, 0)))[:, :-1]
            return jnp.concatenate([t1, t2], axis=-1)

        def l2norm(t):
            return t / jnp.clip(jnp.linalg.norm(t, axis=-1, keepdims=True), 1e-12)

        def rotate_half(x):
            x1, x2 = jnp.split(x, 2, axis=-1)
            return jnp.concatenate([-x2, x1], axis=-1)

        def rotary_xpos(q, k):
            n = q.shape[-2]
            half_idx = jnp.arange(0, DIM_HEAD, 2, dtype=jnp.float32)
            inv_freq = 1.0 / 10000.0 ** (half_idx / DIM_HEAD)
            t = jnp.arange(n, dtype=jnp.float32)
            freqs = t[:, None] * inv_freq[None, :]
            freqs = jnp.concatenate([freqs, freqs], axis=-1)
            base = (half_idx + 0.4 * DIM_HEAD) / (1.4 * DIM_HEAD)
            power = (t - n // 2) / float(WINDOW // 2)
            scale = base[None, :] ** power[:, None]
            scale = jnp.concatenate([scale, scale], axis=-1)
            cos, sin = (jnp.cos(freqs), jnp.sin(freqs))
            q = q * cos * scale + rotate_half(q) * sin * scale
            k = k * cos / scale + rotate_half(k) * sin / scale
            return (q, k)

        def local_attention(q, k, v):
            b, h, n, d = q.shape
            w = n // WINDOW
            bq = q.reshape(b, h, w, WINDOW, d) * QK_SCALE
            bk = k.reshape(b, h, w, WINDOW, d)
            bv = v.reshape(b, h, w, WINDOW, d)

            def look_around(t):
                p = jnp.pad(t, ((0, 0), (0, 0), (1, 0), (0, 0), (0, 0)))
                return jnp.concatenate([p[:, :, :w], p[:, :, 1:]], axis=3)
            bk, bv = (look_around(bk), look_around(bv))
            bt = jnp.arange(n).reshape(w, WINDOW)
            btp = jnp.pad(bt, ((1, 0), (0, 0)), constant_values=-1)
            btk = jnp.concatenate([btp[:w], btp[1:]], axis=1)
            sim = jnp.einsum('bhwid,bhwjd->bhwij', bq, bk)
            i = bt[:, :, None]
            j = btk[:, None, :]
            mask = (i < j) | (i > j + WINDOW) | (j == -1)
            sim = jnp.where(mask, -jnp.finfo(sim.dtype).max, sim)
            attn = jax.nn.softmax(sim, axis=-1)
            out = jnp.einsum('bhwij,bhwjd->bhwid', attn, bv)
            return out.reshape(b, h, n, d)

        def _layer(x, wqkv, qs, ksc, wo, lg, lb, w1, b1, w2, b2):
            b, n, _ = x.shape
            h = shift_token(x)
            qkv = h @ wqkv
            q, k, v = jnp.split(qkv, 3, axis=-1)
            to_heads = lambda t: t.reshape(b, n, HEADS, DIM_HEAD).transpose(0, 2, 1, 3)
            q, k, v = (to_heads(q), to_heads(k), to_heads(v))
            q = l2norm(q) * qs
            k = l2norm(k) * ksc
            q, k = rotary_xpos(q, k)
            o = local_attention(q, k, v)
            o = o.transpose(0, 2, 1, 3).reshape(b, n, INNER)
            x = x + o @ wo
            h = shift_token(x)
            mu = h.mean(-1, keepdims=True)
            var = h.var(-1, keepdims=True)
            h = (h - mu) / jnp.sqrt(var + 1e-05) * lg + lb
            h = h @ w1 + b1
            a, g = jnp.split(h, 2, axis=-1)
            h = a * jax.nn.gelu(g, approximate=False)
            x = x + h @ w2 + b2
            return x
        key = jax.random.key(seed)
        ks = jax.random.split(key, 6)
        return {'x': jax.random.normal(ks[0], (B, N, DIM), jnp.float32), 'wqkv': jax.random.normal(ks[1], (DEPTH, DIM, 3 * INNER), jnp.float32) * 0.02, 'q_scale': jnp.ones((DEPTH, DIM_HEAD), jnp.float32), 'k_scale': jnp.ones((DEPTH, DIM_HEAD), jnp.float32), 'wo': jax.random.normal(ks[2], (DEPTH, INNER, DIM), jnp.float32) * 0.02, 'ln_g': jnp.ones((DEPTH, DIM), jnp.float32), 'ln_b': jnp.zeros((DEPTH, DIM), jnp.float32), 'w1': jax.random.normal(ks[3], (DEPTH, DIM, 2 * HID), jnp.float32) * 0.02, 'b1': jnp.zeros((DEPTH, 2 * HID), jnp.float32), 'w2': jax.random.normal(ks[4], (DEPTH, HID, DIM), jnp.float32) * 0.02, 'b2': jnp.zeros((DEPTH, DIM), jnp.float32)}
    _L0_ffn_in = _L0_ffn_setup()

    def _L1_attn_a_setup():
        import jax, jax.numpy as jnp
        import numpy as np
        DIM = 128
        NUM_HEADS = 16
        HEAD_DIM = DIM // NUM_HEADS
        SCALE = 1.0 / float(np.sqrt(HEAD_DIM))
        key = jax.random.key(seed)
        kx, kw1, kb1, kw2, kb2 = jax.random.split(key, 5)
        b, l = (2, 256)
        s = 1.0 / np.sqrt(DIM)
        return {'x': jax.random.normal(kx, (b, l, DIM), dtype=jnp.float32), 'w_qkv': jax.random.uniform(kw1, (DIM, 3 * DIM), jnp.float32, -s, s), 'b_qkv': jax.random.uniform(kb1, (3 * DIM,), jnp.float32, -s, s), 'w_proj': jax.random.uniform(kw2, (DIM, DIM), jnp.float32, -s, s), 'b_proj': jax.random.uniform(kb2, (DIM,), jnp.float32, -s, s)}
    _L1_attn_a_in = _L1_attn_a_setup()

    def _L1_attn_b_setup():
        import jax, jax.numpy as jnp
        import numpy as np
        import math
        D_MODEL = 128
        NUM_HEADS = 16
        HEAD_DIM = D_MODEL // NUM_HEADS
        LN_EPS = 1e-05

        def _layer_norm(x, g, b):
            mu = jnp.mean(x, axis=-1, keepdims=True)
            var = jnp.mean(jnp.square(x - mu), axis=-1, keepdims=True)
            return (x - mu) * jax.lax.rsqrt(var + LN_EPS) * g + b

        def _rope_tables(seq_len, dim, dtype):
            inv_freq = 1.0 / 10000.0 ** (jnp.arange(0, dim, 2, dtype=jnp.float32) / dim)
            t = jnp.arange(seq_len, dtype=jnp.float32)
            freqs = t[:, None] * inv_freq[None, :]
            emb = jnp.concatenate([freqs, freqs], axis=-1)
            return (jnp.cos(emb).astype(dtype), jnp.sin(emb).astype(dtype))

        def _rotate_half(x):
            x1, x2 = jnp.split(x, 2, axis=-1)
            return jnp.concatenate([-x2, x1], axis=-1)
        key = jax.random.key(seed)
        ks = jax.random.split(key, 8)
        B, S, D = (2, 256, D_MODEL)
        s_in = 1.0 / math.sqrt(D)
        return {'x': jax.random.normal(ks[0], (B, S, D), jnp.float32), 'ln1_g': jnp.ones((D,), jnp.float32), 'ln1_b': jnp.zeros((D,), jnp.float32), 'Wqkv': jax.random.normal(ks[1], (D, 3 * D), jnp.float32) * s_in, 'bqkv': jnp.zeros((3 * D,), jnp.float32), 'Wo': jax.random.normal(ks[2], (D, D), jnp.float32) * s_in, 'bo': jnp.zeros((D,), jnp.float32), 'ln2_g': jnp.ones((D,), jnp.float32), 'ln2_b': jnp.zeros((D,), jnp.float32), 'W1': jax.random.normal(ks[3], (D, 4 * D), jnp.float32) * s_in, 'b1': jnp.zeros((4 * D,), jnp.float32), 'W2': jax.random.normal(ks[4], (4 * D, D), jnp.float32) / math.sqrt(4 * D), 'b2': jnp.zeros((D,), jnp.float32)}
    _L1_attn_b_in = _L1_attn_b_setup()

    def _L1_ffn_setup():
        import jax, jax.numpy as jnp
        import numpy as np
        D = 128
        I = 64
        E = 32
        K = 4
        T = 2 * 256
        C = 2 * T * K // E
        key = jax.random.key(seed)
        ks = jax.random.split(key, 9)
        bf = jnp.bfloat16
        std = 0.02
        x = jax.random.normal(ks[0], (2, 256, D), dtype=jnp.float32).astype(bf)
        gate_w = (std * jax.random.normal(ks[1], (E, D), dtype=jnp.float32)).astype(bf)
        bias = jnp.zeros((E,), jnp.float32)
        W1 = (std * jax.random.normal(ks[2], (E, D, I), dtype=jnp.float32)).astype(bf)
        W3 = (std * jax.random.normal(ks[3], (E, D, I), dtype=jnp.float32)).astype(bf)
        W2 = (std * jax.random.normal(ks[4], (E, I, D), dtype=jnp.float32)).astype(bf)
        sw1 = (std * jax.random.normal(ks[5], (I, D), dtype=jnp.float32)).astype(bf)
        sw3 = (std * jax.random.normal(ks[6], (I, D), dtype=jnp.float32)).astype(bf)
        sw2 = (std * jax.random.normal(ks[7], (D, I), dtype=jnp.float32)).astype(bf)
        return {'x': x, 'gate_w': gate_w, 'bias': bias, 'W1': W1, 'W3': W3, 'W2': W2, 'sw1': sw1, 'sw3': sw3, 'sw2': sw2}
    _L1_ffn_in = _L1_ffn_setup()

    def _L2_attn_a_setup():
        import jax, jax.numpy as jnp
        import numpy as np
        import math
        B, S, D_IN, D_KQ, D_OUT = (4, 256, 128, 128, 128)
        key = jax.random.key(seed)
        ks = jax.random.split(key, 7)
        sc = 0.02
        return {'x': jax.random.normal(ks[0], (B, S, D_IN), jnp.float32), 'Wq': jax.random.normal(ks[1], (D_KQ, D_IN), jnp.float32) * sc, 'bq': jax.random.normal(ks[2], (D_KQ,), jnp.float32) * sc, 'Wk': jax.random.normal(ks[3], (D_KQ, D_IN), jnp.float32) * sc, 'bk': jax.random.normal(ks[4], (D_KQ,), jnp.float32) * sc, 'Wv': jax.random.normal(ks[5], (D_OUT, D_IN), jnp.float32) * sc, 'bv': jax.random.normal(ks[6], (D_OUT,), jnp.float32) * sc}
    _L2_attn_a_in = _L2_attn_a_setup()

    def _L2_attn_b_setup():
        import jax, jax.numpy as jnp
        import numpy as np
        import math
        DIM = 128
        NUM_HEADS = 16
        HEAD_DIM = DIM // NUM_HEADS
        B, S = (2, 256)
        key = jax.random.key(seed)
        ks = jax.random.split(key, 9)
        sc = 0.02
        return {'x': jax.random.normal(ks[0], (B, S, DIM), jnp.float32), 'Wq': jax.random.normal(ks[1], (DIM, DIM), jnp.float32) * sc, 'bq': jax.random.normal(ks[2], (DIM,), jnp.float32) * sc, 'Wk': jax.random.normal(ks[3], (DIM, DIM), jnp.float32) * sc, 'bk': jax.random.normal(ks[4], (DIM,), jnp.float32) * sc, 'Wv': jax.random.normal(ks[5], (DIM, DIM), jnp.float32) * sc, 'bv': jax.random.normal(ks[6], (DIM,), jnp.float32) * sc, 'Wo': jax.random.normal(ks[7], (DIM, DIM), jnp.float32) * sc, 'bo': jax.random.normal(ks[8], (DIM,), jnp.float32) * sc}
    _L2_attn_b_in = _L2_attn_b_setup()

    def _L2_ffn_setup():
        import jax, jax.numpy as jnp
        import numpy as np
        LORA_DIM = 16
        LORA_TOKEN_INDEX = 1
        B, S, D, H = (4, 256, 128, 512)
        key = jax.random.key(seed)
        ks = jax.random.split(key, 6)
        x = jax.random.normal(ks[0], (B, S, D), dtype=jnp.float32)
        W1 = jax.random.normal(ks[1], (H, D), dtype=jnp.float32) * 0.02
        b1 = jnp.zeros((H,), dtype=jnp.float32)
        W2 = jax.random.normal(ks[2], (D, H), dtype=jnp.float32) * 0.02
        b2 = jnp.zeros((D,), dtype=jnp.float32)
        scale = jnp.asarray(0.001, dtype=jnp.float32)
        return {'x': x, 'W1': W1, 'b1': b1, 'W2': W2, 'b2': b2, 'scale': scale}
    _L2_ffn_in = _L2_ffn_setup()

    def _L3_attn_a_setup():
        import jax, jax.numpy as jnp
        import numpy as np
        B, S, D, DV = (1, 512, 128, 128)
        key = jax.random.key(seed)
        kq, kk, kv, ks, kp = jax.random.split(key, 5)
        return {'q': jax.random.normal(kq, (B, S, D), dtype=jnp.float32), 'k': jax.random.normal(kk, (B, S, D), dtype=jnp.float32), 'v': jax.random.normal(kv, (B, S, DV), dtype=jnp.float32), 'scale_factor': jax.random.normal(ks, (1,), dtype=jnp.float32), 'dropout_p': jax.random.uniform(kp, (1,), dtype=jnp.float32)}
    _L3_attn_a_in = _L3_attn_a_setup()

    def _L3_attn_b_setup():
        import jax, jax.numpy as jnp
        import numpy as np
        from math import sqrt
        N_HEAD = 16
        W_SCALE = 0.02

        def _reference_tuple_inner(x, W_dq, W_uq, W_dkv, W_uk, W_uv, W_o):
            B, T, C = x.shape
            nh = N_HEAD
            hs = C // nh
            n_kvl = W_dkv.shape[0]
            k_eff = (W_dq.T @ W_uq.T @ W_uk).reshape(nh, hs, n_kvl)
            v_eff = jnp.transpose((W_uv.T @ W_o.T).reshape(n_kvl, nh, hs), (1, 0, 2))
            c_kv = x @ W_dkv.T
            q = x @ W_dq.T @ W_uq.T
            q = q.reshape(B, T, nh, hs)
            q_lat = jnp.einsum('bqhd,hdl->bhql', q, k_eff)
            attn = jnp.einsum('bhql,bkl->bhqk', q_lat, c_kv) / sqrt(hs)
            causal = jnp.tril(jnp.ones((T, T), dtype=bool))
            attn = jnp.where(causal[None, None], attn, -jnp.inf)
            attn = jax.nn.softmax(attn, axis=-1)
            y_lat = jnp.einsum('bhqk,bkl->bhql', attn, c_kv)
            y = jnp.einsum('bhql,hld->bqhd', y_lat, v_eff).reshape(B, T, C)
            return (y, c_kv)
        key = jax.random.key(seed)
        ks = jax.random.split(key, 7)
        B, T, C = (2, 256, 128)
        QL, KVL = (64, 64)
        return {'x': jax.random.normal(ks[0], (B, T, C), dtype=jnp.float32), 'W_dq': jax.random.normal(ks[1], (QL, C), dtype=jnp.float32) * W_SCALE, 'W_uq': jax.random.normal(ks[2], (C, QL), dtype=jnp.float32) * W_SCALE, 'W_dkv': jax.random.normal(ks[3], (KVL, C), dtype=jnp.float32) * W_SCALE, 'W_uk': jax.random.normal(ks[4], (C, KVL), dtype=jnp.float32) * W_SCALE, 'W_uv': jax.random.normal(ks[5], (C, KVL), dtype=jnp.float32) * W_SCALE, 'W_o': jax.random.normal(ks[6], (C, C), dtype=jnp.float32) * W_SCALE}
    _L3_attn_b_in = _L3_attn_b_setup()

    def _L3_ffn_setup():
        import jax, jax.numpy as jnp
        import numpy as np
        LATENT = 128
        LEAF_W = 64
        DEPTH = 4
        N_LEAVES = 2 ** DEPTH
        N_NODES = 2 ** DEPTH - 1
        B, S = (4, 256)

        def _fff_params(key, prefix):
            ks = jax.random.split(key, 4)
            d, h, l, n = (LATENT, LEAF_W, N_LEAVES, N_NODES)
            s_in = 1.0 / np.sqrt(d).astype(np.float32)
            s_h = 1.0 / np.sqrt(h).astype(np.float32)
            return {f'{prefix}_node_w': jax.random.normal(ks[0], (n, d), jnp.float32) * s_in, f'{prefix}_node_b': jax.random.normal(ks[1], (n,), jnp.float32) * s_in, f'{prefix}_w1': jax.random.normal(ks[2], (l, d, h), jnp.float32) * s_in, f'{prefix}_b1': jnp.zeros((l, h), jnp.float32), f'{prefix}_w2': jax.random.normal(ks[3], (l, h, d), jnp.float32) * s_h, f'{prefix}_b2': jnp.zeros((l, d), jnp.float32)}

        def _fff(x, node_w, node_b, w1, b1, w2, b2):
            Bx, Sx, D = x.shape
            xf = x.reshape(-1, D)
            N = xf.shape[0]
            cur = jnp.zeros((N,), jnp.int32)
            for _ in range(DEPTH):
                pw = node_w[cur]
                score = jnp.einsum('nd,nd->n', xf, pw) + node_b[cur]
                cur = 2 * cur + 1 + (score >= 0).astype(jnp.int32)
            leaf = cur - N_NODES
            sel = jax.nn.one_hot(leaf, N_LEAVES, dtype=xf.dtype)
            hidden_all = jax.nn.relu(jnp.einsum('nd,ldh->lnh', xf, w1) + b1[:, None, :])
            hidden = hidden_all * sel.T[:, :, None]
            out = jnp.einsum('lnh,lho->no', hidden, w2) + sel @ b2
            return out.reshape(Bx, Sx, D)
        key = jax.random.key(seed)
        kx, kq, kk, kv = jax.random.split(key, 4)
        inp = {'x': jax.random.normal(kx, (B, S, LATENT), jnp.float32)}
        inp.update(_fff_params(kq, 'q'))
        inp.update(_fff_params(kk, 'k'))
        inp.update(_fff_params(kv, 'v'))
        return inp
    _L3_ffn_in = _L3_ffn_setup()
    _d = {'L0_attn_a_x': _L0_attn_a_in['x'], 'L0_attn_a_wq': _L0_attn_a_in['wq'], 'L0_attn_a_wk': _L0_attn_a_in['wk'], 'L0_attn_a_wv': _L0_attn_a_in['wv'], 'L0_attn_a_wo': _L0_attn_a_in['wo'], 'L0_attn_b_W_qkv': _L0_attn_b_in['W_qkv'], 'L0_attn_b_W_out': _L0_attn_b_in['W_out'], 'L0_ffn_wqkv': _L0_ffn_in['wqkv'], 'L0_ffn_q_scale': _L0_ffn_in['q_scale'], 'L0_ffn_k_scale': _L0_ffn_in['k_scale'], 'L0_ffn_wo': _L0_ffn_in['wo'], 'L0_ffn_ln_g': _L0_ffn_in['ln_g'], 'L0_ffn_ln_b': _L0_ffn_in['ln_b'], 'L0_ffn_w1': _L0_ffn_in['w1'], 'L0_ffn_b1': _L0_ffn_in['b1'], 'L0_ffn_w2': _L0_ffn_in['w2'], 'L0_ffn_b2': _L0_ffn_in['b2'], 'L1_attn_a_w_qkv': _L1_attn_a_in['w_qkv'], 'L1_attn_a_b_qkv': _L1_attn_a_in['b_qkv'], 'L1_attn_a_w_proj': _L1_attn_a_in['w_proj'], 'L1_attn_a_b_proj': _L1_attn_a_in['b_proj'], 'L1_attn_b_ln1_g': _L1_attn_b_in['ln1_g'], 'L1_attn_b_ln1_b': _L1_attn_b_in['ln1_b'], 'L1_attn_b_Wqkv': _L1_attn_b_in['Wqkv'], 'L1_attn_b_bqkv': _L1_attn_b_in['bqkv'], 'L1_attn_b_Wo': _L1_attn_b_in['Wo'], 'L1_attn_b_bo': _L1_attn_b_in['bo'], 'L1_attn_b_ln2_g': _L1_attn_b_in['ln2_g'], 'L1_attn_b_ln2_b': _L1_attn_b_in['ln2_b'], 'L1_attn_b_W1': _L1_attn_b_in['W1'], 'L1_attn_b_b1': _L1_attn_b_in['b1'], 'L1_attn_b_W2': _L1_attn_b_in['W2'], 'L1_attn_b_b2': _L1_attn_b_in['b2'], 'L1_ffn_gate_w': _L1_ffn_in['gate_w'], 'L1_ffn_bias': _L1_ffn_in['bias'], 'L1_ffn_W1': _L1_ffn_in['W1'], 'L1_ffn_W3': _L1_ffn_in['W3'], 'L1_ffn_W2': _L1_ffn_in['W2'], 'L1_ffn_sw1': _L1_ffn_in['sw1'], 'L1_ffn_sw3': _L1_ffn_in['sw3'], 'L1_ffn_sw2': _L1_ffn_in['sw2'], 'L2_attn_a_Wq': _L2_attn_a_in['Wq'], 'L2_attn_a_bq': _L2_attn_a_in['bq'], 'L2_attn_a_Wk': _L2_attn_a_in['Wk'], 'L2_attn_a_bk': _L2_attn_a_in['bk'], 'L2_attn_a_Wv': _L2_attn_a_in['Wv'], 'L2_attn_a_bv': _L2_attn_a_in['bv'], 'L2_attn_b_Wq': _L2_attn_b_in['Wq'], 'L2_attn_b_bq': _L2_attn_b_in['bq'], 'L2_attn_b_Wk': _L2_attn_b_in['Wk'], 'L2_attn_b_bk': _L2_attn_b_in['bk'], 'L2_attn_b_Wv': _L2_attn_b_in['Wv'], 'L2_attn_b_bv': _L2_attn_b_in['bv'], 'L2_attn_b_Wo': _L2_attn_b_in['Wo'], 'L2_attn_b_bo': _L2_attn_b_in['bo'], 'L2_ffn_W1': _L2_ffn_in['W1'], 'L2_ffn_b1': _L2_ffn_in['b1'], 'L2_ffn_W2': _L2_ffn_in['W2'], 'L2_ffn_b2': _L2_ffn_in['b2'], 'L2_ffn_scale': _L2_ffn_in['scale'], 'L3_attn_a_k': _L3_attn_a_in['k'], 'L3_attn_a_v': _L3_attn_a_in['v'], 'L3_attn_a_scale_factor': _L3_attn_a_in['scale_factor'], 'L3_attn_a_dropout_p': _L3_attn_a_in['dropout_p'], 'L3_attn_b_W_dq': _L3_attn_b_in['W_dq'], 'L3_attn_b_W_uq': _L3_attn_b_in['W_uq'], 'L3_attn_b_W_dkv': _L3_attn_b_in['W_dkv'], 'L3_attn_b_W_uk': _L3_attn_b_in['W_uk'], 'L3_attn_b_W_uv': _L3_attn_b_in['W_uv'], 'L3_attn_b_W_o': _L3_attn_b_in['W_o'], 'L3_ffn_q_node_w': _L3_ffn_in['q_node_w'], 'L3_ffn_q_node_b': _L3_ffn_in['q_node_b'], 'L3_ffn_q_w1': _L3_ffn_in['q_w1'], 'L3_ffn_q_b1': _L3_ffn_in['q_b1'], 'L3_ffn_q_w2': _L3_ffn_in['q_w2'], 'L3_ffn_q_b2': _L3_ffn_in['q_b2'], 'L3_ffn_k_node_w': _L3_ffn_in['k_node_w'], 'L3_ffn_k_node_b': _L3_ffn_in['k_node_b'], 'L3_ffn_k_w1': _L3_ffn_in['k_w1'], 'L3_ffn_k_b1': _L3_ffn_in['k_b1'], 'L3_ffn_k_w2': _L3_ffn_in['k_w2'], 'L3_ffn_k_b2': _L3_ffn_in['k_b2'], 'L3_ffn_v_node_w': _L3_ffn_in['v_node_w'], 'L3_ffn_v_node_b': _L3_ffn_in['v_node_b'], 'L3_ffn_v_w1': _L3_ffn_in['v_w1'], 'L3_ffn_v_b1': _L3_ffn_in['v_b1'], 'L3_ffn_v_w2': _L3_ffn_in['v_w2'], 'L3_ffn_v_b2': _L3_ffn_in['v_b2']}
    _x0 = _d['L0_attn_a_x']
    _d['L0_attn_a_x'] = jax.random.normal(jax.random.fold_in(jax.random.key(seed), 1), (2, 1024, 128), dtype=_x0.dtype)
    del _x0
    return _d

def reference(L0_attn_a_x, L0_attn_a_wq, L0_attn_a_wk, L0_attn_a_wv, L0_attn_a_wo, L0_attn_b_W_qkv, L0_attn_b_W_out, L0_ffn_wqkv, L0_ffn_q_scale, L0_ffn_k_scale, L0_ffn_wo, L0_ffn_ln_g, L0_ffn_ln_b, L0_ffn_w1, L0_ffn_b1, L0_ffn_w2, L0_ffn_b2, L1_attn_a_w_qkv, L1_attn_a_b_qkv, L1_attn_a_w_proj, L1_attn_a_b_proj, L1_attn_b_ln1_g, L1_attn_b_ln1_b, L1_attn_b_Wqkv, L1_attn_b_bqkv, L1_attn_b_Wo, L1_attn_b_bo, L1_attn_b_ln2_g, L1_attn_b_ln2_b, L1_attn_b_W1, L1_attn_b_b1, L1_attn_b_W2, L1_attn_b_b2, L1_ffn_gate_w, L1_ffn_bias, L1_ffn_W1, L1_ffn_W3, L1_ffn_W2, L1_ffn_sw1, L1_ffn_sw3, L1_ffn_sw2, L2_attn_a_Wq, L2_attn_a_bq, L2_attn_a_Wk, L2_attn_a_bk, L2_attn_a_Wv, L2_attn_a_bv, L2_attn_b_Wq, L2_attn_b_bq, L2_attn_b_Wk, L2_attn_b_bk, L2_attn_b_Wv, L2_attn_b_bv, L2_attn_b_Wo, L2_attn_b_bo, L2_ffn_W1, L2_ffn_b1, L2_ffn_W2, L2_ffn_b2, L2_ffn_scale, L3_attn_a_k, L3_attn_a_v, L3_attn_a_scale_factor, L3_attn_a_dropout_p, L3_attn_b_W_dq, L3_attn_b_W_uq, L3_attn_b_W_dkv, L3_attn_b_W_uk, L3_attn_b_W_uv, L3_attn_b_W_o, L3_ffn_q_node_w, L3_ffn_q_node_b, L3_ffn_q_w1, L3_ffn_q_b1, L3_ffn_q_w2, L3_ffn_q_b2, L3_ffn_k_node_w, L3_ffn_k_node_b, L3_ffn_k_w1, L3_ffn_k_b1, L3_ffn_k_w2, L3_ffn_k_b2, L3_ffn_v_node_w, L3_ffn_v_node_b, L3_ffn_v_w1, L3_ffn_v_b1, L3_ffn_v_w2, L3_ffn_v_b2):

    def _L0_attn_a_ref(x, wq, wk, wv, wo):
        import jax, jax.numpy as jnp
        import numpy as np
        NUM_HEADS = 16
        NUM_KV_HEADS = 4
        HEAD_DIM = 64
        ROPE_THETA = 10000.0

        def _rope_tables(seq_len, dtype):
            inv_freq = 1.0 / ROPE_THETA ** (jnp.arange(0, HEAD_DIM, 2, dtype=jnp.float32) / HEAD_DIM)
            freqs = jnp.outer(jnp.arange(seq_len, dtype=jnp.float32), inv_freq)
            emb = jnp.concatenate([freqs, freqs], axis=-1)
            return (jnp.cos(emb).astype(dtype), jnp.sin(emb).astype(dtype))

        def _rotate_half(t):
            t1, t2 = (t[..., :HEAD_DIM // 2], t[..., HEAD_DIM // 2:])
            return jnp.concatenate([-t2, t1], axis=-1)
        B, S, H = x.shape
        q = (x @ wq).reshape(B, S, NUM_HEADS, HEAD_DIM).transpose(0, 2, 1, 3)
        k = (x @ wk).reshape(B, S, NUM_KV_HEADS, HEAD_DIM).transpose(0, 2, 1, 3)
        v = (x @ wv).reshape(B, S, NUM_KV_HEADS, HEAD_DIM).transpose(0, 2, 1, 3)
        cos, sin = _rope_tables(S, x.dtype)
        cos = cos[None, None]
        sin = sin[None, None]
        q = q * cos + _rotate_half(q) * sin
        k = k * cos + _rotate_half(k) * sin
        groups = NUM_HEADS // NUM_KV_HEADS
        k = jnp.repeat(k, groups, axis=1)
        v = jnp.repeat(v, groups, axis=1)
        scores = jnp.einsum('bhqd,bhkd->bhqk', q, k) / jnp.sqrt(jnp.float32(HEAD_DIM)).astype(x.dtype)
        causal = jnp.triu(jnp.ones((S, S), dtype=bool), k=1)
        scores = jnp.where(causal[None, None], jnp.finfo(scores.dtype).min, scores)
        attn = jax.nn.softmax(scores, axis=-1)
        out = jnp.einsum('bhqk,bhkd->bhqd', attn, v)
        out = out.transpose(0, 2, 1, 3).reshape(B, S, NUM_HEADS * HEAD_DIM)
        return out @ wo

    def _L0_attn_b_ref(x, W_qkv, W_out):
        import jax, jax.numpy as jnp
        import numpy as np
        EMB_DIM = 128
        N_HEADS = 16
        HEAD_DIM = 64
        B, S = (4, 256)
        Bv, Sv, _ = x.shape
        hd = N_HEADS * HEAD_DIM
        scale = HEAD_DIM ** (-0.5)
        qkv = x @ W_qkv
        q, k, v = jnp.split(qkv, 3, axis=-1)
        reshape_heads = lambda t: t.reshape(Bv, Sv, N_HEADS, HEAD_DIM).transpose(0, 2, 1, 3)
        q, k, v = (reshape_heads(q), reshape_heads(k), reshape_heads(v))
        scores = scale * jnp.einsum('bhsd,bhtd->bhst', q, k)
        a = jax.nn.softmax(scores, axis=-1)
        z = jnp.einsum('bhst,bhtd->bhsd', a, v)
        z = z.reshape(Bv, Sv, hd)
        return z @ W_out

    def _L0_ffn_ref(x, wqkv, q_scale, k_scale, wo, ln_g, ln_b, w1, b1, w2, b2):
        import jax, jax.numpy as jnp
        import numpy as np
        DIM = 128
        DEPTH = 2
        HEADS = 8
        DIM_HEAD = 64
        WINDOW = 64
        INNER = HEADS * DIM_HEAD
        HID = int(DIM * 4 * 2 / 3)
        B, N = (2, 1024)
        QK_SCALE = 8.0

        def shift_token(t):
            t1, t2 = jnp.split(t, 2, axis=-1)
            t2 = jnp.pad(t2, ((0, 0), (1, 0), (0, 0)))[:, :-1]
            return jnp.concatenate([t1, t2], axis=-1)

        def l2norm(t):
            return t / jnp.clip(jnp.linalg.norm(t, axis=-1, keepdims=True), 1e-12)

        def rotate_half(x):
            x1, x2 = jnp.split(x, 2, axis=-1)
            return jnp.concatenate([-x2, x1], axis=-1)

        def rotary_xpos(q, k):
            n = q.shape[-2]
            half_idx = jnp.arange(0, DIM_HEAD, 2, dtype=jnp.float32)
            inv_freq = 1.0 / 10000.0 ** (half_idx / DIM_HEAD)
            t = jnp.arange(n, dtype=jnp.float32)
            freqs = t[:, None] * inv_freq[None, :]
            freqs = jnp.concatenate([freqs, freqs], axis=-1)
            base = (half_idx + 0.4 * DIM_HEAD) / (1.4 * DIM_HEAD)
            power = (t - n // 2) / float(WINDOW // 2)
            scale = base[None, :] ** power[:, None]
            scale = jnp.concatenate([scale, scale], axis=-1)
            cos, sin = (jnp.cos(freqs), jnp.sin(freqs))
            q = q * cos * scale + rotate_half(q) * sin * scale
            k = k * cos / scale + rotate_half(k) * sin / scale
            return (q, k)

        def local_attention(q, k, v):
            b, h, n, d = q.shape
            w = n // WINDOW
            bq = q.reshape(b, h, w, WINDOW, d) * QK_SCALE
            bk = k.reshape(b, h, w, WINDOW, d)
            bv = v.reshape(b, h, w, WINDOW, d)

            def look_around(t):
                p = jnp.pad(t, ((0, 0), (0, 0), (1, 0), (0, 0), (0, 0)))
                return jnp.concatenate([p[:, :, :w], p[:, :, 1:]], axis=3)
            bk, bv = (look_around(bk), look_around(bv))
            bt = jnp.arange(n).reshape(w, WINDOW)
            btp = jnp.pad(bt, ((1, 0), (0, 0)), constant_values=-1)
            btk = jnp.concatenate([btp[:w], btp[1:]], axis=1)
            sim = jnp.einsum('bhwid,bhwjd->bhwij', bq, bk)
            i = bt[:, :, None]
            j = btk[:, None, :]
            mask = (i < j) | (i > j + WINDOW) | (j == -1)
            sim = jnp.where(mask, -jnp.finfo(sim.dtype).max, sim)
            attn = jax.nn.softmax(sim, axis=-1)
            out = jnp.einsum('bhwij,bhwjd->bhwid', attn, bv)
            return out.reshape(b, h, n, d)

        def _layer(x, wqkv, qs, ksc, wo, lg, lb, w1, b1, w2, b2):
            b, n, _ = x.shape
            h = shift_token(x)
            qkv = h @ wqkv
            q, k, v = jnp.split(qkv, 3, axis=-1)
            to_heads = lambda t: t.reshape(b, n, HEADS, DIM_HEAD).transpose(0, 2, 1, 3)
            q, k, v = (to_heads(q), to_heads(k), to_heads(v))
            q = l2norm(q) * qs
            k = l2norm(k) * ksc
            q, k = rotary_xpos(q, k)
            o = local_attention(q, k, v)
            o = o.transpose(0, 2, 1, 3).reshape(b, n, INNER)
            x = x + o @ wo
            h = shift_token(x)
            mu = h.mean(-1, keepdims=True)
            var = h.var(-1, keepdims=True)
            h = (h - mu) / jnp.sqrt(var + 1e-05) * lg + lb
            h = h @ w1 + b1
            a, g = jnp.split(h, 2, axis=-1)
            h = a * jax.nn.gelu(g, approximate=False)
            x = x + h @ w2 + b2
            return x
        for l in range(DEPTH):
            x = _layer(x, wqkv[l], q_scale[l], k_scale[l], wo[l], ln_g[l], ln_b[l], w1[l], b1[l], w2[l], b2[l])
        return x

    def _L1_attn_a_ref(x, w_qkv, b_qkv, w_proj, b_proj):
        import jax, jax.numpy as jnp
        import numpy as np
        DIM = 128
        NUM_HEADS = 16
        HEAD_DIM = DIM // NUM_HEADS
        SCALE = 1.0 / float(np.sqrt(HEAD_DIM))
        b, l, c = x.shape
        n, d = (NUM_HEADS, HEAD_DIM)
        qkv = x @ w_qkv + b_qkv
        qkv = qkv.reshape(b, l, 3 * n, d)
        q, k, v = (qkv[:, :, :n], qkv[:, :, n:2 * n], qkv[:, :, 2 * n:])
        attn = SCALE * jnp.einsum('binc,bjnc->bnij', q, k)
        attn = jax.nn.softmax(attn.astype(jnp.float32), axis=-1).astype(q.dtype)
        out = jnp.einsum('bnij,bjnc->binc', attn, v)
        out = out.reshape(b, l, c)
        return out @ w_proj + b_proj

    def _L1_attn_b_ref(x, ln1_g, ln1_b, Wqkv, bqkv, Wo, bo, ln2_g, ln2_b, W1, b1, W2, b2):
        import jax, jax.numpy as jnp
        import numpy as np
        import math
        D_MODEL = 128
        NUM_HEADS = 16
        HEAD_DIM = D_MODEL // NUM_HEADS
        LN_EPS = 1e-05

        def _layer_norm(x, g, b):
            mu = jnp.mean(x, axis=-1, keepdims=True)
            var = jnp.mean(jnp.square(x - mu), axis=-1, keepdims=True)
            return (x - mu) * jax.lax.rsqrt(var + LN_EPS) * g + b

        def _rope_tables(seq_len, dim, dtype):
            inv_freq = 1.0 / 10000.0 ** (jnp.arange(0, dim, 2, dtype=jnp.float32) / dim)
            t = jnp.arange(seq_len, dtype=jnp.float32)
            freqs = t[:, None] * inv_freq[None, :]
            emb = jnp.concatenate([freqs, freqs], axis=-1)
            return (jnp.cos(emb).astype(dtype), jnp.sin(emb).astype(dtype))

        def _rotate_half(x):
            x1, x2 = jnp.split(x, 2, axis=-1)
            return jnp.concatenate([-x2, x1], axis=-1)
        B, S, D = x.shape
        H, hd = (NUM_HEADS, HEAD_DIM)
        normed = _layer_norm(x, ln1_g, ln1_b)
        qkv = (normed @ Wqkv + bqkv).reshape(B, S, 3, H, hd)
        qkv = jnp.transpose(qkv, (2, 0, 3, 1, 4))
        q, k, v = (qkv[0], qkv[1], qkv[2])
        cos, sin = _rope_tables(S, hd, q.dtype)
        cos = cos[None, None, :, :]
        sin = sin[None, None, :, :]
        q = q * cos + _rotate_half(q) * sin
        k = k * cos + _rotate_half(k) * sin
        scores = jnp.einsum('bhqd,bhkd->bhqk', q, k) / math.sqrt(hd)
        causal = jnp.triu(jnp.ones((S, S), dtype=bool), k=1)
        scores = jnp.where(causal[None, None], -jnp.inf, scores)
        attn = jax.nn.softmax(scores, axis=-1)
        attn_out = jnp.einsum('bhqk,bhkd->bhqd', attn, v)
        attn_out = jnp.transpose(attn_out, (0, 2, 1, 3)).reshape(B, S, D)
        attn_out = attn_out @ Wo + bo
        x = x + attn_out
        h = _layer_norm(x, ln2_g, ln2_b)
        h = jax.nn.gelu(h @ W1 + b1, approximate=False) @ W2 + b2
        return x + h

    def _L1_ffn_ref(x, gate_w, bias, W1, W3, W2, sw1, sw3, sw2):
        import jax, jax.numpy as jnp
        import numpy as np
        D = 128
        I = 64
        E = 32
        K = 4
        T = 2 * 256
        C = 2 * T * K // E
        X = x.reshape(-1, D)
        logits = (X @ gate_w.T).astype(jnp.float32)
        scores = jax.nn.sigmoid(logits)
        _, idx = jax.lax.top_k(scores + bias[None, :], K)
        w = jnp.take_along_axis(scores, idx, axis=-1)
        w = w / jnp.clip(jnp.sum(w, axis=-1, keepdims=True), 1e-12, None)
        w = w.astype(x.dtype)
        eid = idx.reshape(-1)
        onehot = (eid[:, None] == jnp.arange(E)[None, :]).astype(jnp.int32)
        pos = jnp.take_along_axis(jnp.cumsum(onehot, axis=0) - 1, eid[:, None], axis=1)[:, 0]
        valid = pos < C
        posc = jnp.minimum(pos, C - 1)
        Xrep = jnp.repeat(X, K, axis=0)
        xe = jnp.zeros((E, C, D), x.dtype).at[eid, posc].add(jnp.where(valid[:, None], Xrep, jnp.zeros((), x.dtype)))
        h = jax.nn.silu(jnp.einsum('ecd,edi->eci', xe, W1)) * jnp.einsum('ecd,edi->eci', xe, W3)
        ye = jnp.einsum('eci,eid->ecd', h, W2)
        gflat = jnp.where(valid, w.reshape(-1), jnp.zeros((), x.dtype))
        yrows = ye[eid, posc] * gflat[:, None]
        out = yrows.reshape(-1, K, D).sum(axis=1)
        out = out + jax.nn.silu(X @ sw1.T) * (X @ sw3.T) @ sw2.T
        return out.reshape(x.shape)

    def _L2_attn_a_ref(x, Wq, bq, Wk, bk, Wv, bv):
        import jax, jax.numpy as jnp
        import numpy as np
        import math
        B, S, D_IN, D_KQ, D_OUT = (4, 256, 128, 128, 128)
        Q = jnp.einsum('bsd,kd->bsk', x, Wq) + bq
        K = jnp.einsum('bsd,kd->bsk', x, Wk) + bk
        V = jnp.einsum('bsd,od->bso', x, Wv) + bv
        scale = 1.0 / math.sqrt(D_KQ)
        attn = jnp.einsum('bqk,bsk->bqs', Q, K) * scale
        s = attn.shape[-1]
        causal = jnp.tril(jnp.ones((s, s), dtype=bool))
        attn = jnp.where(causal[None, :, :], attn, -jnp.inf)
        attn = jax.nn.softmax(attn, axis=-1)
        Z = jnp.einsum('bqs,bso->bqo', attn, V)
        return Z

    def _L2_attn_b_ref(x, Wq, bq, Wk, bk, Wv, bv, Wo, bo):
        import jax, jax.numpy as jnp
        import numpy as np
        import math
        DIM = 128
        NUM_HEADS = 16
        HEAD_DIM = DIM // NUM_HEADS
        B, S = (2, 256)
        b, s, d = x.shape
        h, hd = (NUM_HEADS, HEAD_DIM)

        def split_heads(t):
            return t.reshape(b, s, h, hd).transpose(0, 2, 1, 3)
        q = split_heads(x @ Wq + bq)
        k = split_heads(x @ Wk + bk)
        v = split_heads(x @ Wv + bv)
        scores = jnp.einsum('bhqd,bhkd->bhqk', q, k) / math.sqrt(hd)
        causal = jnp.tril(jnp.ones((s, s), dtype=bool))
        scores = jnp.where(causal[None, None], scores, jnp.asarray(-10000.0, scores.dtype))
        probs = jax.nn.softmax(scores, axis=-1)
        ctx = jnp.einsum('bhqk,bhkd->bhqd', probs, v)
        ctx = ctx.transpose(0, 2, 1, 3).reshape(b, s, d)
        return ctx @ Wo + bo

    def _L2_ffn_ref(x, W1, b1, W2, b2, scale):
        import jax, jax.numpy as jnp
        import numpy as np
        LORA_DIM = 16
        LORA_TOKEN_INDEX = 1
        B, S, D, H = (4, 256, 128, 512)
        Bx, Sx, Dx = x.shape
        Hx = W1.shape[0]
        lt = jax.lax.dynamic_slice_in_dim(x, LORA_TOKEN_INDEX, LORA_DIM, axis=1)
        even = lt[:, ::2, :]
        odd = lt[:, 1::2, :]
        m1 = (even[:, :4, :, None] * odd[:, :4, None, :]).reshape(Bx, Hx, Dx)
        m2 = (even[:, 4:, :, None] * odd[:, 4:, None, :]).reshape(Bx, Dx, Hx)
        h = jnp.einsum('bsd,hd->bsh', x, W1) + scale * jnp.einsum('bsd,bhd->bsh', x, m1) + b1
        h = jax.nn.gelu(h, approximate=False)
        out = jnp.einsum('bsh,oh->bso', h, W2) + scale * jnp.einsum('bsh,boh->bso', h, m2) + b2
        return out

    def _L3_attn_a_ref(q, k, v, scale_factor, dropout_p):
        import jax, jax.numpy as jnp
        import numpy as np
        B, S, D, DV = (1, 512, 128, 128)
        b, s, d = q.shape
        step = s // 4
        scale = q[:, ::step].reshape(b, -1)
        qk = jnp.einsum('bsd,btd->bst', q, k)
        scaled_qk = qk * scale[:, None, :]
        softmax_qk = jax.nn.softmax(scaled_qk, axis=-1)
        return jnp.einsum('bst,btv->bsv', softmax_qk, v)

    def _L3_attn_b_ref(x, W_dq, W_uq, W_dkv, W_uk, W_uv, W_o):
        import jax, jax.numpy as jnp
        import numpy as np
        from math import sqrt
        N_HEAD = 16
        W_SCALE = 0.02

        def _reference_tuple_inner(x, W_dq, W_uq, W_dkv, W_uk, W_uv, W_o):
            B, T, C = x.shape
            nh = N_HEAD
            hs = C // nh
            n_kvl = W_dkv.shape[0]
            k_eff = (W_dq.T @ W_uq.T @ W_uk).reshape(nh, hs, n_kvl)
            v_eff = jnp.transpose((W_uv.T @ W_o.T).reshape(n_kvl, nh, hs), (1, 0, 2))
            c_kv = x @ W_dkv.T
            q = x @ W_dq.T @ W_uq.T
            q = q.reshape(B, T, nh, hs)
            q_lat = jnp.einsum('bqhd,hdl->bhql', q, k_eff)
            attn = jnp.einsum('bhql,bkl->bhqk', q_lat, c_kv) / sqrt(hs)
            causal = jnp.tril(jnp.ones((T, T), dtype=bool))
            attn = jnp.where(causal[None, None], attn, -jnp.inf)
            attn = jax.nn.softmax(attn, axis=-1)
            y_lat = jnp.einsum('bhqk,bkl->bhql', attn, c_kv)
            y = jnp.einsum('bhql,hld->bqhd', y_lat, v_eff).reshape(B, T, C)
            return (y, c_kv)
        return _reference_tuple_inner(x, W_dq, W_uq, W_dkv, W_uk, W_uv, W_o)[0]

    def _L3_ffn_ref(x, q_node_w, q_node_b, q_w1, q_b1, q_w2, q_b2, k_node_w, k_node_b, k_w1, k_b1, k_w2, k_b2, v_node_w, v_node_b, v_w1, v_b1, v_w2, v_b2):
        import jax, jax.numpy as jnp
        import numpy as np
        LATENT = 128
        LEAF_W = 64
        DEPTH = 4
        N_LEAVES = 2 ** DEPTH
        N_NODES = 2 ** DEPTH - 1
        B, S = (4, 256)

        def _fff_params(key, prefix):
            ks = jax.random.split(key, 4)
            d, h, l, n = (LATENT, LEAF_W, N_LEAVES, N_NODES)
            s_in = 1.0 / np.sqrt(d).astype(np.float32)
            s_h = 1.0 / np.sqrt(h).astype(np.float32)
            return {f'{prefix}_node_w': jax.random.normal(ks[0], (n, d), jnp.float32) * s_in, f'{prefix}_node_b': jax.random.normal(ks[1], (n,), jnp.float32) * s_in, f'{prefix}_w1': jax.random.normal(ks[2], (l, d, h), jnp.float32) * s_in, f'{prefix}_b1': jnp.zeros((l, h), jnp.float32), f'{prefix}_w2': jax.random.normal(ks[3], (l, h, d), jnp.float32) * s_h, f'{prefix}_b2': jnp.zeros((l, d), jnp.float32)}

        def _fff(x, node_w, node_b, w1, b1, w2, b2):
            Bx, Sx, D = x.shape
            xf = x.reshape(-1, D)
            N = xf.shape[0]
            cur = jnp.zeros((N,), jnp.int32)
            for _ in range(DEPTH):
                pw = node_w[cur]
                score = jnp.einsum('nd,nd->n', xf, pw) + node_b[cur]
                cur = 2 * cur + 1 + (score >= 0).astype(jnp.int32)
            leaf = cur - N_NODES
            sel = jax.nn.one_hot(leaf, N_LEAVES, dtype=xf.dtype)
            hidden_all = jax.nn.relu(jnp.einsum('nd,ldh->lnh', xf, w1) + b1[:, None, :])
            hidden = hidden_all * sel.T[:, :, None]
            out = jnp.einsum('lnh,lho->no', hidden, w2) + sel @ b2
            return out.reshape(Bx, Sx, D)
        q = _fff(x, q_node_w, q_node_b, q_w1, q_b1, q_w2, q_b2)
        k = _fff(x, k_node_w, k_node_b, k_w1, k_b1, k_w2, k_b2)
        v = _fff(x, v_node_w, v_node_b, v_w1, v_b1, v_w2, v_b2)
        scale = 1.0 / np.sqrt(LATENT).astype(np.float32)
        attn = jax.nn.softmax(jnp.einsum('bqd,bkd->bqk', q, k) * scale, axis=-1)
        return jnp.einsum('bqk,bkd->bqd', attn, v)
    x = L0_attn_a_x
    x = x + _L0_attn_a_ref(_layernorm(x, axis=-1), L0_attn_a_wq, L0_attn_a_wk, L0_attn_a_wv, L0_attn_a_wo)
    x = x + _L0_ffn_ref(_layernorm(x, axis=-1), L0_ffn_wqkv, L0_ffn_q_scale, L0_ffn_k_scale, L0_ffn_wo, L0_ffn_ln_g, L0_ffn_ln_b, L0_ffn_w1, L0_ffn_b1, L0_ffn_w2, L0_ffn_b2)
    x = x + _L0_attn_b_ref(_layernorm(x, axis=-1), L0_attn_b_W_qkv, L0_attn_b_W_out)
    x = x + _L0_ffn_ref(_layernorm(x, axis=-1), L0_ffn_wqkv, L0_ffn_q_scale, L0_ffn_k_scale, L0_ffn_wo, L0_ffn_ln_g, L0_ffn_ln_b, L0_ffn_w1, L0_ffn_b1, L0_ffn_w2, L0_ffn_b2)
    x = x + _L1_attn_a_ref(_layernorm(x, axis=-1), L1_attn_a_w_qkv, L1_attn_a_b_qkv, L1_attn_a_w_proj, L1_attn_a_b_proj)
    x = x + _L1_ffn_ref(_layernorm(x, axis=-1), L1_ffn_gate_w, L1_ffn_bias, L1_ffn_W1, L1_ffn_W3, L1_ffn_W2, L1_ffn_sw1, L1_ffn_sw3, L1_ffn_sw2)
    x = x + _L1_attn_b_ref(_layernorm(x, axis=-1), L1_attn_b_ln1_g, L1_attn_b_ln1_b, L1_attn_b_Wqkv, L1_attn_b_bqkv, L1_attn_b_Wo, L1_attn_b_bo, L1_attn_b_ln2_g, L1_attn_b_ln2_b, L1_attn_b_W1, L1_attn_b_b1, L1_attn_b_W2, L1_attn_b_b2)
    x = x + _L1_ffn_ref(_layernorm(x, axis=-1), L1_ffn_gate_w, L1_ffn_bias, L1_ffn_W1, L1_ffn_W3, L1_ffn_W2, L1_ffn_sw1, L1_ffn_sw3, L1_ffn_sw2)
    x = x + _L2_attn_a_ref(_layernorm(x, axis=-1), L2_attn_a_Wq, L2_attn_a_bq, L2_attn_a_Wk, L2_attn_a_bk, L2_attn_a_Wv, L2_attn_a_bv)
    x = x + _L2_ffn_ref(_layernorm(x, axis=-1), L2_ffn_W1, L2_ffn_b1, L2_ffn_W2, L2_ffn_b2, L2_ffn_scale)
    x = x + _L2_attn_b_ref(_layernorm(x, axis=-1), L2_attn_b_Wq, L2_attn_b_bq, L2_attn_b_Wk, L2_attn_b_bk, L2_attn_b_Wv, L2_attn_b_bv, L2_attn_b_Wo, L2_attn_b_bo)
    x = x + _L2_ffn_ref(_layernorm(x, axis=-1), L2_ffn_W1, L2_ffn_b1, L2_ffn_W2, L2_ffn_b2, L2_ffn_scale)
    x = x + _L3_attn_a_ref(_layernorm(x, axis=-1), L3_attn_a_k, L3_attn_a_v, L3_attn_a_scale_factor, L3_attn_a_dropout_p)
    x = x + _L3_ffn_ref(_layernorm(x, axis=-1), L3_ffn_q_node_w, L3_ffn_q_node_b, L3_ffn_q_w1, L3_ffn_q_b1, L3_ffn_q_w2, L3_ffn_q_b2, L3_ffn_k_node_w, L3_ffn_k_node_b, L3_ffn_k_w1, L3_ffn_k_b1, L3_ffn_k_w2, L3_ffn_k_b2, L3_ffn_v_node_w, L3_ffn_v_node_b, L3_ffn_v_w1, L3_ffn_v_b1, L3_ffn_v_w2, L3_ffn_v_b2)
    x = x + _L3_attn_b_ref(_layernorm(x, axis=-1), L3_attn_b_W_dq, L3_attn_b_W_uq, L3_attn_b_W_dkv, L3_attn_b_W_uk, L3_attn_b_W_uv, L3_attn_b_W_o)
    x = x + _L3_ffn_ref(_layernorm(x, axis=-1), L3_ffn_q_node_w, L3_ffn_q_node_b, L3_ffn_q_w1, L3_ffn_q_b1, L3_ffn_q_w2, L3_ffn_q_b2, L3_ffn_k_node_w, L3_ffn_k_node_b, L3_ffn_k_w1, L3_ffn_k_b1, L3_ffn_k_w2, L3_ffn_k_b2, L3_ffn_v_node_w, L3_ffn_v_node_b, L3_ffn_v_w1, L3_ffn_v_b1, L3_ffn_v_w2, L3_ffn_v_b2)
    return x

_drawn_inputs = setup_inputs


def setup_inputs(seed=0):
    import zlib

    import numpy as np

    out = dict(_drawn_inputs(seed))
    spreads = {'L0_ffn_q_scale': (1.0, 0.6),
     'L0_ffn_k_scale': (1.0, 0.6),
     'L0_ffn_ln_g': (1.0, 0.6),
     'L0_ffn_ln_b': (0.0, 0.8),
     'L0_ffn_b1': (0.0, 0.649),
     'L0_ffn_b2': (0.0, 0.1),
     'L1_attn_b_ln1_g': (1.0, 0.2),
     'L1_attn_b_ln1_b': (0.0, 0.1),
     'L1_attn_b_bqkv': (0.0, 0.1),
     'L1_attn_b_bo': (0.0, 0.1),
     'L1_attn_b_ln2_g': (1.0, 0.2),
     'L1_attn_b_ln2_b': (0.0, 0.301),
     'L1_attn_b_b1': (0.0, 0.296),
     'L1_attn_b_b2': (0.0, 0.1),
     'L1_ffn_bias': (0.0, 0.8),
     'L2_ffn_b1': (0.0, 0.47),
     'L2_ffn_b2': (0.0, 0.1),
     'L3_ffn_q_b1': (0.0, 0.8),
     'L3_ffn_q_b2': (0.0, 0.8),
     'L3_ffn_k_b1': (0.0, 0.8),
     'L3_ffn_k_b2': (0.0, 0.8),
     'L3_ffn_v_b1': (0.0, 0.8),
     'L3_ffn_v_b2': (0.0, 0.606)}
    factors = {'L1_attn_a_b_qkv': 3.657,
     'L1_ffn_gate_w': 8.0,
     'L1_ffn_W1': 8.0,
     'L1_ffn_W3': 8.0,
     'L1_ffn_W2': 8.0,
     'L1_ffn_sw1': 8.0,
     'L1_ffn_sw3': 8.0,
     'L1_ffn_sw2': 8.0,
     'L2_attn_a_Wq': 8.0,
     'L2_attn_a_bq': 8.0,
     'L2_attn_a_Wk': 8.0,
     'L2_attn_a_bk': 8.0,
     'L2_attn_a_bv': 7.031,
     'L2_attn_b_Wq': 8.0,
     'L2_attn_b_bq': 8.0,
     'L2_attn_b_Wk': 8.0,
     'L2_attn_b_bk': 8.0,
     'L2_attn_b_Wv': 8.0,
     'L2_attn_b_bv': 8.0,
     'L2_attn_b_Wo': 8.0,
     'L2_attn_b_bo': 6.51,
     'L3_attn_b_W_dq': 8.0,
     'L3_attn_b_W_uq': 8.0,
     'L3_attn_b_W_dkv': 8.0,
     'L3_attn_b_W_uk': 8.0,
     'L3_attn_b_W_uv': 8.0,
     'L3_attn_b_W_o': 8.0,
     'L3_ffn_q_node_w': 8.0,
     'L3_ffn_q_node_b': 8.0,
     'L3_ffn_q_w1': 8.0,
     'L3_ffn_q_w2': 8.0,
     'L3_ffn_k_node_w': 8.0,
     'L3_ffn_k_node_b': 8.0,
     'L3_ffn_k_w1': 8.0,
     'L3_ffn_k_w2': 8.0,
     'L3_ffn_v_node_b': 5.618,
     'L3_ffn_v_w1': 3.197}
    for name, (base, spread) in spreads.items():
        noise = np.random.default_rng([zlib.crc32(name.encode()), seed]).standard_normal(out[name].shape)
        drawn = base * np.exp(spread * noise) if base else spread * noise
        out[name] = jnp.asarray(drawn.astype(out[name].dtype))
    for name, factor in factors.items():
        out[name] = (out[name] * factor).astype(out[name].dtype)
    return out
```

```python
from contextlib import ExitStack, contextmanager

import numpy as np

import concourse.bass as bass
from concourse import mybir

F32 = mybir.dt.float32
BF16 = mybir.dt.bfloat16
ALU = mybir.AluOpType
ACT = mybir.ActivationFunctionType
AX_X = mybir.AxisListType.X

P = 128
S = 1024
NT = S // P
HALF = 512
NH = S // HALF
NEG = -1e30
EXPERTS, TOPK, CAPACITY = 32, 4, 128
GATE_ROWS = EXPERTS + 2
LEAVES = 16


class Core:

    def __init__(self, nc, ctx, dram):
        self.nc, self.ctx, self.dram = nc, ctx, dram
        self.sems = {}

        def sb(name, shape, dt=F32):
            return ctx.enter_context(nc.sbuf_tensor(name, shape, dt))

        self.sb = sb
        self.X = sb("residual", [P, NT, P])
        self.Y = sb("normalised", [P, NT, P])
        self.H = sb("shifted", [P, NT, P])
        self.XT = sb("x_t", [P, S])
        self.QT, self.KT = sb("q_t", [P, S]), sb("k_t", [P, S])
        self.QB, self.KB = sb("q_t_bf16", [P, S], BF16), sb("k_t_bf16", [P, S], BF16)
        self.T1, self.T2 = sb("turned", [P, S]), sb("squares", [P, S])
        self.VA = sb("v_and_ones", [P, NT, 136])
        self.CTX, self.CT = sb("context", [P, NT, P]), sb("context_t", [P, S])
        self.HT = sb("hidden_t", [P, 4, S])
        self.stats, self.mv = sb("ln_stats", [P, NT, 6]), sb("ln_mean_var", [P, NT, 2])
        self.rstd = sb("ln_rstd", [P, NT, 2])
        self.W, self.B = sb("w_qkv", [P, 5, P]), sb("b_qkv", [1, 5, P])
        self.WO, self.BO = sb("w_out", [P, P]), sb("b_out", [1, P])
        self.W1, self.B1 = sb("w_up", [P, 6, P]), sb("b_up", [1, 6, P])
        self.W2, self.B2 = sb("w_down", [P, 4, P]), sb("b_down", [1, P])
        self.W1E, self.W2E = sb("w_up_eff", [P, 4, P]), sb("w_down_eff", [P, 4, P])
        self.WB = sb("w_bf16", [P, 3, P], BF16)
        self.SEL = sb("pick_rows", [GATE_ROWS, P])
        self.gcols = sb("gain_bias", [P, 4])
        self.gates = sb("gates", [P, NT, GATE_ROWS])
        self.gatesT = sb("gates_t", [GATE_ROWS, S])
        self.small = sb("small", [P, 6, NT, EXPERTS])
        self.small8 = sb("top8", [P, NT, 8])
        self.gsum = sb("gate_sums", [P, 2, NT])
        self.ebias = sb("expert_bias", [P, EXPERTS])
        self.carry = [sb(f"expert_count_{n}", [1, EXPERTS]) for n in range(2)]
        self.probs = sb("probs_t", [P, 3, HALF])
        self.negmax = sb("neg_max", [P, 2, 4], BF16)
        self.negmax_row = sb("neg_max_row", [P, 2, HALF], BF16)
        self.rden = sb("rden", [P, 4, 1])
        self.odd = sb("odd_scaled", [P, 9])
        self.ident, self.identb = sb("ident", [P, P]), sb("ident_bf16", [P, P], BF16)
        self.masks = sb("masks", [P, 6, P], BF16)
        self.before = sb("before", [P, P])
        self.block1 = sb("block_ones", [P, P])
        self.pick8 = sb("pick8", [P, 8, P])
        self.ones = sb("ones", [P, HALF])
        self.first = sb("first_rows", [P, 3, P], BF16)
        self.rope64 = sb("rope64", [P, 2, S])
        self.rope8 = sb("rope8", [P, 2, S])
        self.xpos = sb("xpos", [P, 4, S])
        self.PS = ctx.enter_context(nc.psum_tensor("psum", [P, 8, HALF], F32))

    def banks(self, first, n=2):
        return self.PS[:, first:first + n, :].rearrange("p b n -> p (b n)")

    def tiles(self, first):
        return self.banks(first).rearrange("p (t d) -> p t d", d=P)

    @contextmanager
    def stage(self, *names):
        for n in names:
            if n not in self.sems:
                self.sems[n] = self.ctx.enter_context(self.nc.semaphore(n))
        sems = [self.sems[n] for n in names]
        with self.nc.Block() as block:
            yield [block] + sems
        for s in sems:
            self.nc.gpsimd.sem_clear(s)
        self.nc.all_engine_barrier()


def one(ap, i):
    v = ap[bass.ds(i, 1)]
    names = "abcd"[:len(v.shape) - 1]
    if len(names) == 1:
        return v
    return v.rearrange(f"z {' '.join(names)} -> (z {names[0]}) {' '.join(names[1:])}")



def load_constants(c):
    d = c.dram
    with c.stage("const_loaded", "const_set") as (block, loaded, const_set):
        todo = [(c.ident, d["c_ident"]), (c.before, d["c_before"]), (c.block1, d["c_block1"]),
                (c.pick8, d["c_pick8"]), (c.rope64, d["c_rope64"]), (c.rope8, d["c_rope8"]), (c.xpos, d["c_xpos"])]

        @block.sync
        def _(sp):
            for dst, src in todo:
                sp.dma_start(dst[:], src).then_inc(loaded, 16)
            sp.dma_start(c.H[:, 0:6, :], d["c_masks"]).then_inc(loaded, 16)
            sp.dma_start(c.Y[:, 0:3, :], d["c_first"]).then_inc(loaded, 16)

        @block.vector
        def _(dve):
            dve.memset(c.ones[:, :], 1.0).then_inc(const_set, 1)
            dve.memset(c.negmax_row[:, :, :], 0.0).then_inc(const_set, 1)
            dve.memset(c.carry[0][:, :], 0.0).then_inc(const_set, 1)
            dve.memset(c.carry[1][:, :], 0.0).then_inc(const_set, 1)
            dve.wait_ge(loaded, 16 * (len(todo) + 2))
            dve.tensor_copy(c.identb[:, :], c.ident[:, :]).then_inc(const_set, 1)
            dve.tensor_copy(c.masks[:, :, :], c.H[:, 0:6, :]).then_inc(const_set, 1)
            dve.tensor_copy(c.first[:, :, :], c.Y[:, 0:3, :]).then_inc(const_set, 1)


def load_x(c, b):
    with c.stage("x_loaded") as (block, loaded):
        @block.sync
        def _(sp):
            sp.dma_start(c.X[:, :, :], one(c.dram["x"], b).rearrange("(t p) d -> p t d", p=P)).then_inc(loaded, 16)
            sp.wait_ge(loaded, 16)


def store_x(c, b):
    with c.stage("x_stored") as (block, stored):
        @block.sync
        def _(sp):
            sp.dma_start(one(c.dram["out"], b).rearrange("(t p) d -> p t d", p=P), c.X[:, :, :]).then_inc(stored, 16)
            sp.wait_ge(stored, 16)


def add_to(c, target, part):
    with c.stage("added") as (block, added):
        @block.vector
        def _(dve):
            dve.tensor_tensor(target[:, :, :], target[:, :, :], part, ALU.add).then_inc(added, 1)


def shift_tokens(c, src):
    with c.stage("shift_done", "shift_dma") as (block, done, moved):
        @block.vector
        def _(dve):
            dve.tensor_copy(c.H[:, :, 0:64], src[:, :, 0:64]).then_inc(done, 1)
            dve.memset(c.H[0:1, 0:1, 64:P], 0.0).then_inc(done, 1)

        @block.sync
        def _(sp):
            sp.dma_start(c.H[1:P, :, 64:P], src[0:P - 1, :, 64:P]).then_inc(moved, 16)
            sp.dma_start(c.H[0:1, 1:NT, 64:P], src[P - 1:P, 0:NT - 1, 64:P]).then_inc(moved, 16)
            sp.wait_ge(moved, 32)



def norm_and_turn(c, src, norm=None, gains=None, shift=False):
    with c.stage("ln_loaded", "ln_stats_done", "ln_aggr_done", "ln_root", "ln_rstd_done",
                 "ln_done", "turned_tiles", "turned_out") as \
            (block, loaded, stats_done, aggr_done, root, rstd_done, normed, turned, out_done):
        src_t = norm if norm is not None else src
        tiles = c.tiles(0)

        if gains is not None:
            @block.sync
            def _(sp):
                sp.dma_start(c.gcols[:, 0:2], gains).then_inc(loaded, 16)

        if norm is not None:
            @block.vector
            def _(dve):
                for t in range(NT):
                    dve.bn_stats(c.stats[:, t, :], src[:, t, :]).then_inc(stats_done, 1)
                for t in range(NT):
                    dve.wait_ge(stats_done, t + 1)
                    dve.bn_aggr(c.mv[:, t, :], c.stats[:, t, :]).then_inc(aggr_done, 1)
                dve.wait_ge(aggr_done, NT)
                dve.tensor_scalar(c.rstd[:, :, 0], c.mv[:, :, 1], 1e-5, None, ALU.add).then_inc(root, 1)
                dve.wait_ge(root, 2)
                dve.reciprocal(c.rstd[:, :, 1], c.rstd[:, :, 0]).then_inc(rstd_done, 1)
                dve.wait_ge(rstd_done, 1)
                for t in range(NT):
                    dve.tensor_scalar(norm[:, t, :], src[:, t, :], c.mv[:, t, 0:1], c.rstd[:, t, 1:2],
                                      ALU.subtract, ALU.mult).then_inc(normed, 1)

        @block.tensor
        def _(pe):
            for t in range(NT):
                if norm is not None:
                    pe.wait_ge(normed, t + 1)
                pe.transpose(tiles[:, t, :], src_t[:, t, :], c.ident[:, :]).then_inc(turned, 1)

        @block.scalar
        def _(act):
            if norm is not None:
                act.wait_ge(root, 1)
                act.activation(c.rstd[:, :, 0], c.rstd[:, :, 0], ACT.Sqrt).then_inc(root, 1)
            if gains is not None:
                act.wait_ge(loaded, 16)
            if shift:
                act.wait_ge(turned, NT)
                act.activation(c.XT[0:64, :], c.banks(0)[0:64, :], ACT.Copy).then_inc(out_done, 1)
                act.activation(c.XT[64:P, 1:S], c.banks(0)[64:P, 0:S - 1], ACT.Copy).then_inc(out_done, 1)
                act.activation(c.XT[64:P, 0:1], c.ones[64:P, 0:1], ACT.Copy, scale=0.0).then_inc(out_done, 1)
                return
            for h in range(NH):
                act.wait_ge(turned, (h + 1) * (NT // NH))
                part = c.XT[:, h * HALF:(h + 1) * HALF]
                if gains is None:
                    act.activation(part, c.banks(0)[:, h * HALF:(h + 1) * HALF], ACT.Copy).then_inc(out_done, 1)
                else:
                    act.activation(part, c.banks(0)[:, h * HALF:(h + 1) * HALF], ACT.Identity,
                                   bias=c.gcols[:, 1:2], scale=c.gcols[:, 0:1]).then_inc(out_done, 1)



class Heads:

    def __init__(self, dim, n, rows, scale, mode, keys=S):
        self.dim, self.n, self.rows, self.scale, self.mode = dim, n, rows, scale, mode
        self.key_tiles = keys // P

    def v(self, c, tile, h):
        w = self.dim + 1
        return c.VA[:, tile, h * w:(h + 1) * w]

    def sees(self, q):
        return {"full": (0, self.key_tiles), "causal": (0, q + 1), "window": (max(q - 1, 0), q + 1)}[self.mode]

    def mask(self, q, k, turned):
        if self.mode == "causal" and q == k:
            return int(turned)
        if self.mode == "window":
            return (2 if q == k else 4) + int(turned)
        return None


def clear_v(c):
    with c.stage("ones_set") as (block, ones_set):
        @block.vector
        def _(dve):
            dve.memset(c.VA[:, :, :], 1.0).then_inc(ones_set, 1)


def project(c, w, heads, bias=None, rope=None, xpos=None):
    turned = rope is not None or xpos is not None
    slots = 5 if turned else 3
    with c.stage("w_loaded", "projected", "rope_one", "rope_two", "rope_sum", "squared", "norm_summed",
                 "norm_root", "norm_clip", "norm_inv", "evacuated", "v_out", "b_loaded") as \
            (block, loaded, projected, one_done, two_done, summed, squared, norm_summed, norm_root,
             norm_clip, norm_inv, evacuated, v_out, b_loaded):
        outs = [(c.QT, c.QB), (c.KT, c.KB)]
        step = 2 if turned else 1
        w_v = slots - 1

        @block.sync
        def _(sp):
            sp.dma_start(c.W[:, 0:slots, :], w).then_inc(loaded, 16)
            if bias is not None:
                sp.dma_start(c.B[:, 0:slots, :], bias).then_inc(b_loaded, 16)

        @block.tensor
        def _(pe):
            pe.wait_ge(loaded, 16)
            if bias is not None:
                pe.wait_ge(b_loaded, 16)
            for s in range(slots - 1):
                for h in range(NH):
                    out = c.PS[:, 2 * s + h, :]
                    if bias is not None:
                        pe.matmul(out, c.B[:, s, :], c.ones[0:1, :], start=True, stop=False)
                    mm = pe.matmul(out, c.W[:, s, :], c.XT[:, h * HALF:(h + 1) * HALF],
                                   start=bias is None, stop=True)
                mm.then_inc(projected, 1)
            if xpos is not None:
                for n in range(2):
                    pe.wait_ge(squared, n + 1)
                    pe.wait_ge(summed, n + 1)
                    for h in range(NH):
                        mm = pe.matmul(c.PS[:, 4 * n + h, :], c.block1[:, :], c.T2[:, h * HALF:(h + 1) * HALF],
                                       start=True, stop=True)
                    mm.then_inc(norm_summed, 1)
                pe.wait_ge(norm_root, 1)
            else:
                pe.wait_ge(evacuated, 1)
                if turned:
                    pe.wait_ge(summed, 1)
            tiles = c.tiles(0)
            for t in range(NT):
                if bias is not None:
                    pe.matmul(tiles[:, t, :], c.ones[0:1, 0:P], c.B[:, w_v, :], start=True, stop=False)
                mm = pe.matmul(tiles[:, t, :], c.XT[:, t * P:(t + 1) * P], c.W[:, w_v, :],
                               start=bias is None, stop=True)
            mm.then_inc(projected, 1)

        @block.vector
        def _(dve):
            for n, (out, _) in enumerate(outs):
                dve.wait_ge(projected, step * (n + 1))
                straight = c.banks(2 * step * n)
                if not turned:
                    dve.tensor_copy(out[:, :], straight).then_inc(summed, 1)
                    continue
                across = c.banks(2 * step * n + 2)
                if n:
                    dve.wait_ge(summed, n)
                if xpos is None:
                    dve.tensor_tensor(out[:, :], straight, rope[:, 0, :], ALU.mult).then_inc(one_done, 1)
                    dve.tensor_tensor(c.T1[:, :], across, rope[:, 1, :], ALU.mult).then_inc(two_done, 1)
                else:
                    dve.scalar_tensor_tensor(out[:, :], straight, c.gcols[:, 2 * n:2 * n + 1], xpos[:, 2 * n, :],
                                             ALU.mult, ALU.mult).then_inc(one_done, 1)
                    dve.scalar_tensor_tensor(c.T1[:, :], across, c.gcols[:, 2 * n + 1:2 * n + 2],
                                             xpos[:, 2 * n + 1, :], ALU.mult, ALU.mult).then_inc(two_done, 1)
                dve.wait_ge(one_done, n + 1)
                dve.wait_ge(two_done, n + 1)
                dve.tensor_tensor(out[:, :], out[:, :], c.T1[:, :], ALU.add).then_inc(summed, 1)
                if xpos is not None:
                    dve.wait_ge(norm_root, n + 1)
                    dve.tensor_scalar(c.CT[:, :], c.CT[:, :], 1e-12, None, ALU.max).then_inc(norm_clip, 1)
                    dve.wait_ge(norm_clip, n + 1)
                    dve.reciprocal(c.CT[:, :], c.CT[:, :]).then_inc(norm_inv, 1)
                    dve.wait_ge(norm_inv, n + 1)
                    dve.wait_ge(summed, n + 1)
                    dve.tensor_tensor(out[:, :], out[:, :], c.CT[:, :], ALU.mult).then_inc(v_out, 1)

        @block.scalar
        def _(act):
            for n, (out, short) in enumerate(outs):
                act.wait_ge(projected, step * (n + 1))
                if xpos is not None:
                    act.wait_ge(one_done, n + 1)
                    if n:
                        act.wait_ge(norm_summed, n)
                        act.wait_ge(v_out, n)
                    act.activation(c.T2[:, :], c.banks(4 * n), ACT.Square).then_inc(squared, 1)
                    act.wait_ge(norm_summed, n + 1)
                    act.activation(c.CT[:, :], c.banks(4 * n), ACT.Sqrt).then_inc(norm_root, 1)
                    act.wait_ge(v_out, n + 1)
                    act.activation(short[:, :], out[:, :], ACT.Copy).then_inc(evacuated, 1)
                elif turned:
                    act.wait_ge(summed, n + 1)
                    act.activation(short[:, :], out[:, :], ACT.Copy).then_inc(evacuated, 1)
                else:
                    act.wait_ge(summed, n + 1)
                    act.activation(short[:, :], out[:, :], ACT.Copy).then_inc(evacuated, 1)
            act.wait_ge(projected, slots)
            pitch = P // heads.n
            for h in range(heads.n):
                w_ = heads.dim + 1
                act.activation(c.VA[:, :, h * w_:h * w_ + heads.dim],
                               c.tiles(0)[:, :, h * pitch:h * pitch + heads.dim], ACT.Copy).then_inc(evacuated, 1)


def attend(c, heads, out_at):
    units = [(h, half) for h in range(heads.n) for half in range(NH)]
    QPH = HALF // P
    pitch = P // heads.n
    work = []
    for u, (h, half) in enumerate(units):
        for k in range(heads.key_tiles):
            cols = [q - half * QPH for q in range(half * QPH, (half + 1) * QPH)
                    if heads.sees(q)[0] <= k < heads.sees(q)[1]]
            if cols:
                work.append((u, k, cols[0], cols[-1] + 1))
    first = [min(i for i, x in enumerate(work) if x[0] == u) for u in range(len(units))] + [len(work)]
    RING = QPH + 1
    first_index = {32: 0, 64: 1, 128: 2}[pitch]

    with c.stage("rows_ready", "rows_read", "scores_ready", "probs_ready", "pv_done",
                 "rden_done", "out_done") as \
            (block, rows_ready, rows_read, scores_ready, probs_ready, pv_done, rden_done, out_done):

        def rows(h):
            return slice(h * pitch, h * pitch + heads.rows)

        def o_at(q):
            w = heads.dim + 1
            return (6 + q // 2, (q % 2) * w) if heads.dim == P else (6, q * w)

        @block.tensor
        def _(pe):
            def row_scores(u, j):
                h, half = units[u]
                q = half * QPH + j
                use = u * RING + j
                lo, hi = heads.sees(q)
                if use >= 2:
                    pe.wait_ge(rows_read, use - 1)
                k = lo
                while k < hi:
                    n = 1
                    masked = heads.mask(q, k, False)
                    while (masked is None and k + n < hi and (k + n - lo) % QPH and
                           heads.mask(q, k + n, False) is None):
                        n += 1
                    col = (k - lo) % QPH * P
                    out = c.PS[:, 2 * (use % 2) + (k - lo) // QPH, col:col + n * P]
                    mm = pe.matmul(out, c.QB[rows(h), q * P:(q + 1) * P], c.KB[rows(h), k * P:(k + n) * P],
                                   start=True, stop=masked is None)
                    if masked is not None:
                        mm = pe.matmul(out, c.identb[:, :], c.masks[:, masked, :], start=False, stop=True)
                    k += n
                mm.then_inc(rows_ready, 1)

            def max_row(u):
                use = u * RING + QPH
                pe.wait_ge(rows_read, use)
                for j in range(QPH):
                    mm = pe.matmul(c.PS[0:1, 2 * (use % 2), j * P:(j + 1) * P], c.negmax[:, u % 2, j:j + 1],
                                   c.identb[:, :], start=True, stop=True)
                mm.then_inc(rows_ready, 1)

            def scores(n):
                u, k, lo, hi = work[n]
                h, half = units[u]
                if n >= 2:
                    pe.wait_ge(probs_ready, n - 1)
                if n == first[u]:
                    pe.wait_ge(rows_read, (u + 1) * RING)
                out = c.PS[:, 4 + n % 2, lo * P:hi * P]
                q0 = half * HALF
                pe.matmul(out, c.KT[rows(h), k * P:(k + 1) * P], c.QT[rows(h), q0 + lo * P:q0 + hi * P],
                          start=True, stop=False)
                for j in range(lo, hi):
                    masked = heads.mask(half * QPH + j, k, True)
                    if masked is not None:
                        pe.matmul(c.PS[:, 4 + n % 2, j * P:(j + 1) * P], c.identb[:, :], c.masks[:, masked, :],
                                  start=False, stop=False)
                mm = pe.matmul(out, c.first[rows(h), first_index, :], c.negmax_row[rows(h), u % 2, lo * P:hi * P], start=False, stop=True)
                mm.then_inc(scores_ready, 1)

            def weighted(n):
                u, k, lo, hi = work[n]
                h, half = units[u]
                pe.wait_ge(probs_ready, n + 1)
                if n == first[u] and u >= 1:
                    pe.wait_ge(out_done, u)
                for j in range(lo, hi):
                    bank, col = o_at(j)
                    opens = n == first[u] and (j == lo or (heads.dim == P and j % 2 == 0))
                    mm = pe.matmul(c.PS[:, bank, col:col + heads.dim + 1],
                                   c.probs[:, n % 3, j * P:(j + 1) * P], heads.v(c, k, h),
                                   start=opens, stop=k + 1 == heads.sees(half * QPH + j)[1], skip_group_check=True)
                mm.then_inc(pv_done, 1)

            for j in range(QPH):
                row_scores(0, j)
            max_row(0)
            for u in range(len(units)):
                ahead = list(range(QPH)) if u + 1 < len(units) else []
                for n in range(first[u], first[u + 1]):
                    scores(n)
                    if ahead and (n - first[u]) % 2 == 1:
                        row_scores(u + 1, ahead.pop(0))
                    if n > first[u]:
                        weighted(n - 1)
                while ahead:
                    row_scores(u + 1, ahead.pop(0))
                if u + 1 < len(units):
                    max_row(u + 1)
                weighted(first[u + 1] - 1)

        @block.scalar
        def _(act):
            for n, (u, k, lo, hi) in enumerate(work):
                act.wait_ge(scores_ready, n + 1)
                if n >= 3:
                    act.wait_ge(pv_done, n - 2)
                act.activation(c.probs[:, n % 3, lo * P:hi * P], c.PS[:, 4 + n % 2, lo * P:hi * P], ACT.Exp,
                               scale=heads.scale).then_inc(probs_ready, 1)

        @block.vector
        def _(dve):
            def maxima(u):
                h, half = units[u]
                for j in range(QPH):
                    use = u * RING + j
                    lo, hi = heads.sees(half * QPH + j)
                    dve.wait_ge(rows_ready, use + 1)
                    dve.tensor_reduce(c.negmax[:, u % 2, j:j + 1], c.banks(2 * (use % 2))[:, 0:(hi - lo) * P],
                                      AX_X, ALU.max, negate=True).then_inc(rows_read, 1)
                use = u * RING + QPH
                dve.wait_ge(rows_ready, use + 1)
                if u >= 2:
                    dve.wait_ge(scores_ready, first[u - 1])
                dve.wait_ge(rows_read, use)
                dve.tensor_copy(c.negmax_row[h * pitch:h * pitch + 1, u % 2, :], c.PS[0:1, 2 * (use % 2), :]).then_inc(rows_read, 1)

            def divide(u):
                h, half = units[u]
                d = heads.dim
                dve.wait_ge(pv_done, first[u + 1])
                if u:
                    dve.wait_ge(out_done, u)
                if d < P:
                    o = c.PS[:, 6, 0:QPH * (d + 1)].rearrange("p (q w) -> p q w", w=d + 1)
                else:
                    o = c.PS[:, 6:8, 0:2 * (d + 1)].rearrange("p b (q w) -> p b q w", w=d + 1)
                if d < P:
                    dve.reciprocal(c.rden[:, :, :], o[:, :, d:d + 1]).then_inc(rden_done, 1)
                    dve.wait_ge(rden_done, u + 1)
                    dve.tensor_tensor(out_at(h, half), o[:, :, 0:d], c.rden[:, :, :].to_broadcast([P, QPH, d]),
                                      ALU.mult).then_inc(out_done, 1)
                else:
                    for b in range(2):
                        dve.reciprocal(c.rden[:, 2 * b:2 * b + 2, :], o[:, b, :, d:d + 1]).then_inc(rden_done, 1)
                    dve.wait_ge(rden_done, 2 * (u + 1))
                    for b in range(2):
                        mm = dve.tensor_tensor(out_at(h, half)[:, 2 * b:2 * b + 2, :], o[:, b, :, 0:d],
                                               c.rden[:, 2 * b:2 * b + 2, :].to_broadcast([P, 2, d]), ALU.mult)
                    mm.then_inc(out_done, 1)

            maxima(0)
            for u in range(len(units)):
                if u + 1 < len(units):
                    maxima(u + 1)
                divide(u)


def project_out(c, target, w, bias=None):
    with c.stage("wo_loaded", "ctx_turned", "ctx_out", "y_ready", "y_added") as \
            (block, loaded, turned, ctx_out, y_ready, y_added):
        @block.sync
        def _(sp):
            sp.dma_start(c.WO[:, :], w).then_inc(loaded, 16)
            if bias is not None:
                sp.dma_start(c.BO[:, :], bias).then_inc(loaded, 16)

        @block.tensor
        def _(pe):
            for t in range(NT):
                pe.transpose(c.tiles(0)[:, t, :], c.CTX[:, t, :], c.ident[:, :]).then_inc(turned, 1)
            pe.wait_ge(loaded, 32 if bias is not None else 16)
            for t in range(NT):
                if t % (NT // NH) == 0:
                    pe.wait_ge(ctx_out, t // (NT // NH) + 1)
                if bias is not None:
                    pe.matmul(c.tiles(2)[:, t, :], c.ones[0:1, 0:P], c.BO[:, :], start=True, stop=False)
                pe.matmul(c.tiles(2)[:, t, :], c.CT[:, t * P:(t + 1) * P], c.WO[:, :],
                          start=bias is None, stop=True).then_inc(y_ready, 1)

        @block.scalar
        def _(act):
            for h in range(NH):
                act.wait_ge(turned, (h + 1) * (NT // NH))
                act.activation(c.CT[:, h * HALF:(h + 1) * HALF], c.PS[:, h, :], ACT.Copy).then_inc(ctx_out, 1)

        @block.vector
        def _(dve):
            for h in range(NH):
                dve.wait_ge(y_ready, (h + 1) * (NT // NH))
                t = slice(h * (NT // NH), (h + 1) * (NT // NH))
                dve.tensor_tensor(target[:, t, :], target[:, t, :], c.tiles(2)[:, t, :], ALU.add).then_inc(y_added, 1)


def project_rows_out(c, pair):
    per_row = 1024 // 64
    w = c.HT[:, 0:2, :].rearrange("p a (m n) -> p (a m) n", n=P)
    by_place = c.CT[:, :].rearrange("p (m r) -> p r m", m=per_row)
    with c.stage("ctx_turned", "ctx_out", "y_ready", "y_added") as (block, turned, ctx_out, y_ready, y_added):
        @block.tensor
        def _(pe):
            for t in range(NT):
                pe.transpose(c.tiles(0)[:, t, :], c.CTX[:, t, :], c.ident[:, :]).then_inc(turned, 1)
            pe.wait_ge(ctx_out, NH)
            for h in range(2):
                on = slice(64 * h, 64 * h + 64)
                for m in range(per_row):
                    mm = pe.matmul(c.PS[on, 2, 0:P], c.CT[on, 64 * m:64 * m + 64], w[on, m, :],
                                   start=m == 0, stop=m == per_row - 1)
                mm.then_inc(y_ready, 1)

        @block.scalar
        def _(act):
            rows = S // per_row // NH
            for h in range(NH):
                act.wait_ge(turned, (h + 1) * (NT // NH))
                act.activation(by_place[:, h * rows:(h + 1) * rows, :],
                               c.PS[:, h, :].rearrange("p (r m) -> p r m", m=per_row), ACT.Copy).then_inc(ctx_out, 1)

        @block.vector
        def _(dve):
            dve.wait_ge(y_ready, 2)
            tile = c.X[:, bass.ds(pair, 1), :].rearrange("p z d -> p (z d)")
            dve.tensor_tensor(tile, tile, c.PS[:, 2, 0:P], ALU.add).then_inc(y_added, 1)


def pair_out(c):
    return lambda h, half: c.CTX[:, 4 * half:4 * half + 4, 64 * h:64 * h + 64]


def attention64(c, target, w, wo, n_pairs, mode, scale, rope=None, xpos=None):
    heads = Heads(64, 2, 64, scale, mode)
    clear_v(c)
    with c.nc.Fori(0, n_pairs) as pair:
        project(c, one(w, pair), heads, rope=rope, xpos=xpos)
        attend(c, heads, pair_out(c))
        project_out(c, target, one(wo, pair))


def attention8(c, w, bias, mode, rope=None):
    heads = Heads(8, 4, 32, 8.0 ** -0.5, mode)
    clear_v(c)
    with c.nc.Fori(0, 4) as group:
        project(c, one(w, group), heads, bias=None if bias is None else one(bias, group), rope=rope)
        attend(c, heads, lambda h, half: c.CTX[:, 4 * half:4 * half + 4, bass.ds(group * 32 + 8 * h, 8)])



def mlp(c, target, w1, b1, w2, b2, chunks, gated, batch_weights=False):
    with c.stage("mlp_loaded", "up_done", "gelu_done", "hidden_done", "down_done", "mlp_added") as \
            (block, loaded, up, gelu, hidden, down, added):
        n_up = chunks * (2 if gated else 1)
        steps = [(k, h) for k in range(chunks) for h in range(NH)]
        W1, W2 = (c.W1E, c.W2E) if batch_weights else (c.W1, c.W2)
        n_loads = 2 if batch_weights else 4

        @block.sync
        def _(sp):
            if not batch_weights:
                sp.dma_start(W1[:, 0:n_up, :], w1).then_inc(loaded, 16)
                sp.dma_start(W2[:, 0:chunks, :], w2).then_inc(loaded, 16)
            sp.dma_start(c.B1[:, 0:n_up, :], b1).then_inc(loaded, 16)
            sp.dma_start(c.B2[:, :], b2).then_inc(loaded, 16)

        @block.tensor
        def _(pe):
            pe.wait_ge(loaded, 16 * n_loads)
            for n, (k, h) in enumerate(steps):
                if n >= 2:
                    pe.wait_ge(hidden if gated else gelu, n - 1)
                for g in range(2 if gated else 1):
                    out = c.PS[:, 2 * (n % 2) + g, :]
                    pe.matmul(out, c.B1[:, k + g * chunks, :], c.ones[0:1, :], start=True, stop=False)
                    mm = pe.matmul(out, W1[:, k + g * chunks, :], c.XT[:, h * HALF:(h + 1) * HALF],
                                   start=False, stop=True)
                mm.then_inc(up, 1)
            pe.wait_ge(hidden if gated else gelu, len(steps))
            for t in range(NT):
                pe.matmul(c.tiles(6)[:, t, :], c.ones[0:1, 0:P], c.B2[:, :], start=True, stop=False)
                for k in range(chunks):
                    mm = pe.matmul(c.tiles(6)[:, t, :], c.HT[:, k, t * P:(t + 1) * P], W2[:, k, :],
                                   start=False, stop=k == chunks - 1)
                mm.then_inc(down, 1)

        @block.scalar
        def _(act):
            for n, (k, h) in enumerate(steps):
                act.wait_ge(up, n + 1)
                act.activation(c.HT[:, k, h * HALF:(h + 1) * HALF], c.PS[:, 2 * (n % 2) + int(gated), :],
                               ACT.Gelu).then_inc(gelu, 1)

        @block.vector
        def _(dve):
            if gated:
                for n, (k, h) in enumerate(steps):
                    dve.wait_ge(gelu, n + 1)
                    part = c.HT[:, k, h * HALF:(h + 1) * HALF]
                    dve.tensor_tensor(part, part, c.PS[:, 2 * (n % 2), :], ALU.mult).then_inc(hidden, 1)
            for h in range(NH):
                dve.wait_ge(down, (h + 1) * (NT // NH))
                t = slice(h * (NT // NH), (h + 1) * (NT // NH))
                dve.tensor_tensor(target[:, t, :], target[:, t, :], c.tiles(6)[:, t, :], ALU.add).then_inc(added, 1)


def experts(c, i, w, w2, sel, rows, bias=None, cast=False, add_tokens=None, add_turned=None):
    ups = 1 if bias is not None else 2
    with c.stage("pair_loaded", "pair_cast", "pair_up", "pair_act", "pair_gated", "pair_hidden",
                 "pair_down", "pair_added") as (block, loaded, cast_done, up, acted, gated, hidden, down, added):
        @block.sync
        def _(sp):
            if cast:
                sp.dma_start(c.WB[:, 0:2, :], one(w, i)).then_inc(loaded, 16)
                sp.dma_start(c.WB[:, 2, :], one(w2, i)).then_inc(loaded, 16)
            else:
                sp.dma_start(c.W1[:, 0:ups, :], one(w, i)).then_inc(loaded, 16)
                sp.dma_start(c.W2[:, 0, :], one(w2, i)).then_inc(loaded, 16)
                sp.dma_start(c.B1[:, 0, :], one(bias, i)).then_inc(loaded, 16)
            sp.dma_start(c.SEL[0:rows, :], one(sel, i)).then_inc(loaded, 16)

        if cast:
            @block.gpsimd
            def _(pool):
                pool.wait_ge(loaded, 48)
                pool.tensor_copy(c.W1[:, 0:2, :], c.WB[:, 0:2, :]).then_inc(cast_done, 1)
                pool.tensor_copy(c.W2[:, 0, :], c.WB[:, 2, :]).then_inc(cast_done, 1)

        @block.tensor
        def _(pe):
            if cast:
                pe.wait_ge(cast_done, 2)
                pe.wait_ge(loaded, 48)
            else:
                pe.wait_ge(loaded, 64)
            for h in range(NH):
                cols = slice(h * HALF, (h + 1) * HALF)
                if bias is not None:
                    pe.matmul(c.PS[:, 3 * h, :], c.B1[:, 0, :], c.ones[0:1, :], start=True, stop=False)
                for u in range(ups):
                    pe.matmul(c.PS[:, 3 * h + u, :], c.W1[:, u, :], c.XT[:, cols], start=bias is None, stop=True)
                pe.matmul(c.PS[:, 3 * h + 2, :], c.SEL[0:rows, :], c.gatesT[0:rows, cols],
                          start=True, stop=True).then_inc(up, 1)
            if add_tokens is not None:
                for t in range(NT):
                    if t % (NT // NH) == 0:
                        pe.wait_ge(hidden, t // (NT // NH) + 1)
                    pe.matmul(c.tiles(6)[:, t, :], c.HT[:, 0, t * P:(t + 1) * P], c.W2[:, 0, :],
                              start=True, stop=True).then_inc(down, 1)
            else:
                for h in range(NH):
                    pe.wait_ge(hidden, h + 1)
                    pe.matmul(c.PS[:, 6 + h, :], c.W2[:, 0, :], c.HT[:, 0, h * HALF:(h + 1) * HALF],
                              start=True, stop=True).then_inc(down, 1)

        @block.scalar
        def _(act):
            for h in range(NH):
                act.wait_ge(up, h + 1)
                act.activation(c.HT[:, 1, h * HALF:(h + 1) * HALF], c.PS[:, 3 * h, :],
                               ACT.Silu if ups == 2 else ACT.Relu).then_inc(acted, 1)

        @block.vector
        def _(dve):
            for h in range(NH):
                cols = slice(h * HALF, (h + 1) * HALF)
                dve.wait_ge(acted, h + 1)
                if ups == 2:
                    dve.tensor_tensor(c.HT[:, 1, cols], c.HT[:, 1, cols], c.PS[:, 3 * h + 1, :],
                                      ALU.mult).then_inc(gated, 1)
                    dve.wait_ge(gated, h + 1)
                dve.tensor_tensor(c.HT[:, 0, cols], c.HT[:, 1, cols], c.PS[:, 3 * h + 2, :],
                                  ALU.mult).then_inc(hidden, 1)
            for h in range(NH):
                if add_tokens is not None:
                    t = slice(h * (NT // NH), (h + 1) * (NT // NH))
                    dve.wait_ge(down, (h + 1) * (NT // NH))
                    dve.tensor_tensor(add_tokens[:, t, :], add_tokens[:, t, :], c.tiles(6)[:, t, :],
                                      ALU.add).then_inc(added, 1)
                else:
                    cols = slice(h * HALF, (h + 1) * HALF)
                    dve.wait_ge(down, h + 1)
                    dve.tensor_tensor(add_turned[:, cols], add_turned[:, cols], c.PS[:, 6 + h, :],
                                      ALU.add).then_inc(added, 1)


def turn_gates(c, rows):
    with c.stage("gates_turned", "gates_out") as (block, turned, out_done):
        @block.tensor
        def _(pe):
            for t in range(NT):
                pe.transpose(c.banks(0)[0:rows, t * P:(t + 1) * P], c.gates[:, t, 0:rows],
                             c.ident[:, :]).then_inc(turned, 1)

        @block.scalar
        def _(act):
            act.wait_ge(turned, NT)
            act.activation(c.gatesT[0:rows, :], c.banks(0)[0:rows, :], ACT.Copy).then_inc(out_done, 1)


def route_experts(c, n):
    d = c.dram
    carry = c.carry[n]
    score, biased, left, chosen, weight, room = (c.small[:, k] for k in range(6))
    with c.stage("gw_loaded", "gw_cast", "logits_done", "sigmoid_done", "route_step", "counted",
                 "carry_ready", "carry_done") as \
            (block, loaded, cast_done, logits, sigm, step, counted, carry_ready, carry_done):
        @block.sync
        def _(sp):
            sp.dma_start(c.WB[:, 0, 0:EXPERTS], d["moe_gate"]).then_inc(loaded, 16)
            sp.dma_start(c.ebias[:, :], d["moe_bias"].partition_broadcast(P)).then_inc(loaded, 16)

        @block.gpsimd
        def _(pool):
            pool.wait_ge(loaded, 32)
            pool.tensor_copy(c.W1[:, 0, 0:EXPERTS], c.WB[:, 0, 0:EXPERTS]).then_inc(cast_done, 1)

        @block.tensor
        def _(pe):
            pe.wait_ge(cast_done, 1)
            for t in range(NT):
                mm = pe.matmul(c.PS[:, 0, t * EXPERTS:(t + 1) * EXPERTS], c.XT[:, t * P:(t + 1) * P],
                               c.W1[:, 0, 0:EXPERTS], start=True, stop=True)
            mm.then_inc(logits, 1)
            pe.wait_ge(step, NT + 2 + NT + 1)
            for t in range(NT):
                out = c.PS[:, 1, t * EXPERTS:(t + 1) * EXPERTS]
                pe.matmul(out, c.ones[0:1, 0:P], carry[:, :], start=True, stop=False)
                for s in range(t):
                    pe.matmul(out, c.ones[:, 0:P], chosen[:, s, :], start=False, stop=False)
                pe.matmul(out, c.before[:, :], chosen[:, t, :], start=False, stop=True).then_inc(counted, 1)
            out = c.PS[0:1, 2, 0:EXPERTS]
            pe.matmul(out, c.ones[0:1, 0:1], carry[:, :], start=True, stop=False)
            for s in range(NT):
                mm = pe.matmul(out, c.ones[:, 0:1], chosen[:, s, :], start=False, stop=s == NT - 1)
            mm.then_inc(carry_ready, 1)

        @block.scalar
        def _(act):
            act.wait_ge(logits, 1)
            act.activation(score, c.PS[:, 0, 0:NT * EXPERTS].rearrange("p (t e) -> p t e", e=EXPERTS),
                           ACT.Sigmoid).then_inc(sigm, 1)

        @block.vector
        def _(dve):
            at = 0

            def next_step(instruction):
                nonlocal at
                instruction.then_inc(step, 1)
                at += 1

            dve.wait_ge(sigm, 1)
            dve.wait_ge(loaded, 32)
            next_step(dve.tensor_tensor(biased, score, c.ebias[:, None, :].to_broadcast([P, NT, EXPERTS]), ALU.add))
            dve.wait_ge(step, at)
            for t in range(NT):
                next_step(dve.max(c.small8[:, t, :], biased[:, t, :]))
            dve.wait_ge(step, at)
            next_step(dve.memset(c.small8[:, :, TOPK:8], 3e38))
            dve.wait_ge(step, at)
            for t in range(NT):
                next_step(dve.match_replace(left[:, t, :], c.small8[:, t, :], biased[:, t, :], -3e38))
            dve.wait_ge(step, at)
            next_step(dve.tensor_tensor(chosen, left, biased, ALU.not_equal))
            dve.wait_ge(step, at)
            next_step(dve.tensor_tensor(weight, score, chosen, ALU.mult))
            dve.wait_ge(step, at)
            next_step(dve.tensor_reduce(c.gsum[:, 0, :], weight, AX_X, ALU.add))
            dve.wait_ge(step, at)
            next_step(dve.tensor_scalar(c.gsum[:, 0, :], c.gsum[:, 0, :], 1e-12, None, ALU.max))
            dve.wait_ge(step, at)
            next_step(dve.reciprocal(c.gsum[:, 1, :], c.gsum[:, 0, :]))
            dve.wait_ge(step, at)
            next_step(dve.tensor_tensor(weight, weight, c.gsum[:, 1, :, None].to_broadcast([P, NT, EXPERTS]), ALU.mult))
            dve.wait_ge(counted, NT)
            next_step(dve.tensor_scalar(room, c.PS[:, 1, 0:NT * EXPERTS].rearrange("p (t e) -> p t e", e=EXPERTS),
                                        float(CAPACITY), None, ALU.is_lt))
            dve.wait_ge(step, at)
            next_step(dve.tensor_tensor(c.gates[:, :, 0:EXPERTS], weight, room, ALU.mult))
            next_step(dve.memset(c.gates[:, :, EXPERTS:EXPERTS + 1], 1.0))
            next_step(dve.memset(c.gates[:, :, EXPERTS + 1:EXPERTS + 2], 0.0))
            dve.wait_ge(carry_ready, 1)
            dve.tensor_copy(carry[:, :], c.PS[0:1, 2, 0:EXPERTS]).then_inc(carry_done, 1)
    turn_gates(c, GATE_ROWS)


def route_leaves(c, node_w, node_b):
    yes, no = c.small[:, 0, :, 0:LEAVES], c.small[:, 1, :, 0:LEAVES]
    with c.stage("nodes_loaded", "nodes_done", "tree_step") as (block, loaded, nodes, step):
        @block.sync
        def _(sp):
            sp.dma_start(c.W1[:, 0, 0:LEAVES - 1], node_w).then_inc(loaded, 16)
            sp.dma_start(c.B1[:, 0, 0:LEAVES - 1], node_b).then_inc(loaded, 16)

        @block.tensor
        def _(pe):
            pe.wait_ge(loaded, 32)
            for t in range(NT):
                out = c.PS[:, 0, t * LEAVES:t * LEAVES + LEAVES - 1]
                pe.matmul(out, c.XT[:, t * P:(t + 1) * P], c.W1[:, 0, 0:LEAVES - 1], start=True, stop=False)
                mm = pe.matmul(out, c.ones[0:1, 0:P], c.B1[:, 0, 0:LEAVES - 1], start=False, stop=True)
            mm.then_inc(nodes, 1)

        @block.vector
        def _(dve):
            at = 0

            def next_step(instruction):
                nonlocal at
                instruction.then_inc(step, 1)
                at += 1

            dve.wait_ge(nodes, 1)
            score = c.PS[:, 0, 0:NT * LEAVES].rearrange("p (t e) -> p t e", e=LEAVES)[:, :, 0:LEAVES - 1]
            next_step(dve.tensor_scalar(yes[:, :, 0:LEAVES - 1], score, 0.0, None, ALU.is_ge))
            dve.wait_ge(step, at)
            next_step(dve.tensor_scalar(no[:, :, 0:LEAVES - 1], yes[:, :, 0:LEAVES - 1], -1.0, 1.0, ALU.mult, ALU.add))
            dve.wait_ge(step, at)
            path = c.small[:, 2, :, 0:2]
            next_step(dve.tensor_copy(path[:, :, 0:1], no[:, :, 0:1]))
            next_step(dve.tensor_copy(path[:, :, 1:2], yes[:, :, 0:1]))
            n, k = 2, 3
            while n < LEAVES:
                dve.wait_ge(step, at)
                wide = c.small[:, k, :, 0:2 * n] if 2 * n < LEAVES else c.gates[:, :, 0:LEAVES]
                split = wide.rearrange("p t (i s) -> p t i s", s=2)
                next_step(dve.tensor_tensor(split[:, :, :, 0], path, no[:, :, n - 1:2 * n - 1], ALU.mult))
                next_step(dve.tensor_tensor(split[:, :, :, 1], path, yes[:, :, n - 1:2 * n - 1], ALU.mult))
                path, n, k = wide, 2 * n, k + 1
    turn_gates(c, LEAVES)


def leaf_bias(c, b2, turned=None, tokens=None):
    with c.stage("b2_loaded", "b2_done", "b2_out") as (block, loaded, done, out_done):
        @block.sync
        def _(sp):
            sp.dma_start(c.SEL[0:LEAVES, :], b2).then_inc(loaded, 16)

        @block.tensor
        def _(pe):
            pe.wait_ge(loaded, 16)
            if turned is not None:
                for h in range(NH):
                    mm = pe.matmul(c.PS[:, h, :], c.SEL[0:LEAVES, :], c.gatesT[0:LEAVES, h * HALF:(h + 1) * HALF],
                                   start=True, stop=True)
            else:
                for t in range(NT):
                    mm = pe.matmul(c.tiles(0)[:, t, :], c.gatesT[0:LEAVES, t * P:(t + 1) * P], c.SEL[0:LEAVES, :],
                                   start=True, stop=True)
            mm.then_inc(done, 1)

        @block.scalar
        def _(act):
            act.wait_ge(done, 1)
            if turned is not None:
                act.activation(turned[:, :], c.banks(0), ACT.Copy).then_inc(out_done, 1)
            else:
                act.activation(tokens, c.tiles(0), ACT.Copy).then_inc(out_done, 1)


def shorten_q_k(c, keys=S):
    with c.stage("short_q", "short_k") as (block, short_q, short_k):
        @block.scalar
        def _(act):
            act.activation(c.QB[:, :], c.QT[:, :], ACT.Copy).then_inc(short_q, 1)

        @block.vector
        def _(dve):
            dve.tensor_copy(c.KB[:, 0:keys], c.KT[:, 0:keys]).then_inc(short_k, 1)


def whole_out(c):
    return lambda h, half: c.CTX[:, 4 * half:4 * half + 4, :]



def local_transformer(c):
    d = c.dram
    norm_and_turn(c, c.X, norm=c.Y)
    for layer in range(2):
        norm_and_turn(c, c.Y, shift=True)
        with c.stage("qk_scales") as (block, loaded):
            @block.sync
            def _(sp):
                sp.dma_start(c.gcols[:, :], d["l0f_scales"][layer]).then_inc(loaded, 16)
                sp.wait_ge(loaded, 16)
        attention64(c, c.Y, d["l0f_w"][layer], d["l0f_wo"][layer], 4, "window", 8.0, xpos=c.xpos)
        shift_tokens(c, c.Y)
        norm_and_turn(c, c.H, norm=c.CTX, gains=d["l0f_ln"][layer])
        mlp(c, c.Y, d["l0f_w1"][layer], d["l0f_b1"][layer], d["l0f_w2"][layer], d["l0f_b2"][layer], 3, True)
    add_to(c, c.X, c.Y[:, :, :])


def mixture(c, n):
    d = c.dram
    norm_and_turn(c, c.X, norm=c.Y)
    route_experts(c, n)
    with c.nc.Fori(0, GATE_ROWS // 2) as i:
        experts(c, i, d["moe_w"], d["moe_w2"], d["c_sel34"], GATE_ROWS, cast=True, add_tokens=c.X)


def transformer_block(c):
    d = c.dram
    norm_and_turn(c, c.X, norm=c.Y)
    norm_and_turn(c, c.Y, norm=c.H, gains=d["l1b_ln1"])
    attention8(c, d["l1b_w"], d["l1b_b"], "causal", rope=c.rope8)
    project_out(c, c.Y, d["l1b_wo"], d["l1b_bo"])
    norm_and_turn(c, c.Y, norm=c.H, gains=d["l1b_ln2"])
    mlp(c, c.Y, d["l1b_w1"], d["l1b_b1"], d["l1b_w2"], d["l1b_b2"], 4, False)
    add_to(c, c.X, c.Y[:, :, :])


def adapted_mlp(c):
    d = c.dram
    norm_and_turn(c, c.X, norm=c.Y)
    with c.stage("lora_loaded", "lora_scaled", "lora_rows", "lora_sum") as (block, loaded, scaled, rows, summed):
        @block.sync
        def _(sp):
            sp.dma_start(c.W1[:, 0:4, :], d["l2f_w1"]).then_inc(loaded, 16)
            sp.dma_start(c.W2[:, :, :], d["l2f_w2"]).then_inc(loaded, 16)
            sp.dma_start(c.odd[:, 8:9], d["l2f_scale"].partition_broadcast(P)).then_inc(loaded, 16)

        @block.tensor
        def _(pe):
            for j in range(8):
                pe.matmul(c.tiles(0)[:, j, :], c.pick8[:, j, :], c.Y[:, 0, :], start=True, stop=True).then_inc(rows, 1)

        @block.vector
        def _(dve):
            dve.wait_ge(loaded, 48)
            dve.tensor_scalar(c.odd[:, 0:8], c.XT[:, 2:18:2], c.odd[:, 8:9], None, ALU.mult).then_inc(scaled, 1)
            dve.wait_ge(scaled, 1)
            dve.wait_ge(rows, 8)
            for j in range(4):
                dve.scalar_tensor_tensor(c.W1E[:, j, :], c.tiles(0)[:, j, :], c.odd[:, j:j + 1], c.W1[:, j, :],
                                         ALU.mult, ALU.add).then_inc(summed, 1)
            for j in range(4):
                for r in range(4):
                    dve.scalar_tensor_tensor(c.W2E[:, r, 32 * j:32 * j + 32],
                                             c.tiles(0)[:, 4 + j, r:P:4], c.odd[:, 4 + j:5 + j],
                                             c.W2[:, r, 32 * j:32 * j + 32],
                                             ALU.mult, ALU.add).then_inc(summed, 1)
    mlp(c, c.X, None, d["l2f_b1"], None, d["l2f_b2"], 4, False, batch_weights=True)


def single_head(c):
    heads = Heads(P, 1, P, P ** -0.5, "causal")
    norm_and_turn(c, c.X, norm=c.Y)
    clear_v(c)
    project(c, c.dram["l2a_w"], heads, bias=c.dram["l2a_b"])
    attend(c, heads, whole_out(c))
    add_to(c, c.X, c.CTX[:, :, :])


def cross_attention(c):
    d = c.dram
    keys = 512
    heads = Heads(P, 1, P, 1.0, "full", keys=keys)
    norm_and_turn(c, c.X, norm=c.Y)
    clear_v(c)
    with c.stage("kv_loaded", "v_in", "k_scaled", "k_turned", "k_out") as (block, loaded, v_in, k_scaled, turned, k_out):
        @block.sync
        def _(sp):
            sp.dma_start(c.W1[:, 0:4, :], d["l3a_k"].rearrange("(t p) d -> p t d", p=P)).then_inc(loaded, 16)
            sp.dma_start(c.VA[:, 0:4, 0:P], d["l3a_v"].rearrange("(t p) d -> p t d", p=P)).then_inc(v_in, 16)
            sp.wait_ge(v_in, 16)

        @block.vector
        def _(dve):
            dve.wait_ge(loaded, 16)
            for t in range(4):
                dve.tensor_scalar(c.W1E[:, t, :], c.W1[:, t, :], c.XT[:, 256 * t:256 * t + 1], None,
                                  ALU.mult).then_inc(k_scaled, 1)

        @block.tensor
        def _(pe):
            for t in range(4):
                pe.wait_ge(k_scaled, t + 1)
                pe.transpose(c.PS[:, 0, t * P:(t + 1) * P], c.W1E[:, t, :], c.ident[:, :]).then_inc(turned, 1)

        @block.scalar
        def _(act):
            act.activation(c.QT[:, :], c.XT[:, :], ACT.Copy).then_inc(k_out, 1)
            act.wait_ge(turned, 4)
            act.activation(c.KT[:, 0:keys], c.PS[:, 0, :], ACT.Copy).then_inc(k_out, 1)
    shorten_q_k(c, keys)
    attend(c, heads, whole_out(c))
    add_to(c, c.X, c.CTX[:, :, :])


def tree_attention(c):
    d = c.dram
    heads = Heads(P, 1, P, P ** -0.5, "full")
    norm_and_turn(c, c.X, norm=c.Y)
    clear_v(c)
    for name, turned in (("q", c.QT), ("k", c.KT), ("v", None)):
        tokens = None if turned is not None else c.VA[:, :, 0:P]
        route_leaves(c, d[f"l3f_{name}_node"], d[f"l3f_{name}_nodeb"])
        leaf_bias(c, d[f"l3f_{name}_b2"], turned, tokens)
        with c.nc.Fori(0, LEAVES // 2) as i:
            experts(c, i, d[f"l3f_{name}_w1"], d[f"l3f_{name}_w2"], d["c_sel16"], LEAVES, bias=d[f"l3f_{name}_b1"],
                    add_tokens=tokens, add_turned=turned)
    shorten_q_k(c)
    attend(c, heads, whole_out(c))
    add_to(c, c.X, c.CTX[:, :, :])


def latent_attention(c):
    d = c.dram
    norm_and_turn(c, c.X, norm=c.Y)
    with c.stage("lat_loaded", "lat_mm", "lat_out", "lat_zero", "lat_stored") as (block, loaded, mm_done, out_done, zeroed, stored):
        dq, uqT, dkv = (c.W1[0:64, s, :] for s in (0, 1, 3))
        uk, uv = c.W1[:, 2, 0:64], c.W1[:, 4, 0:64]
        woT = c.W1[:, 5, :]
        aT, keT, veT = c.W2[:, 0, :], c.W2[0:64, 1, :], c.W2[0:64, 2, :]
        wide = c.HT[:, 0:2, :].rearrange("p a n -> p (a n)")[:, 0:4 * 3 * P].rearrange("p (g s n) -> p g s n", g=4, s=3)

        @block.sync
        def _(sp):
            for dst, src in ((dq, "dq"), (uqT, "uqT"), (dkv, "dkv"), (uk, "uk"), (uv, "uv"), (woT, "woT")):
                sp.dma_start(dst, d[f"l3b_{src}"]).then_inc(loaded, 16)
            sp.wait_ge(out_done, 6)
            sp.dma_start(d["scratch_w"].rearrange("g p s n -> p g s n"), wide).then_inc(stored, 16)
            sp.wait_ge(stored, 16)

        @block.tensor
        def _(pe):
            pe.wait_ge(loaded, 96)
            pe.matmul(c.PS[:, 0, 0:P], uqT, dq, start=True, stop=True).then_inc(mm_done, 1)
            pe.matmul(c.PS[0:64, 1, 0:P], uv, woT, start=True, stop=True).then_inc(mm_done, 1)
            pe.matmul(c.PS[:, 2, 0:P], dq, uqT, start=True, stop=True).then_inc(mm_done, 1)
            pe.wait_ge(out_done, 1)
            pe.matmul(c.PS[0:64, 3, 0:P], uk, aT, start=True, stop=True).then_inc(mm_done, 1)
            pe.wait_ge(out_done, 3)
            pe.matmul(c.PS[:, 4, 0:P], dkv, keT, start=True, stop=True).then_inc(mm_done, 1)
            pe.matmul(c.PS[:, 5, 0:P], dkv, veT, start=True, stop=True).then_inc(mm_done, 1)

        @block.vector
        def _(dve):
            dve.memset(wide, 0.0).then_inc(zeroed, 1)
            dve.wait_ge(mm_done, 1)
            dve.tensor_copy(aT, c.PS[:, 0, 0:P]).then_inc(out_done, 1)
            dve.wait_ge(mm_done, 2)
            dve.tensor_copy(veT, c.PS[0:64, 1, 0:P]).then_inc(out_done, 1)
            dve.wait_ge(mm_done, 4)
            dve.tensor_copy(keT, c.PS[0:64, 3, 0:P]).then_inc(out_done, 1)
            dve.wait_ge(zeroed, 1)
            dve.wait_ge(mm_done, 6)
            for s, bank in enumerate((2, 4, 5)):
                for g in range(4):
                    ins = dve.tensor_copy(wide[:, g, s, :].rearrange("p (h w) -> p h w", w=32)[:, :, 0:8],
                                          c.PS[:, bank, 32 * g:32 * g + 32].rearrange("p (h e) -> p h e", e=8))
                ins.then_inc(out_done, 1)
    attention8(c, d["scratch_w"], None, "causal")
    add_to(c, c.X, c.CTX[:, :, :])


def network(nc, dram):
    with ExitStack() as ctx:
        c = Core(nc, ctx, dram)
        d = dram
        load_constants(c)

        def gqa():
            norm_and_turn(c, c.X, norm=c.Y)
            attention64(c, c.X, d["l0a_w"], d["l0a_wo"], 8, "causal", 0.125, rope=c.rope64)

        def mha():
            norm_and_turn(c, c.X, norm=c.Y)
            clear_v(c)
            with c.stage("wo_loaded") as (block, loaded):
                @block.sync
                def _(sp):
                    w = c.HT[:, 0:2, :].rearrange("p a (m n) -> p (a m) n", n=P)
                    sp.dma_start(w, d["l0b_wo"]).then_inc(loaded, 16)
                    sp.wait_ge(loaded, 16)
            heads = Heads(64, 2, 64, 0.125, "full")
            with nc.Fori(0, 8) as pair:
                project(c, one(d["l0b_w"], pair), heads)
                attend(c, heads, pair_out(c))
                project_rows_out(c, pair)

        def small_full():
            norm_and_turn(c, c.X, norm=c.Y)
            attention8(c, d["l1a_w"], d["l1a_b"], "full")
            project_out(c, c.X, d["l1a_wo"], d["l1a_bo"])

        def small_causal():
            norm_and_turn(c, c.X, norm=c.Y)
            attention8(c, d["l2b_w"], d["l2b_b"], "causal")
            project_out(c, c.X, d["l2b_wo"], d["l2b_bo"])

        layers = [gqa, lambda: local_transformer(c), mha, lambda: local_transformer(c),
                  small_full, lambda: mixture(c, 0), lambda: transformer_block(c), lambda: mixture(c, 1),
                  lambda: single_head(c), lambda: adapted_mlp(c), small_causal, lambda: adapted_mlp(c),
                  lambda: cross_attention(c), lambda: tree_attention(c), lambda: latent_attention(c),
                  lambda: tree_attention(c)]
        with nc.Fori(0, 2) as b:
            load_x(c, b)
            for layer in layers:
                layer()
            store_x(c, b)



def constants():
    f = np.float32
    i = np.arange(P)
    q, k = i[:, None], i[None, :]
    causal = np.where(k > q, f(NEG), f(0))
    old = np.where(q + P - k > 64, f(NEG), f(0))
    near = np.where((k > q) | (q - k > 64), f(NEG), f(0))
    out = {"c_ident": np.eye(P, dtype=f), "c_before": (q < k).astype(f),
           "c_block1": (q // 64 == k // 64).astype(f)}
    out["c_masks"] = np.stack([causal, causal.T, near, near.T, old, old.T], 1).astype(f)
    out["c_first"] = np.zeros((P, 3, P), f)
    for n, pitch in enumerate((32, 64, 128)):
        out["c_first"][::pitch, n] = 1
    pick = np.zeros((P, 8, P), f)
    for j in range(8):
        pick[1 + 2 * j, j, :] = 1
    out["c_pick8"] = pick
    t = np.arange(S, dtype=f)

    def frequencies(dim):
        return (f(1) / np.power(f(10000), np.arange(0, dim, 2, dtype=f) / f(dim))).astype(f)

    fr = t[None, :] * frequencies(64)[:, None]
    cos, sin = np.cos(fr), np.sin(fr)
    out["c_rope64"] = np.stack([np.tile(cos, (4, 1)), np.concatenate([-sin, sin] * 2)], 1).astype(f)
    base = ((np.arange(0, 64, 2, dtype=f) + f(0.4 * 64)) / f(1.4 * 64)).astype(f)
    power = ((t - f(S // 2)) / f(32)).astype(f)
    scale = np.power(base[:, None], power[None, :]).astype(f)
    out["c_xpos"] = np.stack([np.tile(cos * scale, (4, 1)), np.concatenate([-sin * scale, sin * scale] * 2),
                              np.tile(cos / scale, (4, 1)), np.concatenate([-sin / scale, sin / scale] * 2)],
                             1).astype(f)
    fr8 = t[None, :] * frequencies(8)[:, None]
    rope8 = np.zeros((4, 32, 2, S), f)
    rope8[:, 0:8, 0] = np.tile(np.cos(fr8), (2, 1))
    rope8[:, 0:8, 1] = np.concatenate([-np.sin(fr8), np.sin(fr8)])
    out["c_rope8"] = rope8.reshape(P, 2, S)
    for name, rows in (("c_sel34", GATE_ROWS), ("c_sel16", LEAVES)):
        sel = np.zeros((rows // 2, rows, P), f)
        for n in range(rows // 2):
            sel[n, 2 * n, 0:64] = 1
            sel[n, 2 * n + 1, 64:P] = 1
        out[name] = sel
    return out


def swap_halves(w, dim):
    lead = w.shape[:-1]
    v = w.reshape(*lead, -1, 2, dim // 2)
    return v[..., ::-1, :].reshape(w.shape)


def by_pairs(parts, n_pairs):
    return np.ascontiguousarray(np.stack([w.reshape(w.shape[0], n_pairs, P) for w in parts], 2).transpose(1, 0, 2, 3))


def by_fours(parts):
    rows = parts[0].shape[0]
    out = np.zeros((4, rows, len(parts), 4, 32), parts[0].dtype)
    for s, w in enumerate(parts):
        out[:, :, s, :, 0:8] = w.reshape(rows, 4, 4, 8).transpose(1, 0, 2, 3)
    return out.reshape(4, rows, len(parts), P)


def by_chunks(w, n):
    return np.ascontiguousarray(w.reshape(n, P, w.shape[-1]).transpose(1, 0, 2))


def layouts(a):
    d = {"x": a["L0_attn_a_x"]}

    def doubled(w):
        return np.broadcast_to(w.reshape(P, 4, 1, 64), (P, 4, 4, 64)).reshape(P, 1024)

    q, k, v = a["L0_attn_a_wq"], doubled(a["L0_attn_a_wk"]), doubled(a["L0_attn_a_wv"])
    d["l0a_w"] = by_pairs([q, swap_halves(q, 64), k, swap_halves(k, 64), v], 8)
    d["l0a_wo"] = a["L0_attn_a_wo"].reshape(8, P, P)
    w = a["L0_attn_b_W_qkv"]
    d["l0b_w"] = by_pairs([w[:, 0:1024], w[:, 1024:2048], w[:, 2048:]], 8)
    d["l0b_wo"] = np.concatenate([a["L0_attn_b_W_out"].reshape(16, 64, P).transpose(1, 0, 2)] * 2)

    stacks = {"w": [], "wo": [], "scales": [], "ln": [], "w1": [], "b1": [], "w2": [], "b2": []}
    hid = a["L0_ffn_w2"].shape[1]
    for n in range(2):
        w = a["L0_ffn_wqkv"][n]
        q, k, v = w[:, 0:512], w[:, 512:1024], w[:, 1024:]
        stacks["w"].append(by_pairs([q, swap_halves(q, 64), k, swap_halves(k, 64), v], 4))
        stacks["wo"].append(a["L0_ffn_wo"][n].reshape(4, P, P))
        qs, ks = a["L0_ffn_q_scale"][n], a["L0_ffn_k_scale"][n]
        stacks["scales"].append(np.stack([np.tile(s, 2) for s in (qs, swap_halves(qs, 64), ks, swap_halves(ks, 64))], 1))
        stacks["ln"].append(np.stack([a["L0_ffn_ln_g"][n], a["L0_ffn_ln_b"][n]], 1))
        w1 = np.zeros((P, 2, 3 * P), np.float32)
        w1[:, :, 0:hid] = a["L0_ffn_w1"][n].reshape(P, 2, hid)
        b1 = np.zeros((1, 2, 3 * P), np.float32)
        b1[:, :, 0:hid] = a["L0_ffn_b1"][n].reshape(1, 2, hid)
        w2 = np.zeros((3 * P, P), np.float32)
        w2[0:hid] = a["L0_ffn_w2"][n]
        stacks["w1"].append(w1.reshape(P, 6, P))
        stacks["b1"].append(b1.reshape(1, 6, P))
        stacks["w2"].append(by_chunks(w2, 3))
        stacks["b2"].append(a["L0_ffn_b2"][n].reshape(1, P))
    for name, parts in stacks.items():
        d[f"l0f_{name}"] = np.stack(parts)

    def thirds(w):
        return [w[..., 0:128], w[..., 128:256], w[..., 256:384]]

    d["l1a_w"] = by_fours(thirds(a["L1_attn_a_w_qkv"]))
    d["l1a_b"] = by_fours(thirds(a["L1_attn_a_b_qkv"].reshape(1, 384)))
    d["l1a_wo"], d["l1a_bo"] = a["L1_attn_a_w_proj"], a["L1_attn_a_b_proj"].reshape(1, P)
    for name, w in (("l1b_w", a["L1_attn_b_Wqkv"]), ("l1b_b", a["L1_attn_b_bqkv"].reshape(1, 384))):
        q, k, v = thirds(w)
        d[name] = by_fours([q, swap_halves(q, 8), k, swap_halves(k, 8), v])
    d["l1b_wo"], d["l1b_bo"] = a["L1_attn_b_Wo"], a["L1_attn_b_bo"].reshape(1, P)
    d["l1b_ln1"] = np.stack([a["L1_attn_b_ln1_g"], a["L1_attn_b_ln1_b"]], 1)
    d["l1b_ln2"] = np.stack([a["L1_attn_b_ln2_g"], a["L1_attn_b_ln2_b"]], 1)
    d["l1b_w1"], d["l1b_b1"] = a["L1_attn_b_W1"].reshape(P, 4, P), a["L1_attn_b_b1"].reshape(1, 4, P)
    d["l1b_w2"], d["l1b_b2"] = by_chunks(a["L1_attn_b_W2"], 4), a["L1_attn_b_b2"].reshape(1, P)

    dt = a["L1_ffn_W1"].dtype
    w = np.zeros((GATE_ROWS, P, 2, 64), dt)
    w[0:EXPERTS, :, 0], w[0:EXPERTS, :, 1] = a["L1_ffn_W1"], a["L1_ffn_W3"]
    w[EXPERTS, :, 0], w[EXPERTS, :, 1] = a["L1_ffn_sw1"].T, a["L1_ffn_sw3"].T
    d["moe_w"] = np.ascontiguousarray(w.reshape(GATE_ROWS // 2, 2, P, 2, 64).transpose(0, 2, 3, 1, 4)
                                      ).reshape(GATE_ROWS // 2, P, 2, P)
    w2 = np.zeros((GATE_ROWS, 64, P), dt)
    w2[0:EXPERTS], w2[EXPERTS] = a["L1_ffn_W2"], a["L1_ffn_sw2"].T
    d["moe_w2"] = w2.reshape(GATE_ROWS // 2, P, P)
    d["moe_gate"] = a["L1_ffn_gate_w"].T
    d["moe_bias"] = a["L1_ffn_bias"].reshape(EXPERTS)

    d["l2a_w"] = np.stack([a[f"L2_attn_a_W{s}"].T for s in "qkv"], 1)
    d["l2a_b"] = np.stack([a[f"L2_attn_a_b{s}"] for s in "qkv"]).reshape(1, 3, P)
    d["l2b_w"] = by_fours([a[f"L2_attn_b_W{s}"] for s in "qkv"])
    d["l2b_b"] = by_fours([a[f"L2_attn_b_b{s}"].reshape(1, P) for s in "qkv"])
    d["l2b_wo"], d["l2b_bo"] = a["L2_attn_b_Wo"], a["L2_attn_b_bo"].reshape(1, P)
    d["l2f_w1"], d["l2f_b1"] = a["L2_ffn_W1"].T.reshape(P, 4, P), a["L2_ffn_b1"].reshape(1, 4, P)
    d["l2f_w2"], d["l2f_b2"] = by_chunks(a["L2_ffn_W2"].T, 4), a["L2_ffn_b2"].reshape(1, P)
    d["l2f_scale"] = a["L2_ffn_scale"].reshape(1)

    d["l3a_k"], d["l3a_v"] = a["L3_attn_a_k"][0], a["L3_attn_a_v"][0]
    for s in "qkv":
        d[f"l3f_{s}_node"], d[f"l3f_{s}_nodeb"] = a[f"L3_ffn_{s}_node_w"].T, a[f"L3_ffn_{s}_node_b"].reshape(1, 15)
        d[f"l3f_{s}_w1"] = np.ascontiguousarray(a[f"L3_ffn_{s}_w1"].reshape(8, 2, P, 64).transpose(0, 2, 1, 3)
                                                ).reshape(8, P, 1, P)
        d[f"l3f_{s}_b1"] = a[f"L3_ffn_{s}_b1"].reshape(8, 1, P)
        d[f"l3f_{s}_w2"] = a[f"L3_ffn_{s}_w2"].reshape(8, P, P)
        d[f"l3f_{s}_b2"] = a[f"L3_ffn_{s}_b2"]
    for s in ("dq", "dkv", "uk", "uv"):
        d[f"l3b_{s}"] = a[f"L3_attn_b_W_{s}"]
    d["l3b_uqT"], d["l3b_woT"] = a["L3_attn_b_W_uq"].T, a["L3_attn_b_W_o"].T
    return d


def kernel(**inputs):
    import concourse.bacc as _bacc
    from concourse.bass_utils import run_bass_kernel_spmd as _run

    nc = _bacc.Bacc("TRN2", target_bir_lowering=False, num_devices=1)
    arrays, dram = {}, {}
    for name, value in {**layouts({k: np.asarray(v) for k, v in inputs.items()}), **constants()}.items():
        value = np.ascontiguousarray(value)
        arrays[f"in_{name}"] = value
        dram[name] = nc.dram_tensor(f"in_{name}", value.shape, mybir.dt.from_np(value.dtype), kind="ExternalInput").ap()
    dram["scratch_w"] = nc.dram_tensor("latent_weights", (4, P, 3, P), F32).ap()
    dram["out"] = nc.dram_tensor("out", (2, S, P), F32, kind="ExternalOutput").ap()
    network(nc, dram)
    return _run(nc, [arrays], core_ids=[0]).results[0]["out"]
```

```python
from contextlib import ExitStack, contextmanager

import numpy as np

import concourse.bass as bass
from concourse import mybir

F32 = mybir.dt.float32
BF16 = mybir.dt.bfloat16
ALU = mybir.AluOpType
ACT = mybir.ActivationFunctionType
AX_X = mybir.AxisListType.X

P = 128
S = 1024
NT = S // P
HALF = 512
NH = S // HALF
NEG = -1e30
EXPERTS, TOPK, CAPACITY = 32, 4, 128
GATE_ROWS = EXPERTS + 2
LEAVES = 16


class Core:

    def __init__(self, nc, ctx, dram):
        self.nc, self.ctx, self.dram = nc, ctx, dram
        self.sems = {}

        def sb(name, shape, dt=F32):
            return ctx.enter_context(nc.sbuf_tensor(name, shape, dt))

        self.sb = sb
        self.X = sb("residual", [P, NT, P])
        self.Y = sb("normalised", [P, NT, P])
        self.H = sb("shifted", [P, NT, P])
        self.XT = sb("x_t", [P, S])
        self.QT, self.KT = sb("q_t", [P, S]), sb("k_t", [P, S])
        self.QB, self.KB = sb("q_t_bf16", [P, S], BF16), sb("k_t_bf16", [P, S], BF16)
        self.QS, self.KS = sb("q_pieces", [P, 4, S], BF16), sb("k_pieces", [P, 4, S], BF16)
        self.T1, self.T2 = sb("turned", [P, S]), sb("squares", [P, S])
        self.VA = sb("v_and_ones", [P, NT, 136])
        self.K3 = sb("k_third", [P, 2, S], BF16)
        self.onehot = sb("onehot", [P, 4])
        self.coef64 = sb("piece_coefs64", [P, 3])
        self.probs8 = sb("probs8_t", [P, 3, 4, HALF])
        self.rowmax = sb("row_max", [P, 2, 4, 4, 2])
        self.negmax8 = sb("neg_max8", [P, 2, 4, 4], BF16)
        self.out8 = sb("out8_t", [P, 2, HALF])
        self.rden8 = sb("rden8", [P, 2, 4, 4])
        self.wrows = self.probs8[:, 0, :, :].rearrange("p a (m n) -> p (a m) n", n=P)
        self.vbias = sb("v_bias", [P, P])
        self.bcols = sb("bias_columns", [P, 6])
        self.CTX, self.CT = sb("context", [P, NT, P]), sb("context_t", [P, S])
        self.HT = sb("hidden_t", [P, 4, S])
        self.rest = self.HT[:, 0:2, :]
        self.top = self.HT[:, 2, :].bitcast(BF16).rearrange("p (n s) -> p n s", n=2)
        self.mid = self.HT[:, 3, :].bitcast(BF16).rearrange("p (n s) -> p n s", n=2)
        self.stats, self.mv = sb("ln_stats", [P, NT, 6]), sb("ln_mean_var", [P, NT, 2])
        self.rstd = sb("ln_rstd", [P, NT, 2])
        self.W = sb("w_qkv", [P, 9, P])
        self.WO, self.BO = sb("w_out", [P, P]), sb("b_out", [1, P])
        self.W1, self.B1 = sb("w_up", [P, 6, P]), sb("b_up", [1, 6, P])
        self.W2, self.B2 = sb("w_down", [P, 4, P]), sb("b_down", [1, P])
        self.W1E, self.W2E = sb("w_up_eff", [P, 4, P]), sb("w_down_eff", [P, 4, P])
        self.WB = sb("w_bf16", [P, 3, P], BF16)
        self.SEL, self.selb = sb("pick_rows", [3 * GATE_ROWS, 4, P]), sb("pick_rows_bf16", [3 * GATE_ROWS, 4, P], BF16)
        self.gcols = sb("gain_bias", [P, 4])
        self.gates = sb("gates", [P, NT, GATE_ROWS])
        self.gates_rest = sb("gates_rest", [P, NT, GATE_ROWS])
        self.gate_pieces = sb("gate_pieces", [P, NT, 3 * GATE_ROWS], BF16)
        self.gatesT = sb("gates_t", [3 * GATE_ROWS, S], BF16)
        self.EW, self.EW2 = sb("w_pair_up", [P, 4, 1, P]), sb("w_pair_down", [P, 4, P])
        self.EWB = self.KS[:, 0, :].rearrange("p (i u n) -> p i u n", i=4, u=2)
        self.EW2B = self.KS[:, 1, 0:4 * P].rearrange("p (i n) -> p i n", i=4)
        self.small = sb("small", [P, 6, NT, EXPERTS])
        self.small8 = sb("top8", [P, NT, 8])
        self.gsum = sb("gate_sums", [P, 2, NT])
        self.ebias = sb("expert_bias", [P, EXPERTS])
        self.carry = [sb(f"expert_count_{n}", [1, EXPERTS]) for n in range(2)]
        self.probs = sb("probs_t", [P, 3, HALF])
        self.negmax = sb("neg_max", [P, 2, 4], BF16)
        self.negmax_row = sb("neg_max_row", [P, 2, HALF], BF16)
        self.rden = sb("rden", [P, 4, 1])
        self.odd = sb("odd_scaled", [P, 9])
        self.ident, self.identb = sb("ident", [P, P]), sb("ident_bf16", [P, P], BF16)
        self.masks = sb("masks", [P, 6, P], BF16)
        self.before = sb("before", [P, P])
        self.block1 = sb("block_ones", [P, P])
        self.pick8 = sb("pick8", [P, 8, P])
        self.ones = sb("ones", [P, HALF])
        self.first = sb("first_rows", [P, 3, P], BF16)
        self.rep = sb("replicate", [P, 4, P])
        self.coef = sb("piece_coefs", [P, 4])
        self.rope64 = sb("rope64", [P, 2, S])
        self.rope8 = sb("rope8", [P, 2, S])
        self.xpos = sb("xpos", [P, 4, S])
        self.PS = ctx.enter_context(nc.psum_tensor("psum", [P, 8, HALF], F32))

    def banks(self, first, n=2):
        return self.PS[:, first:first + n, :].rearrange("p b n -> p (b n)")

    def tiles(self, first):
        return self.banks(first).rearrange("p (t d) -> p t d", d=P)

    @contextmanager
    def stage(self, *names):
        for n in names:
            if n not in self.sems:
                self.sems[n] = self.ctx.enter_context(self.nc.semaphore(n))
        sems = [self.sems[n] for n in names]
        with self.nc.Block() as block:
            yield [block] + sems
        for s in sems:
            self.nc.gpsimd.sem_clear(s)
        self.nc.all_engine_barrier()


def one(ap, i):
    v = ap[bass.ds(i, 1)]
    names = "abcd"[:len(v.shape) - 1]
    if len(names) == 1:
        return v
    return v.rearrange(f"z {' '.join(names)} -> (z {names[0]}) {' '.join(names[1:])}")



def load_constants(c):
    d = c.dram
    with c.stage("const_loaded", "const_set") as (block, loaded, const_set):
        todo = [(c.ident, d["c_ident"]), (c.before, d["c_before"]), (c.block1, d["c_block1"]),
                (c.pick8, d["c_pick8"]), (c.rep, d["c_rep"]), (c.coef, d["c_coef"]), (c.coef64, d["c_coef64"]), (c.rope64, d["c_rope64"]), (c.rope8, d["c_rope8"]), (c.xpos, d["c_xpos"])]

        @block.sync
        def _(sp):
            for dst, src in todo:
                sp.dma_start(dst[:], src).then_inc(loaded, 16)
            sp.dma_start(c.H[:, 0:6, :], d["c_masks"]).then_inc(loaded, 16)
            sp.dma_start(c.Y[:, 0:3, :], d["c_first"]).then_inc(loaded, 16)
            sp.dma_start(c.onehot[96:100, :], d["c_ident"][0:4, 0:4]).then_inc(loaded, 16)

        @block.vector
        def _(dve):
            dve.memset(c.ones[:, :], 1.0).then_inc(const_set, 1)
            dve.memset(c.negmax_row[:, :, :], 0.0).then_inc(const_set, 1)
            dve.memset(c.carry[0][:, :], 0.0).then_inc(const_set, 1)
            dve.memset(c.carry[1][:, :], 0.0).then_inc(const_set, 1)
            dve.wait_ge(loaded, 16 * (len(todo) + 3))
            dve.tensor_copy(c.identb[:, :], c.ident[:, :]).then_inc(const_set, 1)
            dve.tensor_copy(c.masks[:, :, :], c.H[:, 0:6, :]).then_inc(const_set, 1)
            dve.tensor_copy(c.first[:, :, :], c.Y[:, 0:3, :]).then_inc(const_set, 1)


def load_x(c, b):
    with c.stage("x_loaded") as (block, loaded):
        @block.sync
        def _(sp):
            sp.dma_start(c.X[:, :, :], one(c.dram["x"], b).rearrange("(t p) d -> p t d", p=P)).then_inc(loaded, 16)
            sp.wait_ge(loaded, 16)


def store_x(c, b):
    with c.stage("x_stored") as (block, stored):
        @block.sync
        def _(sp):
            sp.dma_start(one(c.dram["out"], b).rearrange("(t p) d -> p t d", p=P), c.X[:, :, :]).then_inc(stored, 16)
            sp.wait_ge(stored, 16)


def add_to(c, target, part):
    with c.stage("added") as (block, added):
        @block.vector
        def _(dve):
            dve.tensor_tensor(target[:, :, :], target[:, :, :], part, ALU.add).then_inc(added, 1)


def shift_tokens(c, src):
    with c.stage("shift_done", "shift_dma") as (block, done, moved):
        @block.vector
        def _(dve):
            dve.tensor_copy(c.H[:, :, 0:64], src[:, :, 0:64]).then_inc(done, 1)
            dve.memset(c.H[0:1, 0:1, 64:P], 0.0).then_inc(done, 1)

        @block.sync
        def _(sp):
            sp.dma_start(c.H[1:P, :, 64:P], src[0:P - 1, :, 64:P]).then_inc(moved, 16)
            sp.dma_start(c.H[0:1, 1:NT, 64:P], src[P - 1:P, 0:NT - 1, 64:P]).then_inc(moved, 16)
            sp.wait_ge(moved, 32)



def norm_and_turn(c, src, norm=None, gains=None, shift=False):
    with c.stage("ln_loaded", "ln_stats_done", "ln_aggr_done", "ln_root", "ln_rstd_done",
                 "ln_done", "turned_tiles", "turned_out") as \
            (block, loaded, stats_done, aggr_done, root, rstd_done, normed, turned, out_done):
        src_t = norm if norm is not None else src
        tiles = c.tiles(0)

        if gains is not None:
            @block.sync
            def _(sp):
                sp.dma_start(c.gcols[:, 0:2], gains).then_inc(loaded, 16)

        if norm is not None:
            @block.vector
            def _(dve):
                for t in range(NT):
                    dve.bn_stats(c.stats[:, t, :], src[:, t, :]).then_inc(stats_done, 1)
                for t in range(NT):
                    dve.wait_ge(stats_done, t + 1)
                    dve.bn_aggr(c.mv[:, t, :], c.stats[:, t, :]).then_inc(aggr_done, 1)
                dve.wait_ge(aggr_done, NT)
                dve.tensor_scalar(c.rstd[:, :, 0], c.mv[:, :, 1], 1e-5, None, ALU.add).then_inc(root, 1)
                dve.wait_ge(root, 2)
                dve.reciprocal(c.rstd[:, :, 1], c.rstd[:, :, 0]).then_inc(rstd_done, 1)
                dve.wait_ge(rstd_done, 1)
                for t in range(NT):
                    dve.tensor_scalar(norm[:, t, :], src[:, t, :], c.mv[:, t, 0:1], c.rstd[:, t, 1:2],
                                      ALU.subtract, ALU.mult).then_inc(normed, 1)

        @block.tensor
        def _(pe):
            for t in range(NT):
                if norm is not None:
                    pe.wait_ge(normed, t + 1)
                pe.transpose(tiles[:, t, :], src_t[:, t, :], c.ident[:, :]).then_inc(turned, 1)

        @block.scalar
        def _(act):
            if norm is not None:
                act.wait_ge(root, 1)
                act.activation(c.rstd[:, :, 0], c.rstd[:, :, 0], ACT.Sqrt).then_inc(root, 1)
            if gains is not None:
                act.wait_ge(loaded, 16)
            if shift:
                act.wait_ge(turned, NT)
                act.activation(c.XT[0:64, :], c.banks(0)[0:64, :], ACT.Copy).then_inc(out_done, 1)
                act.activation(c.XT[64:P, 1:S], c.banks(0)[64:P, 0:S - 1], ACT.Copy).then_inc(out_done, 1)
                act.activation(c.XT[64:P, 0:1], c.ones[64:P, 0:1], ACT.Copy, scale=0.0).then_inc(out_done, 1)
                return
            for h in range(NH):
                act.wait_ge(turned, (h + 1) * (NT // NH))
                part = c.XT[:, h * HALF:(h + 1) * HALF]
                if gains is None:
                    act.activation(part, c.banks(0)[:, h * HALF:(h + 1) * HALF], ACT.Copy).then_inc(out_done, 1)
                else:
                    act.activation(part, c.banks(0)[:, h * HALF:(h + 1) * HALF], ACT.Identity,
                                   bias=c.gcols[:, 1:2], scale=c.gcols[:, 0:1]).then_inc(out_done, 1)



class Heads:

    def __init__(self, dim, n, rows, scale, mode, keys=S):
        self.dim, self.n, self.rows, self.scale, self.mode = dim, n, rows, scale, mode
        self.key_tiles = keys // P

    def v(self, c, tile, h):
        w = self.dim + 1
        return c.VA[:, tile, h * w:(h + 1) * w]

    def sees(self, q):
        return {"full": (0, self.key_tiles), "causal": (0, q + 1), "window": (max(q - 1, 0), q + 1)}[self.mode]

    def mask(self, q, k, turned):
        if self.mode == "causal" and q == k:
            return int(turned)
        if self.mode == "window":
            return (2 if q == k else 4) + int(turned)
        return None


def clear_v(c, dim=64):
    with c.stage("ones_set") as (block, ones_set):
        @block.vector
        def _(dve):
            dve.memset(c.VA[:, :, :], 0.0 if dim == 8 else 1.0).then_inc(ones_set, 1)
            if dim == 8:
                dve.wait_ge(ones_set, 1)
                dve.memset(c.VA[:, :, 8:P:32], 1.0).then_inc(ones_set, 1)
                dve.tensor_copy(c.KS[96:100, :, :], c.onehot[96:100, :, None].to_broadcast([4, 4, S])
                                ).then_inc(ones_set, 1)


def project(c, w, heads, bias=None, rope=None, xpos=None):
    turned = rope is not None or xpos is not None
    slots = 5 if turned else 3
    with c.stage("w_loaded", "projected", "rope_one", "rope_two", "rope_sum", "squared", "norm_summed",
                 "norm_root", "norm_clip", "norm_inv", "evacuated", "v_out", "b_loaded") as \
            (block, loaded, projected, one_done, two_done, summed, squared, norm_summed, norm_root,
             norm_clip, norm_inv, evacuated, v_out, b_loaded):
        outs = [(c.QT, c.QB), (c.KT, c.KB)]
        step = 2 if turned else 1
        w_v = slots - 1
        pitch = P // heads.n

        def v_to(h):
            at = h * (32 if heads.dim == 8 else heads.dim + 1)
            return c.VA[:, :, at:at + heads.dim]

        def v_from(h):
            return c.tiles(0)[:, :, h * pitch:h * pitch + heads.dim]


        @block.sync
        def _(sp):
            sp.dma_start(c.W[:, 0:slots, :], w).then_inc(loaded, 16)
            if bias is not None:
                cols, row = bias
                sp.dma_start(c.bcols[:, 0:slots - 1], cols).then_inc(b_loaded, 16)
                sp.dma_start(c.vbias[:, :], row.partition_broadcast(P)).then_inc(b_loaded, 16)

        @block.tensor
        def _(pe):
            pe.wait_ge(loaded, 16)
            for s in range(slots - 1):
                for h in range(NH):
                    out = c.PS[:, 2 * s + h, :]
                    mm = pe.matmul(out, c.W[:, s, :], c.XT[:, h * HALF:(h + 1) * HALF], start=True, stop=True)
                mm.then_inc(projected, 1)
            if xpos is not None:
                for n in range(2):
                    pe.wait_ge(squared, n + 1)
                    pe.wait_ge(summed, n + 1)
                    for h in range(NH):
                        mm = pe.matmul(c.PS[:, 4 * n + h, :], c.block1[:, :], c.T2[:, h * HALF:(h + 1) * HALF],
                                       start=True, stop=True)
                    mm.then_inc(norm_summed, 1)
                pe.wait_ge(norm_root, 1)
            else:
                pe.wait_ge(summed, 1)
            tiles = c.tiles(0)
            for t in range(NT):
                mm = pe.matmul(tiles[:, t, :], c.XT[:, t * P:(t + 1) * P], c.W[:, w_v, :], start=True, stop=True)
            mm.then_inc(projected, 1)

        @block.vector
        def _(dve):
            for n, (out, _) in enumerate(outs):
                dve.wait_ge(projected, step * (n + 1))
                straight = c.banks(2 * step * n)
                if n == 0 and bias is not None:
                    dve.wait_ge(b_loaded, 32)
                if not turned:
                    if bias is None:
                        dve.tensor_copy(out[:, :], straight).then_inc(summed, 1)
                    else:
                        dve.tensor_scalar(out[:, :], straight, c.bcols[:, n:n + 1], None, ALU.add).then_inc(summed, 1)
                    continue
                across = c.banks(2 * step * n + 2)
                if n:
                    dve.wait_ge(summed, n)
                if bias is not None:
                    dve.scalar_tensor_tensor(out[:, :], straight, c.bcols[:, 2 * n:2 * n + 1], rope[:, 0, :],
                                             ALU.add, ALU.mult).then_inc(one_done, 1)
                    dve.scalar_tensor_tensor(c.T1[:, :], across, c.bcols[:, 2 * n + 1:2 * n + 2], rope[:, 1, :],
                                             ALU.add, ALU.mult).then_inc(two_done, 1)
                elif xpos is None:
                    dve.tensor_tensor(out[:, :], straight, rope[:, 0, :], ALU.mult).then_inc(one_done, 1)
                    dve.tensor_tensor(c.T1[:, :], across, rope[:, 1, :], ALU.mult).then_inc(two_done, 1)
                else:
                    dve.scalar_tensor_tensor(out[:, :], straight, c.gcols[:, 2 * n:2 * n + 1], xpos[:, 2 * n, :],
                                             ALU.mult, ALU.mult).then_inc(one_done, 1)
                    dve.scalar_tensor_tensor(c.T1[:, :], across, c.gcols[:, 2 * n + 1:2 * n + 2],
                                             xpos[:, 2 * n + 1, :], ALU.mult, ALU.mult).then_inc(two_done, 1)
                dve.wait_ge(one_done, n + 1)
                dve.wait_ge(two_done, n + 1)
                dve.tensor_tensor(out[:, :], out[:, :], c.T1[:, :], ALU.add).then_inc(summed, 1)
                if xpos is not None:
                    dve.wait_ge(norm_root, n + 1)
                    dve.tensor_scalar(c.CT[:, :], c.CT[:, :], 1e-12, None, ALU.max).then_inc(norm_clip, 1)
                    dve.wait_ge(norm_clip, n + 1)
                    dve.reciprocal(c.CT[:, :], c.CT[:, :]).then_inc(norm_inv, 1)
                    dve.wait_ge(norm_inv, n + 1)
                    dve.wait_ge(summed, n + 1)
                    dve.tensor_tensor(out[:, :], out[:, :], c.CT[:, :], ALU.mult).then_inc(v_out, 1)

            if bias is not None:
                dve.wait_ge(projected, slots)
                for h in range(heads.n):
                    dve.tensor_tensor(v_to(h), v_from(h), c.vbias[:, None, pitch * h:pitch * h + heads.dim]
                                      .to_broadcast([P, NT, heads.dim]), ALU.add).then_inc(v_out, 1)

        @block.scalar
        def _(act):
            for n, (out, short) in enumerate(outs):
                act.wait_ge(projected, step * (n + 1))
                if xpos is not None:
                    act.wait_ge(one_done, n + 1)
                    if n:
                        act.wait_ge(norm_summed, n)
                        act.wait_ge(v_out, n)
                    act.activation(c.T2[:, :], c.banks(4 * n), ACT.Square).then_inc(squared, 1)
                    act.wait_ge(norm_summed, n + 1)
                    act.activation(c.CT[:, :], c.banks(4 * n), ACT.Sqrt).then_inc(norm_root, 1)
                    act.wait_ge(v_out, n + 1)
                    act.activation(short[:, :], out[:, :], ACT.Copy).then_inc(evacuated, 1)
                elif turned:
                    act.wait_ge(summed, n + 1)
                    if heads.dim > 8:
                        act.activation(short[:, :], out[:, :], ACT.Copy).then_inc(evacuated, 1)
                elif heads.dim > 8:
                    act.wait_ge(summed, n + 1)
                    act.activation(short[:, :], out[:, :], ACT.Copy).then_inc(evacuated, 1)
            act.wait_ge(projected, slots)
            for h in range(heads.n):
                if bias is None:
                    act.activation(v_to(h), v_from(h), ACT.Copy).then_inc(v_out, 1)


def attend(c, heads, out_at):
    units = [(h, half) for h in range(heads.n) for half in range(NH)]
    QPH = HALF // P
    pitch = P // heads.n
    work = []
    for u, (h, half) in enumerate(units):
        for k in range(heads.key_tiles):
            cols = [q - half * QPH for q in range(half * QPH, (half + 1) * QPH)
                    if heads.sees(q)[0] <= k < heads.sees(q)[1]]
            if cols:
                work.append((u, k, cols[0], cols[-1] + 1))
    first = [min(i for i, x in enumerate(work) if x[0] == u) for u in range(len(units))] + [len(work)]
    RING = QPH + 1
    first_index = {32: 0, 64: 1, 128: 2}[pitch]

    with c.stage("rows_ready", "rows_read", "scores_ready", "probs_ready", "pv_done",
                 "rden_done", "out_done") as \
            (block, rows_ready, rows_read, scores_ready, probs_ready, pv_done, rden_done, out_done):

        def rows(h):
            return slice(h * pitch, h * pitch + heads.rows)

        def o_at(q):
            w = heads.dim + 1
            return (6 + q // 2, (q % 2) * w) if heads.dim == P else (6, q * w)

        @block.tensor
        def _(pe):
            def row_scores(u, j):
                h, half = units[u]
                q = half * QPH + j
                use = u * RING + j
                lo, hi = heads.sees(q)
                if use >= 2:
                    pe.wait_ge(rows_read, use - 1)
                k = lo
                while k < hi:
                    n = 1
                    masked = heads.mask(q, k, False)
                    while (masked is None and k + n < hi and (k + n - lo) % QPH and
                           heads.mask(q, k + n, False) is None):
                        n += 1
                    col = (k - lo) % QPH * P
                    out = c.PS[:, 2 * (use % 2) + (k - lo) // QPH, col:col + n * P]
                    mm = pe.matmul(out, c.QB[rows(h), q * P:(q + 1) * P], c.KB[rows(h), k * P:(k + n) * P],
                                   start=True, stop=masked is None)
                    if masked is not None:
                        mm = pe.matmul(out, c.identb[:, :], c.masks[:, masked, :], start=False, stop=True)
                    k += n
                mm.then_inc(rows_ready, 1)

            def max_row(u):
                use = u * RING + QPH
                pe.wait_ge(rows_read, use)
                for j in range(QPH):
                    mm = pe.matmul(c.PS[0:1, 2 * (use % 2), j * P:(j + 1) * P], c.negmax[:, u % 2, j:j + 1],
                                   c.identb[:, :], start=True, stop=True)
                mm.then_inc(rows_ready, 1)

            def scores(n):
                u, k, lo, hi = work[n]
                h, half = units[u]
                if n >= 2:
                    pe.wait_ge(probs_ready, n - 1)
                if n == first[u]:
                    pe.wait_ge(rows_read, (u + 1) * RING)
                out = c.PS[:, 4 + n % 2, lo * P:hi * P]
                q0 = half * HALF
                pe.matmul(out, c.KT[rows(h), k * P:(k + 1) * P], c.QT[rows(h), q0 + lo * P:q0 + hi * P],
                          start=True, stop=False)
                for j in range(lo, hi):
                    masked = heads.mask(half * QPH + j, k, True)
                    if masked is not None:
                        pe.matmul(c.PS[:, 4 + n % 2, j * P:(j + 1) * P], c.identb[:, :], c.masks[:, masked, :],
                                  start=False, stop=False)
                mm = pe.matmul(out, c.first[rows(h), first_index, :], c.negmax_row[rows(h), u % 2, lo * P:hi * P], start=False, stop=True)
                mm.then_inc(scores_ready, 1)

            def weighted(n):
                u, k, lo, hi = work[n]
                h, half = units[u]
                pe.wait_ge(probs_ready, n + 1)
                if n == first[u] and u >= 1:
                    pe.wait_ge(out_done, u)
                for j in range(lo, hi):
                    bank, col = o_at(j)
                    opens = n == first[u] and (j == lo or (heads.dim == P and j % 2 == 0))
                    mm = pe.matmul(c.PS[:, bank, col:col + heads.dim + 1],
                                   c.probs[:, n % 3, j * P:(j + 1) * P], heads.v(c, k, h),
                                   start=opens, stop=k + 1 == heads.sees(half * QPH + j)[1], skip_group_check=True)
                mm.then_inc(pv_done, 1)

            for j in range(QPH):
                row_scores(0, j)
            max_row(0)
            for u in range(len(units)):
                ahead = list(range(QPH)) if u + 1 < len(units) else []
                for n in range(first[u], first[u + 1]):
                    scores(n)
                    if ahead and (n - first[u]) % 2 == 1:
                        row_scores(u + 1, ahead.pop(0))
                    if n > first[u]:
                        weighted(n - 1)
                while ahead:
                    row_scores(u + 1, ahead.pop(0))
                if u + 1 < len(units):
                    max_row(u + 1)
                weighted(first[u + 1] - 1)

        @block.scalar
        def _(act):
            for n, (u, k, lo, hi) in enumerate(work):
                act.wait_ge(scores_ready, n + 1)
                if n >= 3:
                    act.wait_ge(pv_done, n - 2)
                act.activation(c.probs[:, n % 3, lo * P:hi * P], c.PS[:, 4 + n % 2, lo * P:hi * P], ACT.Exp,
                               scale=heads.scale).then_inc(probs_ready, 1)

        @block.vector
        def _(dve):
            def maxima(u):
                h, half = units[u]
                for j in range(QPH):
                    use = u * RING + j
                    lo, hi = heads.sees(half * QPH + j)
                    dve.wait_ge(rows_ready, use + 1)
                    dve.tensor_reduce(c.negmax[:, u % 2, j:j + 1], c.banks(2 * (use % 2))[:, 0:(hi - lo) * P],
                                      AX_X, ALU.max, negate=True).then_inc(rows_read, 1)
                use = u * RING + QPH
                dve.wait_ge(rows_ready, use + 1)
                if u >= 2:
                    dve.wait_ge(scores_ready, first[u - 1])
                dve.wait_ge(rows_read, use)
                dve.tensor_copy(c.negmax_row[h * pitch:h * pitch + 1, u % 2, :], c.PS[0:1, 2 * (use % 2), :]).then_inc(rows_read, 1)

            def divide(u):
                h, half = units[u]
                d = heads.dim
                dve.wait_ge(pv_done, first[u + 1])
                if u:
                    dve.wait_ge(out_done, u)
                if d < P:
                    o = c.PS[:, 6, 0:QPH * (d + 1)].rearrange("p (q w) -> p q w", w=d + 1)
                else:
                    o = c.PS[:, 6:8, 0:2 * (d + 1)].rearrange("p b (q w) -> p b q w", w=d + 1)
                if d < P:
                    dve.reciprocal(c.rden[:, :, :], o[:, :, d:d + 1]).then_inc(rden_done, 1)
                    dve.wait_ge(rden_done, u + 1)
                    dve.tensor_tensor(out_at(h, half), o[:, :, 0:d], c.rden[:, :, :].to_broadcast([P, QPH, d]),
                                      ALU.mult).then_inc(out_done, 1)
                else:
                    for b in range(2):
                        dve.reciprocal(c.rden[:, 2 * b:2 * b + 2, :], o[:, b, :, d:d + 1]).then_inc(rden_done, 1)
                    dve.wait_ge(rden_done, 2 * (u + 1))
                    for b in range(2):
                        mm = dve.tensor_tensor(out_at(h, half)[:, 2 * b:2 * b + 2, :], o[:, b, :, 0:d],
                                               c.rden[:, 2 * b:2 * b + 2, :].to_broadcast([P, 2, d]), ALU.mult)
                    mm.then_inc(out_done, 1)

            maxima(0)
            for u in range(len(units)):
                if u + 1 < len(units):
                    maxima(u + 1)
                divide(u)


def project_out(c, target, w, bias=None):
    with c.stage("wo_loaded", "ctx_turned", "ctx_out", "y_ready", "y_added") as \
            (block, loaded, turned, ctx_out, y_ready, y_added):
        @block.sync
        def _(sp):
            sp.dma_start(c.WO[:, :], w).then_inc(loaded, 16)
            if bias is not None:
                sp.dma_start(c.vbias[:, :], bias.partition_broadcast(P)).then_inc(loaded, 16)

        @block.tensor
        def _(pe):
            for t in range(NT):
                pe.transpose(c.tiles(0)[:, t, :], c.CTX[:, t, :], c.ident[:, :]).then_inc(turned, 1)
            pe.wait_ge(loaded, 32 if bias is not None else 16)
            for t in range(NT):
                if t % (NT // NH) == 0:
                    pe.wait_ge(ctx_out, t // (NT // NH) + 1)
                pe.matmul(c.tiles(2)[:, t, :], c.CT[:, t * P:(t + 1) * P], c.WO[:, :],
                          start=True, stop=True).then_inc(y_ready, 1)

        @block.scalar
        def _(act):
            for h in range(NH):
                act.wait_ge(turned, (h + 1) * (NT // NH))
                act.activation(c.CT[:, h * HALF:(h + 1) * HALF], c.PS[:, h, :], ACT.Copy).then_inc(ctx_out, 1)

        @block.vector
        def _(dve):
            if bias is not None:
                dve.wait_ge(loaded, 32)
                dve.tensor_tensor(target[:, :, :], target[:, :, :], c.vbias[:, None, :].to_broadcast([P, NT, P]),
                                  ALU.add).then_inc(y_added, 1)
                dve.wait_ge(y_added, 1)
            for h in range(NH):
                dve.wait_ge(y_ready, (h + 1) * (NT // NH))
                t = slice(h * (NT // NH), (h + 1) * (NT // NH))
                dve.tensor_tensor(target[:, t, :], target[:, t, :], c.tiles(2)[:, t, :], ALU.add).then_inc(y_added, 1)


def attend_pair(c, pair, w, mode, scale, rope=None, xpos=None, target=None, wo=None):
    heads = Heads(64, 2, 64, scale, mode)
    turned = rope is not None or xpos is not None
    per_item = 2 if turned else 1
    items = [(h, side) for h in range(2) for side in range(2)]
    ring = 2 if turned else 4
    slots = 4 * per_item + 1
    QPH = HALF // P
    units = [(half, h) for half in range(NH) for h in range(2)]
    USES = QPH + 1
    work = []
    for u, (half, h) in enumerate(units):
        for k in range(heads.key_tiles):
            cols = [j for j in range(QPH) if heads.sees(half * QPH + j)[0] <= k < heads.sees(half * QPH + j)[1]]
            if cols:
                work.append((u, k, cols[0], cols[-1] + 1))
    first = [min(i for i, x in enumerate(work) if x[0] == u) for u in range(len(units))] + [len(work)]
    rows_mode = target is None
    pieces = ((c.QS[:, 0:2, :], c.QS[:, 2:4, :]), (c.KS[:, 0:2, :], c.KS[:, 2:4, :], c.K3))
    PER_ROW = 1024 // 64
    row_w = c.wrows
    by_place = c.CT[:, :].rearrange("p (m r) -> p r m", m=PER_ROW)

    def item_banks(n):
        return 2 * per_item * (n % ring)

    v_banks = item_banks(4)

    with c.stage("w_loaded", "projected", "turn_one", "turn_two", "turn_sum", "top_done", "rest_done", "piece2_done",
                 "pieces_done", "v_out", "rows_ready", "rows_read", "scores_ready", "probs_ready", "pv_done",
                 "rden_done", "out_done", "ctx_turned", "ctx_out", "y_ready", "y_added", "wo_loaded",
                 "nat_ready", "nat_square", "nat_sum", "norm_step", "norm_root", "norm_turned", "norm_rows",
                 "norm_wide") as \
            (block, w_loaded, projected, turn_one, turn_two, turn_sum, top_done, rest_done, piece2_done,
             pieces_done, v_out, rows_ready, rows_read, scores_ready, probs_ready, pv_done,
             rden_done, out_done, ctx_turned, ctx_out, y_ready, y_added, wo_loaded,
             nat_ready, nat_square, nat_sum, norm_step, norm_root, norm_turned, norm_rows, norm_wide):

        @block.sync
        def _(sp):
            sp.dma_start(c.W[:, 0:slots, :], one(w, pair)).then_inc(w_loaded, 16)
            if not rows_mode:
                sp.dma_start(c.WO[:, :], one(wo, pair)).then_inc(wo_loaded, 16)

        @block.tensor
        def _(pe):
            def item(n):
                if n >= ring:
                    pe.wait_ge(rest_done, n - ring + 1)
                for s in range(per_item):
                    for h in range(NH):
                        mm = pe.matmul(c.PS[:, item_banks(n) + 2 * s + h, :], c.W[:, per_item * n + s, :],
                                       c.XT[:, h * HALF:(h + 1) * HALF], start=True, stop=True)
                mm.then_inc(projected, 1)

            def values():
                pe.wait_ge(rest_done, 5 - ring)
                for t in range(NT):
                    mm = pe.matmul(c.tiles(v_banks)[:, t, :], c.XT[:, t * P:(t + 1) * P], c.W[:, slots - 1, :],
                                   start=True, stop=True)
                mm.then_inc(projected, 1)

            def row_scores(u, j):
                half, h = units[u]
                q = half * QPH + j
                use = u * USES + j
                lo, hi = heads.sees(q)
                if use >= 2:
                    pe.wait_ge(rows_read, use - 1)
                k = lo
                while k < hi:
                    n = 1
                    masked = heads.mask(q, k, False)
                    while (masked is None and k + n < hi and (k + n - lo) % QPH and
                           heads.mask(q, k + n, False) is None):
                        n += 1
                    col = (k - lo) % QPH * P
                    out = c.PS[:, 2 * (use % 2) + (k - lo) // QPH, col:col + n * P]
                    mm = pe.matmul(out, pieces[0][0][:, h, q * P:(q + 1) * P], pieces[1][0][:, h, k * P:(k + n) * P],
                                   start=True, stop=masked is None)
                    if masked is not None:
                        mm = pe.matmul(out, c.identb[:, :], c.masks[:, masked, :], start=False, stop=True)
                    k += n
                mm.then_inc(rows_ready, 1)

            def max_row(u):
                use = u * USES + QPH
                pe.wait_ge(rows_read, use)
                for j in range(QPH):
                    mm = pe.matmul(c.PS[0:1, 2 * (use % 2), j * P:(j + 1) * P], c.negmax[:, u % 2, j:j + 1],
                                   c.identb[:, :], start=True, stop=True)
                mm.then_inc(rows_ready, 1)

            def scores(n):
                u, k, lo, hi = work[n]
                half, h = units[u]
                if n >= 2:
                    pe.wait_ge(probs_ready, n - 1)
                if n == first[u]:
                    pe.wait_ge(rows_read, (u + 1) * USES)
                out = c.PS[:, 4 + n % 2, lo * P:hi * P]
                q0 = half * HALF
                for i, (qp, kp) in enumerate(((0, 0), (1, 1), (0, 2))):
                    pe.matmul(out, pieces[1][kp][:, h, k * P:(k + 1) * P],
                              pieces[0][qp][:, h, q0 + lo * P:q0 + hi * P], start=i == 0, stop=False)
                for j in range(lo, hi):
                    masked = heads.mask(half * QPH + j, k, True)
                    if masked is not None:
                        pe.matmul(c.PS[:, 4 + n % 2, j * P:(j + 1) * P], c.identb[:, :], c.masks[:, masked, :],
                                  start=False, stop=False)
                mm = pe.matmul(out, c.first[:, 2, :], c.negmax_row[:, u % 2, lo * P:hi * P], start=False, stop=True)
                mm.then_inc(scores_ready, 1)

            def weighted(n):
                u, k, lo, hi = work[n]
                half, h = units[u]
                pe.wait_ge(probs_ready, n + 1)
                if n == first[u] and u >= 1:
                    pe.wait_ge(out_done, u)
                for j in range(lo, hi):
                    mm = pe.matmul(c.PS[:, 6, j * 65:(j + 1) * 65], c.probs[:, n % 3, j * P:(j + 1) * P],
                                   heads.v(c, k, h), start=n == first[u] and j == lo,
                                   stop=k + 1 == heads.sees(half * QPH + j)[1], skip_group_check=True)
                mm.then_inc(pv_done, 1)

            def turn_context(half):
                pe.wait_ge(out_done, 2 * (half + 1))
                if half:
                    pe.wait_ge(y_added, half)
                for j in range(QPH):
                    mm = pe.transpose(c.PS[:, 7, j * P:(j + 1) * P], c.CTX[:, half * QPH + j, :], c.ident[:, :])
                mm.then_inc(ctx_turned, 1)

            def project_context(half):
                pe.wait_ge(ctx_out, half + 1)
                if rows_mode:
                    n = 32
                    for h in range(2):
                        on = slice(64 * h, 64 * h + 64)
                        at = 64 * h + n * half
                        for m in range(PER_ROW):
                            mm = pe.matmul(c.PS[at:at + n, 7, 0:P], c.CT[on, 64 * m + n * half:64 * m + n * half + n],
                                           row_w[on, m, :], start=m == 0, stop=m == PER_ROW - 1)
                        mm.then_inc(y_ready, 1)
                    return
                pe.wait_ge(wo_loaded, 16)
                for j in range(QPH):
                    t = half * QPH + j
                    mm = pe.matmul(c.PS[:, 7, j * P:(j + 1) * P], c.CT[:, t * P:(t + 1) * P], c.WO[:, :],
                                   start=True, stop=True)
                mm.then_inc(y_ready, 1)

            pe.wait_ge(w_loaded, 16)
            for n in range(len(items)):
                item(n)
            values()
            pe.wait_ge(v_out, 1)
            pe.wait_ge(rest_done, 4)
            pe.wait_ge(pieces_done, 4)
            for j in range(QPH):
                row_scores(0, j)
            max_row(0)
            for u in range(len(units)):
                ahead = list(range(QPH)) if u + 1 < len(units) else []
                for n in range(first[u], first[u + 1]):
                    scores(n)
                    if ahead and ((n - first[u]) % 2 == 1 or first[u + 1] - first[u] < 8):
                        row_scores(u + 1, ahead.pop(0))
                    if n > first[u]:
                        weighted(n - 1)
                    if u == 2 and n == first[u] + 1:
                        turn_context(0)
                    if u == 2 and n == first[u] + 3:
                        project_context(0)
                while ahead:
                    row_scores(u + 1, ahead.pop(0))
                if u + 1 < len(units):
                    max_row(u + 1)
                weighted(first[u + 1] - 1)
            turn_context(1)
            project_context(1)

        @block.scalar
        def _(act):
            def source(n):
                return c.rest[:, n % 2, :] if turned else c.banks(item_banks(n))

            def top(n):
                h, side = items[n]
                act.wait_ge(turn_sum if turned else projected, n + 1)
                if side == 0:
                    if n >= 2:
                        act.wait_ge(rest_done, n - 1)
                    act.activation(c.top[:, 0, :], source(n), ACT.Copy, scale=c.coef64[:, 0:1]).then_inc(top_done, 1)
                else:
                    act.activation(pieces[1][0][:, h, :], source(n), ACT.Copy).then_inc(top_done, 1)

            def second(n):
                h, side = items[n]
                act.wait_ge(rest_done, n + 1)
                dst = pieces[0][0] if side == 0 else pieces[1][1]
                act.activation(dst[:, h, :], c.rest[:, n % 2, :], ACT.Copy).then_inc(piece2_done, 1)

            for n in range(len(items) + 1):
                if n < len(items):
                    top(n)
                if n:
                    second(n - 1)
            act.wait_ge(projected, 5)
            act.activation(c.VA[:, :, 0:130].rearrange("p t (h w) -> p t h w", h=2)[:, :, :, 0:64],
                           c.tiles(v_banks).rearrange("p t (h w) -> p t h w", h=2), ACT.Copy).then_inc(v_out, 1)

            def context_out(half):
                act.wait_ge(ctx_turned, half + 1)
                if rows_mode:
                    act.activation(by_place[:, 32 * half:32 * half + 32, :],
                                   c.PS[:, 7, :].rearrange("p (r m) -> p r m", m=PER_ROW), ACT.Copy).then_inc(ctx_out, 1)
                else:
                    act.activation(c.CT[:, half * HALF:(half + 1) * HALF], c.PS[:, 7, :], ACT.Copy).then_inc(ctx_out, 1)

            for n, (u, k, lo, hi) in enumerate(work):
                act.wait_ge(scores_ready, n + 1)
                if n >= 3:
                    act.wait_ge(pv_done, n - 2)
                act.activation(c.probs[:, n % 3, lo * P:hi * P], c.PS[:, 4 + n % 2, lo * P:hi * P], ACT.Exp,
                               scale=scale).then_inc(probs_ready, 1)
                if u == 2 and n == first[u] + 2:
                    context_out(0)
            context_out(1)

        @block.vector
        def _(dve):
            def turn(n):
                x = c.rest[:, n % 2, :]
                side = items[n][1]
                straight, across = c.banks(item_banks(n)), c.banks(item_banks(n) + 2)
                dve.wait_ge(projected, n + 1)
                if n >= 2:
                    dve.wait_ge(pieces_done, n - 1)
                if xpos is None:
                    dve.tensor_tensor(x, straight, rope[:, 0, :], ALU.mult).then_inc(turn_one, 1)
                    dve.tensor_tensor(c.T1[:, :], across, rope[:, 1, :], ALU.mult).then_inc(turn_two, 1)
                dve.wait_ge(turn_one, n + 1)
                dve.wait_ge(turn_two, n + 1)
                dve.tensor_tensor(x, x, c.T1[:, :], ALU.add).then_inc(turn_sum, 1)

            def rest(n):
                h, side = items[n]
                x = c.rest[:, n % 2, :]
                source = x if turned else c.banks(item_banks(n))
                dve.wait_ge(top_done, n + 1)
                if n >= 2:
                    dve.wait_ge(pieces_done, n - 1)
                if side == 0:
                    dve.tensor_tensor(x, source, c.top[:, 0, :], ALU.subtract).then_inc(rest_done, 1)
                else:
                    dve.scalar_tensor_tensor(x, pieces[1][0][:, h, :], c.coef64[:, 2:3], source,
                                             ALU.mult, ALU.add).then_inc(rest_done, 1)

            def third(n):
                h, side = items[n]
                x = c.rest[:, n % 2, :]
                dve.wait_ge(piece2_done, n + 1)
                if side == 0:
                    dve.scalar_tensor_tensor(pieces[0][1][:, h, :], pieces[0][0][:, h, :], c.coef64[:, 1:2], x,
                                             ALU.mult, ALU.add).then_inc(pieces_done, 1)
                else:
                    dve.tensor_tensor(pieces[1][2][:, h, :], x, pieces[1][1][:, h, :],
                                      ALU.subtract).then_inc(pieces_done, 1)

            for n in range(len(items) + 1):
                if turned and n < len(items):
                    turn(n)
                if n and turned:
                    third(n - 1)
                if n < len(items):
                    rest(n)
                if n and not turned:
                    third(n - 1)

            def maxima(u):
                half, h = units[u]
                for j in range(QPH):
                    use = u * USES + j
                    lo, hi = heads.sees(half * QPH + j)
                    dve.wait_ge(rows_ready, use + 1)
                    dve.tensor_reduce(c.negmax[:, u % 2, j:j + 1], c.banks(2 * (use % 2))[:, 0:(hi - lo) * P],
                                      AX_X, ALU.max, negate=True).then_inc(rows_read, 1)
                use = u * USES + QPH
                dve.wait_ge(rows_ready, use + 1)
                if u >= 2:
                    dve.wait_ge(scores_ready, first[u - 1])
                dve.tensor_copy(c.negmax_row[0:1, u % 2, :], c.PS[0:1, 2 * (use % 2), :]).then_inc(rows_read, 1)

            def divide(u):
                half, h = units[u]
                dve.wait_ge(pv_done, first[u + 1])
                if u:
                    dve.wait_ge(out_done, u)
                o = c.PS[:, 6, 0:QPH * 65].rearrange("p (q w) -> p q w", w=65)
                dve.reciprocal(c.rden[:, :, :], o[:, :, 64:65]).then_inc(rden_done, 1)
                dve.wait_ge(rden_done, u + 1)
                dve.tensor_tensor(c.CTX[:, half * QPH:(half + 1) * QPH, 64 * h:64 * h + 64], o[:, :, 0:64],
                                  c.rden[:, :, :].to_broadcast([P, QPH, 64]), ALU.mult).then_inc(out_done, 1)

            def add_out(half):
                if rows_mode:
                    dve.wait_ge(y_ready, 2 * (half + 1))
                    for h in range(2):
                        at = 64 * h + 32 * half
                        tile = c.X[at:at + 32, bass.ds(pair, 1), :].rearrange("p z d -> p (z d)")
                        ins = dve.tensor_tensor(tile, tile, c.PS[at:at + 32, 7, 0:P], ALU.add)
                    ins.then_inc(y_added, 1)
                    return
                dve.wait_ge(y_ready, half + 1)
                part = target[:, half * QPH:(half + 1) * QPH, :]
                dve.tensor_tensor(part, part, c.PS[:, 7, :].rearrange("p (t d) -> p t d", d=P), ALU.add
                                  ).then_inc(y_added, 1)

            maxima(0)
            for u in range(len(units)):
                if u + 1 < len(units):
                    maxima(u + 1)
                if u == 2:
                    add_out(0)
                divide(u)
            add_out(1)


def attention64(c, target, w, wo, n_pairs, mode, scale, rope=None, xpos=None):
    clear_v(c)
    with c.nc.Fori(0, n_pairs) as pair:
        attend_pair(c, pair, w, mode, scale, rope=rope, xpos=xpos, target=target, wo=wo)


def pair_out(c):
    return lambda h, half: c.CTX[:, 4 * half:4 * half + 4, 64 * h:64 * h + 64]


def attention64_old(c, target, w, wo, n_pairs, mode, scale, rope=None, xpos=None):
    heads = Heads(64, 2, 64, scale, mode)
    clear_v(c)
    with c.nc.Fori(0, n_pairs) as pair:
        project(c, one(w, pair), heads, rope=rope, xpos=xpos)
        attend(c, heads, pair_out(c))
        project_out(c, target, one(wo, pair))


def attention8(c, w, bias, mode, rope=None):
    heads = Heads(8, 4, 32, 8.0 ** -0.5, mode)
    clear_v(c, 8)
    with c.nc.Fori(0, 4) as group:
        project(c, one(w, group), heads, bias=None if bias is None else (one(bias[0], group), bias[1][bass.ds(group, 1)].rearrange("z n -> (z n)")),
                rope=rope)
        attend_four(c, heads, group)


def attend_four(c, heads, group):
    QPH = HALF // P
    ROWS, TOP = 96, 100
    items = [(j, side) for j in range(4) for side in range(2)]
    sources = ((c.QT, c.QS), (c.KT, c.KS))
    uses = []
    for u in range(NH):
        for h in range(4):
            for j in range(QPH):
                lo, hi = heads.sees(u * QPH + j)
                uses += [(u, h, j, k, min(QPH, hi - k)) for k in range(lo, hi, QPH)]
        uses.append((u, None, None, None, None))
    last_use = [max(i for i, x in enumerate(uses) if x[0] == u) for u in range(NH)]
    chunks = [max(x[3] or 0 for x in uses if x[0] == u) // QPH + 1 for u in range(NH)]
    work = []
    for u in range(NH):
        for k in range(heads.key_tiles):
            cols = [j for j in range(QPH) if heads.sees(u * QPH + j)[0] <= k < heads.sees(u * QPH + j)[1]]
            if cols:
                work.append((u, k, cols[0], cols[-1] + 1))
    first = [min(i for i, x in enumerate(work) if x[0] == u) for u in range(NH)] + [len(work)]

    with c.stage("replicated", "top_done", "rest_done", "mid_done", "pieces_done", "rows_ready", "rows_read",
                 "maxima_done", "scores_ready", "probs_ready", "pv_done", "o_out", "o_turned", "rden_done",
                 "out_done") as \
            (block, replicated, top_done, rest_done, mid_done, pieces_done, rows_ready, rows_read, maxima_done,
             scores_ready, probs_ready, pv_done, o_out, o_turned, rden_done, out_done):

        def item_banks(n):
            return 2 * (n % 3)

        @block.tensor
        def _(pe):
            def replicate(n):
                j, side = items[n]
                if n >= 3:
                    pe.wait_ge(rest_done, n - 2)
                for h in range(NH):
                    mm = pe.matmul(c.PS[0:ROWS, item_banks(n) + h, :], c.rep[:, j, 0:ROWS],
                                   sources[side][0][:, h * HALF:(h + 1) * HALF], start=True, stop=True)
                mm.then_inc(replicated, 1)

            def row_scores(i):
                u, h, j, k, n = uses[i]
                q = u * QPH + j
                if i >= 2:
                    pe.wait_ge(rows_read, i - 1)
                if u == 0 and (i == 0 or uses[i - 1][1] != h):
                    pe.wait_ge(pieces_done, 2 * (h + 1))
                bank = 6 + i % 2
                plain = n - 1 if heads.mask(q, k + n - 1, False) is not None else n
                if plain:
                    mm = pe.matmul(c.PS[:, bank, 0:plain * P], c.QS[0:ROWS, h, q * P:(q + 1) * P],
                                   c.KS[0:ROWS, h, k * P:(k + plain) * P], start=True, stop=True)
                if plain < n:
                    out = c.PS[:, bank, plain * P:n * P]
                    pe.matmul(out, c.QS[0:ROWS, h, q * P:(q + 1) * P],
                              c.KS[0:ROWS, h, (k + plain) * P:(k + n) * P], start=True, stop=False)
                    mm = pe.matmul(out, c.identb[:, :], c.masks[:, heads.mask(q, k + n - 1, False), :],
                                   start=False, stop=True)
                mm.then_inc(rows_ready, 1)

            def max_rows(u):
                i = last_use[u]
                pe.wait_ge(maxima_done, u + 1)
                for j in range(QPH):
                    mm = pe.matmul(c.PS[ROWS:TOP, 6 + i % 2, j * P:(j + 1) * P], c.negmax8[:, u, :, j],
                                   c.identb[:, :], start=True, stop=True)
                mm.then_inc(rows_ready, 1)

            def scores(n, pair):
                u, k, lo, hi = work[n]
                m = 2 * n + pair
                if m >= 2:
                    pe.wait_ge(probs_ready, m - 1)
                if m == 0:
                    pe.wait_ge(rest_done, len(items))
                if n == first[u] and pair == 0:
                    pe.wait_ge(rows_read, last_use[u] + 1)
                for hh in range(2):
                    h = 2 * pair + hh
                    bank = 2 * (m % 2) + hh
                    mm = pe.matmul(c.PS[:, bank, lo * P:hi * P], c.KS[0:TOP, h, k * P:(k + 1) * P],
                                   c.QS[0:TOP, h, u * HALF + lo * P:u * HALF + hi * P], start=True, stop=True)
                    for j in range(lo, hi):
                        masked = heads.mask(u * QPH + j, k, True)
                        if masked is not None:
                            mm = pe.matmul(c.PS[:, bank, j * P:(j + 1) * P], c.identb[:, :], c.masks[:, masked, :],
                                           start=False, stop=True, skip_group_check=True)
                mm.then_inc(scores_ready, 1)

            def weighted(n):
                u, k, lo, hi = work[n]
                pe.wait_ge(probs_ready, 2 * (n + 1))
                for h in range(4):
                    mm = pe.matmul(c.PS[32 * h:32 * h + 32, 4 + u, lo * P:hi * P], c.VA[:, k, 32 * h:32 * h + 32],
                                   c.probs8[:, n % 3, h, lo * P:hi * P], start=n == first[u], stop=True,
                                   skip_group_check=True)
                mm.then_inc(pv_done, 1)

            def turn_out(u):
                pe.wait_ge(o_out, u + 1)
                for j in range(QPH):
                    mm = pe.transpose(c.PS[:, 4 + u, j * P:(j + 1) * P], c.out8[:, u, j * P:(j + 1) * P],
                                      c.ident[:, :])
                mm.then_inc(o_turned, 1)

            for n in range(len(items)):
                replicate(n)
                if n >= 3 and n % 2 == 1:
                    for i in range(last_use[0]):
                        if uses[i][1] == (n - 3) // 2:
                            row_scores(i)
            for i in range(last_use[0]):
                if uses[i][1] == 3:
                    row_scores(i)
            max_rows(0)
            ahead = list(range(last_use[0] + 1, last_use[1]))
            for u in range(NH):
                count = first[u + 1] - first[u]
                for n in range(first[u], first[u + 1]):
                    for pair in range(2):
                        scores(n, pair)
                        if u == 0:
                            steps_left = 2 * (first[1] - n) - pair
                            for _ in range(-(-len(ahead) // steps_left)):
                                row_scores(ahead.pop(0))
                    if n > first[u]:
                        weighted(n - 1)
                    if u and n == first[u] + min(1, count - 1):
                        turn_out(u - 1)
                if u + 1 < NH:
                    max_rows(u + 1)
                weighted(first[u + 1] - 1)
            turn_out(NH - 1)

        @block.scalar
        def _(act):
            def top(n):
                side = items[n][1]
                act.wait_ge(replicated, n + 1)
                if n >= 2:
                    act.wait_ge(rest_done, n - 1)
                act.activation(c.top[0:ROWS, n % 2, :], c.banks(item_banks(n))[0:ROWS, :], ACT.Copy,
                               scale=c.coef[0:ROWS, 2 * side:2 * side + 1]).then_inc(top_done, 1)

            def mid(n):
                side = items[n][1]
                act.wait_ge(rest_done, n + 1)
                if n >= 2:
                    act.wait_ge(pieces_done, n - 1)
                act.activation(c.mid[0:ROWS, n % 2, :], c.rest[0:ROWS, n % 2, :], ACT.Copy,
                               scale=c.coef[0:ROWS, 2 * side + 1:2 * side + 2]).then_inc(mid_done, 1)

            for n in range(len(items) + 1):
                if n < len(items):
                    top(n)
                if n:
                    mid(n - 1)
            for n, (u, k, lo, hi) in enumerate(work):
                for pair in range(2):
                    m = 2 * n + pair
                    act.wait_ge(scores_ready, m + 1)
                    if n >= 3:
                        act.wait_ge(pv_done, n - 2)
                    act.activation(c.probs8[:, n % 3, 2 * pair:2 * pair + 2, lo * P:hi * P],
                                   c.PS[:, 2 * (m % 2):2 * (m % 2) + 2, lo * P:hi * P], ACT.Exp,
                                   scale=heads.scale).then_inc(probs_ready, 1)
                if u and n == first[u]:
                    act.wait_ge(pv_done, first[u])
                    act.activation(c.out8[:, u - 1, :], c.PS[:, 4 + u - 1, :], ACT.Copy).then_inc(o_out, 1)
            act.wait_ge(pv_done, len(work))
            act.activation(c.out8[:, NH - 1, :], c.PS[:, 4 + NH - 1, :], ACT.Copy).then_inc(o_out, 1)

        @block.vector
        def _(dve):
            def rest(n):
                dve.wait_ge(top_done, n + 1)
                if n >= 2:
                    dve.wait_ge(pieces_done, n - 1)
                dve.tensor_tensor(c.rest[0:ROWS, n % 2, :], c.banks(item_banks(n))[0:ROWS, :],
                                  c.top[0:ROWS, n % 2, :], ALU.subtract).then_inc(rest_done, 1)

            def pieces(n):
                j, side = items[n]
                dve.wait_ge(mid_done, n + 1)
                dve.tensor_tensor(sources[side][1][0:ROWS, j, :], c.rest[0:ROWS, n % 2, :],
                                  c.mid[0:ROWS, n % 2, :], ALU.subtract).then_inc(pieces_done, 1)

            def maximum(i):
                u, h, j, k, n = uses[i]
                dve.wait_ge(rows_ready, i + 1)
                dve.tensor_reduce(c.rowmax[:, u, h, j, k // QPH:k // QPH + 1], c.PS[:, 6 + i % 2, 0:n * P],
                                  AX_X, ALU.max).then_inc(rows_read, 1)

            def combine(u):
                dve.wait_ge(rows_read, last_use[u])
                dve.tensor_reduce(c.negmax8[:, u, :, :], c.rowmax[:, u, :, :, 0:chunks[u]], AX_X, ALU.max,
                                  negate=True).then_inc(maxima_done, 1)
                i = last_use[u]
                dve.wait_ge(rows_ready, i + 1)
                dve.tensor_copy(c.QS[ROWS:TOP, :, u * HALF:(u + 1) * HALF],
                                c.PS[ROWS:TOP, 6 + i % 2, :][:, None, :].to_broadcast([TOP - ROWS, 4, HALF])
                                ).then_inc(rows_read, 1)

            def divide(u):
                dve.wait_ge(o_turned, u + 1)
                o = c.PS[:, 4 + u, :].rearrange("p (q h w) -> p q h w", q=QPH, h=4)
                dve.reciprocal(c.rden8[:, u, :, :], o[:, :, :, 8]).then_inc(rden_done, 1)
                dve.wait_ge(rden_done, u + 1)
                out = c.CTX[:, QPH * u:QPH * (u + 1), bass.ds(group * 32, 32)].rearrange("p q (h e) -> p q h e", h=4)
                dve.tensor_tensor(out, o[:, :, :, 0:8], c.rden8[:, u, :, :, None].to_broadcast([P, QPH, 4, 8]),
                                  ALU.mult).then_inc(out_done, 1)

            for n in range(len(items) + 1):
                if n < len(items):
                    rest(n)
                if n:
                    pieces(n - 1)
                if n >= 3 and n % 2 == 1:
                    for i in range(last_use[0]):
                        if uses[i][1] == (n - 3) // 2:
                            maximum(i)
            for i in range(last_use[0]):
                if uses[i][1] == 3:
                    maximum(i)
            combine(0)
            for i in range(last_use[0] + 1, last_use[1]):
                maximum(i)
            combine(1)
            divide(0)
            divide(1)



def mlp(c, target, w1, b1, w2, b2, chunks, gated, batch_weights=False):
    with c.stage("mlp_loaded", "mlp_b_loaded", "up_done", "gelu_done", "hidden_done", "down_done", "mlp_added") as \
            (block, loaded, b_loaded, up, gelu, hidden, down, added):
        n_up = chunks * (2 if gated else 1)
        steps = [(k, h) for k in range(chunks) for h in range(NH)]
        W1, W2 = (c.W1E, c.W2E) if batch_weights else (c.W1, c.W2)

        @block.sync
        def _(sp):
            if not batch_weights:
                sp.dma_start(W1[:, 0:n_up, :], w1).then_inc(loaded, 16)
                sp.dma_start(W2[:, 0:chunks, :], w2).then_inc(loaded, 16)
            sp.dma_start(c.bcols[:, 0:n_up], b1).then_inc(b_loaded, 16)
            sp.dma_start(c.vbias[:, :], b2.partition_broadcast(P)).then_inc(b_loaded, 16)

        @block.tensor
        def _(pe):
            if not batch_weights:
                pe.wait_ge(loaded, 32)
            for n, (k, h) in enumerate(steps):
                if n >= 3:
                    pe.wait_ge(hidden if gated else gelu, n - 2)
                for g in range(2 if gated else 1):
                    mm = pe.matmul(c.PS[:, 2 * (n % 3) + g, :], W1[:, k + g * chunks, :],
                                   c.XT[:, h * HALF:(h + 1) * HALF], start=True, stop=True)
                mm.then_inc(up, 1)
            pe.wait_ge(hidden if gated else gelu, len(steps))
            for t in range(NT):
                for k in range(chunks):
                    mm = pe.matmul(c.tiles(6)[:, t, :], c.HT[:, k, t * P:(t + 1) * P], W2[:, k, :],
                                   start=k == 0, stop=k == chunks - 1)
                mm.then_inc(down, 1)

        @block.scalar
        def _(act):
            act.wait_ge(b_loaded, 32)
            for n, (k, h) in enumerate(steps):
                act.wait_ge(up, n + 1)
                gate = k + chunks * int(gated)
                act.activation(c.HT[:, k, h * HALF:(h + 1) * HALF], c.PS[:, 2 * (n % 3) + int(gated), :],
                               ACT.Gelu, bias=c.bcols[:, gate:gate + 1]).then_inc(gelu, 1)

        @block.vector
        def _(dve):
            dve.wait_ge(b_loaded, 32)
            dve.tensor_tensor(target[:, :, :], target[:, :, :], c.vbias[:, None, :].to_broadcast([P, NT, P]),
                              ALU.add).then_inc(added, 1)
            if gated:
                for n, (k, h) in enumerate(steps):
                    dve.wait_ge(gelu, n + 1)
                    part = c.HT[:, k, h * HALF:(h + 1) * HALF]
                    dve.scalar_tensor_tensor(part, c.PS[:, 2 * (n % 3), :], c.bcols[:, k:k + 1], part,
                                             ALU.add, ALU.mult).then_inc(hidden, 1)
            dve.wait_ge(added, 1)
            for h in range(NH):
                dve.wait_ge(down, (h + 1) * (NT // NH))
                t = slice(h * (NT // NH), (h + 1) * (NT // NH))
                dve.tensor_tensor(target[:, t, :], target[:, t, :], c.tiles(6)[:, t, :], ALU.add).then_inc(added, 1)


def experts(c, w, w2, sel, rows, n_pairs, bias=None, add_tokens=None, add_turned=None):
    routed = bias is None
    ups = 2 if routed else 1
    steps = [(i, h) for i in range(n_pairs) for h in range(NH)]
    sel_bf = c.selb
    with c.stage("pair_loaded", "sel_loaded", "w2_loaded", "bias_loaded", "sel_cast", "w2_cast", "pair_up", "pair_act", "pair_gated",
                 "pair_hidden", "pair_down", "pair_added") as \
            (block, loaded, sel_loaded, w2_loaded, bias_loaded, sel_cast, w2_cast, up, acted, gated, hidden, down, added):
        @block.sync
        def _(sp):
            sp.dma_start((c.EWB if routed else c.EW)[:, 0:n_pairs, 0:ups, :], w).then_inc(loaded, 16)
            sp.dma_start(c.SEL[0:rows, 0:n_pairs, :], sel).then_inc(sel_loaded, 16)
            sp.dma_start((c.EW2B if routed else c.EW2)[:, 0:n_pairs, :], w2).then_inc(w2_loaded, 16)
            if not routed:
                sp.dma_start(c.bcols[:, 0:n_pairs], bias).then_inc(bias_loaded, 16)

        @block.tensor
        def _(pe):
            def ups_of(n):
                i, h = steps[n]
                cols = slice(h * HALF, (h + 1) * HALF)
                if n == 0:
                    pe.wait_ge(loaded, 16)
                if n >= 2:
                    pe.wait_ge(hidden, n - 1)
                for u in range(ups):
                    out = c.PS[:, 3 * (n % 2) + u, :]
                    if routed:
                        for piece in range(3):
                            pe.matmul(out, c.EWB[:, i, u, :], c.QS[:, piece, cols], start=piece == 0, stop=piece == 2)
                    else:
                        pe.matmul(out, c.EW[:, i, u, :], c.XT[:, cols], start=True, stop=True)
                if n == 0:
                    pe.wait_ge(sel_cast, 1)
                pe.matmul(c.PS[:, 3 * (n % 2) + 2, :], sel_bf[0:rows, i, :], c.gatesT[0:rows, cols],
                          start=True, stop=True).then_inc(up, 1)

            def down_of(n):
                i, h = steps[n]
                if n == 0:
                    pe.wait_ge(w2_cast if routed else w2_loaded, 1 if routed else 16)
                pe.wait_ge(hidden, n + 1)
                if add_tokens is not None:
                    for t in range(h * (NT // NH), (h + 1) * (NT // NH)):
                        mm = pe.matmul(c.tiles(6)[:, t, :], c.HT[:, i % 2, t * P:(t + 1) * P], c.EW2[:, i, :],
                                       start=i == 0 and t % (NT // NH) == 0, stop=i == n_pairs - 1,
                                       skip_group_check=True)
                else:
                    mm = pe.matmul(c.PS[:, 6 + h, :], c.EW2[:, i, :], c.HT[:, i % 2, h * HALF:(h + 1) * HALF],
                                   start=i == 0, stop=i == n_pairs - 1)
                mm.then_inc(down, 1)

            for n in range(len(steps)):
                ups_of(n)
                if n:
                    down_of(n - 1)
            down_of(len(steps) - 1)

        @block.scalar
        def _(act):
            if not routed:
                act.wait_ge(bias_loaded, 16)
            for n, (i, h) in enumerate(steps):
                act.wait_ge(up, n + 1)
                if n >= 4:
                    act.wait_ge(down, n - 3)
                part = c.HT[:, i % 2, h * HALF:(h + 1) * HALF]
                if routed:
                    act.activation(part, c.PS[:, 3 * (n % 2), :], ACT.Silu).then_inc(acted, 1)
                else:
                    act.activation(part, c.PS[:, 3 * (n % 2), :], ACT.Relu, bias=c.bcols[:, i:i + 1]).then_inc(acted, 1)

        @block.vector
        def _(dve):
            dve.wait_ge(sel_loaded, 16)
            dve.tensor_copy(sel_bf[0:rows, 0:n_pairs, :], c.SEL[0:rows, 0:n_pairs, :]).then_inc(sel_cast, 1)
            if routed:
                dve.wait_ge(w2_loaded, 16)
                dve.tensor_copy(c.EW2[:, 0:n_pairs, :], c.EW2B[:, 0:n_pairs, :]).then_inc(w2_cast, 1)
            for n, (i, h) in enumerate(steps):
                part = c.HT[:, i % 2, h * HALF:(h + 1) * HALF]
                dve.wait_ge(acted, n + 1)
                if routed:
                    dve.tensor_tensor(part, part, c.PS[:, 3 * (n % 2) + 1, :], ALU.mult).then_inc(gated, 1)
                    dve.wait_ge(gated, n + 1)
                dve.tensor_tensor(part, part, c.PS[:, 3 * (n % 2) + 2, :], ALU.mult).then_inc(hidden, 1)
            for h in range(NH):
                dve.wait_ge(down, len(steps) - NH + h + 1)
                if add_tokens is not None:
                    t = slice(h * (NT // NH), (h + 1) * (NT // NH))
                    dve.tensor_tensor(add_tokens[:, t, :], add_tokens[:, t, :], c.tiles(6)[:, t, :],
                                      ALU.add).then_inc(added, 1)
                else:
                    cols = slice(h * HALF, (h + 1) * HALF)
                    dve.tensor_tensor(add_turned[:, cols], add_turned[:, cols], c.PS[:, 6 + h, :],
                                      ALU.add).then_inc(added, 1)


def some(ap, i, n):
    v = ap[bass.ds(i * n, n)]
    names = "abcd"[:len(v.shape) - 1]
    return v.rearrange(f"z {' '.join(names)} -> {names[0]} z {' '.join(names[1:])}")


def turn_gates(c, rows, exact=False):
    n = 1 if exact else 3
    with c.stage("gate_piece", "gates_turned", "gates_out", "x_piece") as (block, piece, turned, out_done, x_piece):
        out = c.banks(0).bitcast(BF16)

        @block.vector
        def _(dve):
            at = 0

            def next_step(instruction):
                nonlocal at
                instruction.then_inc(piece, 1)
                at += 1
                dve.wait_ge(piece, at)

            g, r = c.gates[:, :, 0:rows], c.gates_rest[:, :, 0:rows]
            pieces = [c.gate_pieces[:, :, i * rows:(i + 1) * rows] for i in range(n)]
            next_step(dve.tensor_copy(pieces[0], g))
            if not exact:
                next_step(dve.tensor_tensor(r, g, pieces[0], ALU.subtract))
                next_step(dve.tensor_copy(pieces[1], r))
                next_step(dve.tensor_tensor(pieces[2], r, pieces[1], ALU.subtract))
                x1, x2, x3 = (c.QS[:, i, :] for i in range(3))
                rest = c.HT[:, 0, :]
                dve.tensor_copy(x1, c.XT[:, :]).then_inc(x_piece, 1)
                dve.wait_ge(x_piece, 1)
                dve.tensor_tensor(rest, c.XT[:, :], x1, ALU.subtract).then_inc(x_piece, 1)
                dve.wait_ge(x_piece, 2)
                dve.tensor_copy(x2, rest).then_inc(x_piece, 1)
                dve.wait_ge(x_piece, 3)
                dve.tensor_tensor(x3, rest, x2, ALU.subtract).then_inc(x_piece, 1)

        @block.tensor
        def _(pe):
            pe.wait_ge(piece, 1 if exact else 4)
            for t in range(NT):
                pe.transpose(out[0:n * rows, t * P:(t + 1) * P], c.gate_pieces[:, t, 0:n * rows],
                             c.identb[:, :]).then_inc(turned, 1)

        @block.scalar
        def _(act):
            act.wait_ge(turned, NT)
            act.activation(c.gatesT[0:n * rows, :], out[0:n * rows, 0:S], ACT.Copy).then_inc(out_done, 1)


def route_experts(c, n):
    d = c.dram
    carry = c.carry[n]
    score, biased, left, chosen, weight, room = (c.small[:, k] for k in range(6))
    with c.stage("gw_loaded", "gw_cast", "logits_done", "sigmoid_done", "route_step", "counted",
                 "carry_ready", "carry_done") as \
            (block, loaded, cast_done, logits, sigm, step, counted, carry_ready, carry_done):
        @block.sync
        def _(sp):
            sp.dma_start(c.WB[:, 0, 0:EXPERTS], d["moe_gate"]).then_inc(loaded, 16)
            sp.dma_start(c.ebias[:, :], d["moe_bias"].partition_broadcast(P)).then_inc(loaded, 16)

        @block.gpsimd
        def _(pool):
            pool.wait_ge(loaded, 32)
            pool.tensor_copy(c.W1[:, 0, 0:EXPERTS], c.WB[:, 0, 0:EXPERTS]).then_inc(cast_done, 1)

        @block.tensor
        def _(pe):
            pe.wait_ge(cast_done, 1)
            for t in range(NT):
                mm = pe.matmul(c.PS[:, 0, t * EXPERTS:(t + 1) * EXPERTS], c.XT[:, t * P:(t + 1) * P],
                               c.W1[:, 0, 0:EXPERTS], start=True, stop=True)
            mm.then_inc(logits, 1)
            pe.wait_ge(step, NT + 2 + NT + 1)
            for t in range(NT):
                out = c.PS[:, 1, t * EXPERTS:(t + 1) * EXPERTS]
                pe.matmul(out, c.ones[0:1, 0:P], carry[:, :], start=True, stop=False)
                for s in range(t):
                    pe.matmul(out, c.ones[:, 0:P], chosen[:, s, :], start=False, stop=False)
                pe.matmul(out, c.before[:, :], chosen[:, t, :], start=False, stop=True).then_inc(counted, 1)
            out = c.PS[0:1, 2, 0:EXPERTS]
            pe.matmul(out, c.ones[0:1, 0:1], carry[:, :], start=True, stop=False)
            for s in range(NT):
                mm = pe.matmul(out, c.ones[:, 0:1], chosen[:, s, :], start=False, stop=s == NT - 1)
            mm.then_inc(carry_ready, 1)

        @block.scalar
        def _(act):
            act.wait_ge(logits, 1)
            act.activation(score, c.PS[:, 0, 0:NT * EXPERTS].rearrange("p (t e) -> p t e", e=EXPERTS),
                           ACT.Sigmoid).then_inc(sigm, 1)

        @block.vector
        def _(dve):
            at = 0

            def next_step(instruction):
                nonlocal at
                instruction.then_inc(step, 1)
                at += 1

            dve.wait_ge(sigm, 1)
            dve.wait_ge(loaded, 32)
            next_step(dve.tensor_tensor(biased, score, c.ebias[:, None, :].to_broadcast([P, NT, EXPERTS]), ALU.add))
            dve.wait_ge(step, at)
            for t in range(NT):
                next_step(dve.max(c.small8[:, t, :], biased[:, t, :]))
            dve.wait_ge(step, at)
            next_step(dve.memset(c.small8[:, :, TOPK:8], 3e38))
            dve.wait_ge(step, at)
            for t in range(NT):
                next_step(dve.match_replace(left[:, t, :], c.small8[:, t, :], biased[:, t, :], -3e38))
            dve.wait_ge(step, at)
            next_step(dve.tensor_tensor(chosen, left, biased, ALU.not_equal))
            dve.wait_ge(step, at)
            next_step(dve.tensor_tensor(weight, score, chosen, ALU.mult))
            dve.wait_ge(step, at)
            next_step(dve.tensor_reduce(c.gsum[:, 0, :], weight, AX_X, ALU.add))
            dve.wait_ge(step, at)
            next_step(dve.tensor_scalar(c.gsum[:, 0, :], c.gsum[:, 0, :], 1e-12, None, ALU.max))
            dve.wait_ge(step, at)
            next_step(dve.reciprocal(c.gsum[:, 1, :], c.gsum[:, 0, :]))
            dve.wait_ge(step, at)
            next_step(dve.tensor_tensor(weight, weight, c.gsum[:, 1, :, None].to_broadcast([P, NT, EXPERTS]), ALU.mult))
            dve.wait_ge(counted, NT)
            next_step(dve.tensor_scalar(room, c.PS[:, 1, 0:NT * EXPERTS].rearrange("p (t e) -> p t e", e=EXPERTS),
                                        float(CAPACITY), None, ALU.is_lt))
            dve.wait_ge(step, at)
            next_step(dve.tensor_tensor(c.gates[:, :, 0:EXPERTS], weight, room, ALU.mult))
            next_step(dve.memset(c.gates[:, :, EXPERTS:EXPERTS + 1], 1.0))
            next_step(dve.memset(c.gates[:, :, EXPERTS + 1:EXPERTS + 2], 0.0))
            dve.wait_ge(carry_ready, 1)
            dve.tensor_copy(carry[:, :], c.PS[0:1, 2, 0:EXPERTS]).then_inc(carry_done, 1)
    turn_gates(c, GATE_ROWS)


def route_leaves(c, node_w, node_b):
    yes, no = c.small[:, 0, :, 0:LEAVES], c.small[:, 1, :, 0:LEAVES]
    with c.stage("nodes_loaded", "nodes_done", "tree_step") as (block, loaded, nodes, step):
        @block.sync
        def _(sp):
            sp.dma_start(c.W1[:, 0, 0:LEAVES - 1], node_w).then_inc(loaded, 16)
            sp.dma_start(c.B1[:, 0, 0:LEAVES - 1], node_b).then_inc(loaded, 16)

        @block.tensor
        def _(pe):
            pe.wait_ge(loaded, 32)
            for t in range(NT):
                out = c.PS[:, 0, t * LEAVES:t * LEAVES + LEAVES - 1]
                pe.matmul(out, c.XT[:, t * P:(t + 1) * P], c.W1[:, 0, 0:LEAVES - 1], start=True, stop=False)
                mm = pe.matmul(out, c.ones[0:1, 0:P], c.B1[:, 0, 0:LEAVES - 1], start=False, stop=True)
            mm.then_inc(nodes, 1)

        @block.vector
        def _(dve):
            at = 0

            def next_step(instruction):
                nonlocal at
                instruction.then_inc(step, 1)
                at += 1

            dve.wait_ge(nodes, 1)
            score = c.PS[:, 0, 0:NT * LEAVES].rearrange("p (t e) -> p t e", e=LEAVES)[:, :, 0:LEAVES - 1]
            next_step(dve.tensor_scalar(yes[:, :, 0:LEAVES - 1], score, 0.0, None, ALU.is_ge))
            dve.wait_ge(step, at)
            next_step(dve.tensor_scalar(no[:, :, 0:LEAVES - 1], yes[:, :, 0:LEAVES - 1], -1.0, 1.0, ALU.mult, ALU.add))
            dve.wait_ge(step, at)
            path = c.small[:, 2, :, 0:2]
            next_step(dve.tensor_copy(path[:, :, 0:1], no[:, :, 0:1]))
            next_step(dve.tensor_copy(path[:, :, 1:2], yes[:, :, 0:1]))
            n, k = 2, 3
            while n < LEAVES:
                dve.wait_ge(step, at)
                wide = c.small[:, k, :, 0:2 * n] if 2 * n < LEAVES else c.gates[:, :, 0:LEAVES]
                split = wide.rearrange("p t (i s) -> p t i s", s=2)
                next_step(dve.tensor_tensor(split[:, :, :, 0], path, no[:, :, n - 1:2 * n - 1], ALU.mult))
                next_step(dve.tensor_tensor(split[:, :, :, 1], path, yes[:, :, n - 1:2 * n - 1], ALU.mult))
                path, n, k = wide, 2 * n, k + 1
    turn_gates(c, LEAVES, exact=True)


def leaf_bias(c, b2, turned=None, tokens=None):
    with c.stage("b2_loaded", "gates_wide", "b2_done", "b2_out") as (block, loaded, wide, done, out_done):
        b2s = c.SEL[0:LEAVES, 0, :]

        @block.sync
        def _(sp):
            sp.dma_start(b2s, b2).then_inc(loaded, 16)

        @block.tensor
        def _(pe):
            pe.wait_ge(loaded, 16)
            pe.wait_ge(wide, 1)
            if turned is not None:
                for h in range(NH):
                    mm = pe.matmul(c.PS[:, h, :], b2s, c.T1[0:LEAVES, h * HALF:(h + 1) * HALF], start=True, stop=True)
            else:
                for t in range(NT):
                    mm = pe.matmul(c.tiles(0)[:, t, :], c.T1[0:LEAVES, t * P:(t + 1) * P], b2s, start=True, stop=True)
            mm.then_inc(done, 1)

        @block.vector
        def _(dve):
            dve.tensor_copy(c.T1[0:LEAVES, :], c.gatesT[0:LEAVES, :]).then_inc(wide, 1)

        @block.scalar
        def _(act):
            act.wait_ge(done, 1)
            if turned is not None:
                act.activation(turned[:, :], c.banks(0), ACT.Copy).then_inc(out_done, 1)
            else:
                act.activation(tokens, c.tiles(0), ACT.Copy).then_inc(out_done, 1)


def shorten_q_k(c, keys=S):
    with c.stage("short_q", "short_k") as (block, short_q, short_k):
        @block.scalar
        def _(act):
            act.activation(c.QB[:, :], c.QT[:, :], ACT.Copy).then_inc(short_q, 1)

        @block.vector
        def _(dve):
            dve.tensor_copy(c.KB[:, 0:keys], c.KT[:, 0:keys]).then_inc(short_k, 1)


def whole_out(c):
    return lambda h, half: c.CTX[:, 4 * half:4 * half + 4, :]



def local_transformer(c):
    d = c.dram
    norm_and_turn(c, c.X, norm=c.Y)
    for layer in range(2):
        norm_and_turn(c, c.Y, shift=True)
        with c.stage("qk_scales") as (block, loaded):
            @block.sync
            def _(sp):
                sp.dma_start(c.gcols[:, :], d["l0f_scales"][layer]).then_inc(loaded, 16)
                sp.wait_ge(loaded, 16)
        attention64_old(c, c.Y, d["l0f_w"][layer], d["l0f_wo"][layer], 4, "window", 8.0, xpos=c.xpos)
        shift_tokens(c, c.Y)
        norm_and_turn(c, c.H, norm=c.CTX, gains=d["l0f_ln"][layer])
        mlp(c, c.Y, d["l0f_w1"][layer], d["l0f_b1"][layer], d["l0f_w2"][layer], d["l0f_b2"][layer], 3, True)
    add_to(c, c.X, c.Y[:, :, :])


def mixture(c, n):
    d = c.dram
    norm_and_turn(c, c.X, norm=c.Y)
    route_experts(c, n)
    rows = 3 * GATE_ROWS
    with c.nc.Fori(0, EXPERTS // 8) as i:
        experts(c, some(d["moe_w"], i, 4), some(d["moe_w2"], i, 4), some(d["c_sel34"], i, 4), rows, 4, add_tokens=c.X)
    shared = GATE_ROWS // 2 - 1
    experts(c, some(d["moe_w"], shared, 1), some(d["moe_w2"], shared, 1), some(d["c_sel34"], shared, 1), rows, 1,
            add_tokens=c.X)


def transformer_block(c):
    d = c.dram
    norm_and_turn(c, c.X, norm=c.Y)
    norm_and_turn(c, c.Y, norm=c.H, gains=d["l1b_ln1"])
    attention8(c, d["l1b_w"], (d["l1b_b"], d["l1b_bv"]), "causal", rope=c.rope8)
    project_out(c, c.Y, d["l1b_wo"], d["l1b_bo"])
    norm_and_turn(c, c.Y, norm=c.H, gains=d["l1b_ln2"])
    mlp(c, c.Y, d["l1b_w1"], d["l1b_b1"], d["l1b_w2"], d["l1b_b2"], 4, False)
    add_to(c, c.X, c.Y[:, :, :])


def adapted_mlp(c):
    d = c.dram
    norm_and_turn(c, c.X, norm=c.Y)
    with c.stage("lora_loaded", "lora_scaled", "lora_rows", "lora_sum") as (block, loaded, scaled, rows, summed):
        @block.sync
        def _(sp):
            sp.dma_start(c.W1[:, 0:4, :], d["l2f_w1"]).then_inc(loaded, 16)
            sp.dma_start(c.W2[:, :, :], d["l2f_w2"]).then_inc(loaded, 16)
            sp.dma_start(c.odd[:, 8:9], d["l2f_scale"].partition_broadcast(P)).then_inc(loaded, 16)

        @block.tensor
        def _(pe):
            for j in range(8):
                pe.matmul(c.tiles(0)[:, j, :], c.pick8[:, j, :], c.Y[:, 0, :], start=True, stop=True).then_inc(rows, 1)

        @block.vector
        def _(dve):
            dve.wait_ge(loaded, 48)
            dve.tensor_scalar(c.odd[:, 0:8], c.XT[:, 2:18:2], c.odd[:, 8:9], None, ALU.mult).then_inc(scaled, 1)
            dve.wait_ge(scaled, 1)
            dve.wait_ge(rows, 8)
            for j in range(4):
                dve.scalar_tensor_tensor(c.W1E[:, j, :], c.tiles(0)[:, j, :], c.odd[:, j:j + 1], c.W1[:, j, :],
                                         ALU.mult, ALU.add).then_inc(summed, 1)
            for j in range(4):
                for r in range(4):
                    dve.scalar_tensor_tensor(c.W2E[:, r, 32 * j:32 * j + 32],
                                             c.tiles(0)[:, 4 + j, r:P:4], c.odd[:, 4 + j:5 + j],
                                             c.W2[:, r, 32 * j:32 * j + 32],
                                             ALU.mult, ALU.add).then_inc(summed, 1)
    mlp(c, c.X, None, d["l2f_b1"], None, d["l2f_b2"], 4, False, batch_weights=True)


def single_head(c):
    heads = Heads(P, 1, P, P ** -0.5, "causal")
    norm_and_turn(c, c.X, norm=c.Y)
    clear_v(c)
    project(c, c.dram["l2a_w"], heads, bias=(c.dram["l2a_b"], c.dram["l2a_bv"]))
    attend(c, heads, whole_out(c))
    add_to(c, c.X, c.CTX[:, :, :])


def cross_attention(c):
    d = c.dram
    keys = 512
    heads = Heads(P, 1, P, 1.0, "full", keys=keys)
    norm_and_turn(c, c.X, norm=c.Y)
    clear_v(c)
    with c.stage("kv_loaded", "v_in", "k_scaled", "k_turned", "k_out") as (block, loaded, v_in, k_scaled, turned, k_out):
        @block.sync
        def _(sp):
            sp.dma_start(c.W1[:, 0:4, :], d["l3a_k"].rearrange("(t p) d -> p t d", p=P)).then_inc(loaded, 16)
            sp.dma_start(c.VA[:, 0:4, 0:P], d["l3a_v"].rearrange("(t p) d -> p t d", p=P)).then_inc(v_in, 16)
            sp.wait_ge(v_in, 16)

        @block.vector
        def _(dve):
            dve.wait_ge(loaded, 16)
            for t in range(4):
                dve.tensor_scalar(c.W1E[:, t, :], c.W1[:, t, :], c.XT[:, 256 * t:256 * t + 1], None,
                                  ALU.mult).then_inc(k_scaled, 1)

        @block.tensor
        def _(pe):
            for t in range(4):
                pe.wait_ge(k_scaled, t + 1)
                pe.transpose(c.PS[:, 0, t * P:(t + 1) * P], c.W1E[:, t, :], c.ident[:, :]).then_inc(turned, 1)

        @block.scalar
        def _(act):
            act.activation(c.QT[:, :], c.XT[:, :], ACT.Copy).then_inc(k_out, 1)
            act.wait_ge(turned, 4)
            act.activation(c.KT[:, 0:keys], c.PS[:, 0, :], ACT.Copy).then_inc(k_out, 1)
    shorten_q_k(c, keys)
    attend(c, heads, whole_out(c))
    add_to(c, c.X, c.CTX[:, :, :])


def tree_attention(c):
    d = c.dram
    heads = Heads(P, 1, P, P ** -0.5, "full")
    norm_and_turn(c, c.X, norm=c.Y)
    clear_v(c)
    for name, turned in (("q", c.QT), ("k", c.KT), ("v", None)):
        tokens = None if turned is not None else c.VA[:, :, 0:P]
        route_leaves(c, d[f"l3f_{name}_node"], d[f"l3f_{name}_nodeb"])
        leaf_bias(c, d[f"l3f_{name}_b2"], turned, tokens)
        with c.nc.Fori(0, LEAVES // 8) as i:
            experts(c, some(d[f"l3f_{name}_w1"], i, 4), some(d[f"l3f_{name}_w2"], i, 4), some(d["c_sel16"], i, 4), LEAVES,
                    4, bias=one(d[f"l3f_{name}_b1"], i), add_tokens=tokens, add_turned=turned)
    shorten_q_k(c)
    attend(c, heads, whole_out(c))
    add_to(c, c.X, c.CTX[:, :, :])


def latent_attention(c):
    d = c.dram
    norm_and_turn(c, c.X, norm=c.Y)
    with c.stage("lat_loaded", "lat_mm", "lat_out", "lat_zero", "lat_stored") as (block, loaded, mm_done, out_done, zeroed, stored):
        dq, uqT, dkv = (c.W1[0:64, s, :] for s in (0, 1, 3))
        uk, uv = c.W1[:, 2, 0:64], c.W1[:, 4, 0:64]
        woT = c.W1[:, 5, :]
        aT, keT, veT = c.W2[:, 0, :], c.W2[0:64, 1, :], c.W2[0:64, 2, :]
        wide = c.HT[:, 0:2, :].rearrange("p a n -> p (a n)")[:, 0:4 * 3 * P].rearrange("p (g s n) -> p g s n", g=4, s=3)

        @block.sync
        def _(sp):
            for dst, src in ((dq, "dq"), (uqT, "uqT"), (dkv, "dkv"), (uk, "uk"), (uv, "uv"), (woT, "woT")):
                sp.dma_start(dst, d[f"l3b_{src}"]).then_inc(loaded, 16)
            sp.wait_ge(out_done, 6)
            sp.dma_start(d["scratch_w"].rearrange("g p s n -> p g s n"), wide).then_inc(stored, 16)
            sp.wait_ge(stored, 16)

        @block.tensor
        def _(pe):
            pe.wait_ge(loaded, 96)
            pe.matmul(c.PS[:, 0, 0:P], uqT, dq, start=True, stop=True).then_inc(mm_done, 1)
            pe.matmul(c.PS[0:64, 1, 0:P], uv, woT, start=True, stop=True).then_inc(mm_done, 1)
            pe.matmul(c.PS[:, 2, 0:P], dq, uqT, start=True, stop=True).then_inc(mm_done, 1)
            pe.wait_ge(out_done, 1)
            pe.matmul(c.PS[0:64, 3, 0:P], uk, aT, start=True, stop=True).then_inc(mm_done, 1)
            pe.wait_ge(out_done, 3)
            pe.matmul(c.PS[:, 4, 0:P], dkv, keT, start=True, stop=True).then_inc(mm_done, 1)
            pe.matmul(c.PS[:, 5, 0:P], dkv, veT, start=True, stop=True).then_inc(mm_done, 1)

        @block.vector
        def _(dve):
            dve.memset(wide, 0.0).then_inc(zeroed, 1)
            dve.wait_ge(mm_done, 1)
            dve.tensor_copy(aT, c.PS[:, 0, 0:P]).then_inc(out_done, 1)
            dve.wait_ge(mm_done, 2)
            dve.tensor_copy(veT, c.PS[0:64, 1, 0:P]).then_inc(out_done, 1)
            dve.wait_ge(mm_done, 4)
            dve.tensor_copy(keT, c.PS[0:64, 3, 0:P]).then_inc(out_done, 1)
            dve.wait_ge(zeroed, 1)
            dve.wait_ge(mm_done, 6)
            for s, bank in enumerate((2, 4, 5)):
                for g in range(4):
                    ins = dve.tensor_copy(wide[:, g, s, :].rearrange("p (h w) -> p h w", w=32)[:, :, 0:8],
                                          c.PS[:, bank, 32 * g:32 * g + 32].rearrange("p (h e) -> p h e", e=8))
                ins.then_inc(out_done, 1)
    attention8(c, d["scratch_w"], None, "causal")
    add_to(c, c.X, c.CTX[:, :, :])


def network(nc, dram):
    with ExitStack() as ctx:
        c = Core(nc, ctx, dram)
        d = dram
        load_constants(c)

        def gqa():
            norm_and_turn(c, c.X, norm=c.Y)
            attention64(c, c.X, d["l0a_w"], d["l0a_wo"], 8, "causal", 0.125, rope=c.rope64)

        def mha():
            norm_and_turn(c, c.X, norm=c.Y)
            clear_v(c)
            with c.stage("wo_loaded") as (block, loaded):
                @block.sync
                def _(sp):
                    sp.dma_start(c.wrows, d["l0b_wo"]).then_inc(loaded, 16)
                    sp.wait_ge(loaded, 16)
            with nc.Fori(0, 8) as pair:
                attend_pair(c, pair, d["l0b_w"], "full", 0.125)

        def small_full():
            norm_and_turn(c, c.X, norm=c.Y)
            attention8(c, d["l1a_w"], (d["l1a_b"], d["l1a_bv"]), "full")
            project_out(c, c.X, d["l1a_wo"], d["l1a_bo"])

        def small_causal():
            norm_and_turn(c, c.X, norm=c.Y)
            attention8(c, d["l2b_w"], (d["l2b_b"], d["l2b_bv"]), "causal")
            project_out(c, c.X, d["l2b_wo"], d["l2b_bo"])

        layers = [gqa, lambda: local_transformer(c), mha, lambda: local_transformer(c),
                  small_full, lambda: mixture(c, 0), lambda: transformer_block(c), lambda: mixture(c, 1),
                  lambda: single_head(c), lambda: adapted_mlp(c), small_causal, lambda: adapted_mlp(c),
                  lambda: cross_attention(c), lambda: tree_attention(c), lambda: latent_attention(c),
                  lambda: tree_attention(c)]
        with nc.Fori(0, 2) as b:
            load_x(c, b)
            for layer in layers:
                layer()
            store_x(c, b)



def constants():
    f = np.float32
    i = np.arange(P)
    q, k = i[:, None], i[None, :]
    causal = np.where(k > q, f(NEG), f(0))
    old = np.where(q + P - k > 64, f(NEG), f(0))
    near = np.where((k > q) | (q - k > 64), f(NEG), f(0))
    out = {"c_ident": np.eye(P, dtype=f), "c_before": (q < k).astype(f),
           "c_block1": (q // 64 == k // 64).astype(f)}
    out["c_masks"] = np.stack([causal, causal.T, near, near.T, old, old.T], 1).astype(f)
    out["c_first"] = np.zeros((P, 3, P), f)
    for n, pitch in enumerate((32, 64, 128)):
        out["c_first"][::pitch, n] = 1
    pick = np.zeros((P, 8, P), f)
    for j in range(8):
        pick[1 + 2 * j, j, :] = 1
    out["c_pick8"] = pick
    rep, coef = np.zeros((P, 4, P), f), np.zeros((P, 4), f)
    for a in range(3):
        for b in range(3):
            for n in range(8):
                row = 32 * a + 8 * b + n
                coef[row] = (a >= 1, a == 2, b >= 1, b == 2)
                for j in range(4):
                    rep[32 * j + n, j, row] = 1
    out["c_rep"], out["c_coef"] = rep, coef
    out["c_coef64"] = np.stack([i >= 64, -(i >= 64).astype(f), -(i < 64).astype(f)], 1).astype(f)
    t = np.arange(S, dtype=f)

    def frequencies(dim):
        return (f(1) / np.power(f(10000), np.arange(0, dim, 2, dtype=f) / f(dim))).astype(f)

    fr = t[None, :] * frequencies(64)[:, None]
    cos, sin = np.cos(fr), np.sin(fr)
    out["c_rope64"] = np.stack([np.tile(cos, (4, 1)), np.concatenate([-sin, sin] * 2)], 1).astype(f)
    base = ((np.arange(0, 64, 2, dtype=f) + f(0.4 * 64)) / f(1.4 * 64)).astype(f)
    power = ((t - f(S // 2)) / f(32)).astype(f)
    scale = np.power(base[:, None], power[None, :]).astype(f)
    out["c_xpos"] = np.stack([np.tile(cos * scale, (4, 1)), np.concatenate([-sin * scale, sin * scale] * 2),
                              np.tile(cos / scale, (4, 1)), np.concatenate([-sin / scale, sin / scale] * 2)],
                             1).astype(f)
    fr8 = t[None, :] * frequencies(8)[:, None]
    rope8 = np.zeros((4, 32, 2, S), f)
    rope8[:, 0:8, 0] = np.tile(np.cos(fr8), (2, 1))
    rope8[:, 0:8, 1] = np.concatenate([-np.sin(fr8), np.sin(fr8)])
    out["c_rope8"] = rope8.reshape(P, 2, S)
    for name, rows in (("c_sel34", GATE_ROWS), ("c_sel16", LEAVES)):
        pieces = 3 if rows == GATE_ROWS else 1
        sel = np.zeros((rows // 2, pieces, rows, P), f)
        for n in range(rows // 2):
            sel[n, :, 2 * n, 0:64] = 1
            sel[n, :, 2 * n + 1, 64:P] = 1
        out[name] = sel.reshape(rows // 2, pieces * rows, P)
    return out


def swap_halves(w, dim):
    lead = w.shape[:-1]
    v = w.reshape(*lead, -1, 2, dim // 2)
    return v[..., ::-1, :].reshape(w.shape)


def by_pairs(parts, n_pairs):
    return np.ascontiguousarray(np.stack([w.reshape(w.shape[0], n_pairs, P) for w in parts], 2).transpose(1, 0, 2, 3))


def doubled_pairs(parts, v, n_pairs):
    out = np.zeros((n_pairs, P, 2 * len(parts) + 1, P), v.dtype)
    sides = out[:, :, 0:-1].reshape(n_pairs, P, 2, len(parts), 2, 64)
    for s, w in enumerate(parts):
        sides[:, :, :, s] = w.reshape(P, n_pairs, 2, 1, 64).transpose(1, 0, 2, 3, 4)
    out[:, :, 0:-1] = sides.reshape(n_pairs, P, 2 * len(parts), P)
    out[:, :, -1] = v.reshape(P, n_pairs, P).transpose(1, 0, 2)
    return out


def by_fours(parts):
    rows = parts[0].shape[0]
    out = np.zeros((4, rows, len(parts), 4, 32), parts[0].dtype)
    for s, w in enumerate(parts):
        out[:, :, s, :, 0:8] = w.reshape(rows, 4, 4, 8).transpose(1, 0, 2, 3)
    return out.reshape(4, rows, len(parts), P)


def by_chunks(w, n):
    return np.ascontiguousarray(w.reshape(n, P, w.shape[-1]).transpose(1, 0, 2))


def layouts(a):
    d = {"x": a["L0_attn_a_x"]}

    def small_biases(name, q_k, v):
        d[name] = by_fours([b.reshape(1, P) for b in q_k])[:, 0].transpose(0, 2, 1)
        d[name + "v"] = by_fours([v.reshape(1, P)])[:, 0, 0]

    def doubled(w):
        return np.broadcast_to(w.reshape(P, 4, 1, 64), (P, 4, 4, 64)).reshape(P, 1024)

    q, k, v = a["L0_attn_a_wq"], doubled(a["L0_attn_a_wk"]), doubled(a["L0_attn_a_wv"])
    d["l0a_w"] = doubled_pairs([q, swap_halves(q, 64), k, swap_halves(k, 64)], v, 8)
    d["l0a_wo"] = a["L0_attn_a_wo"].reshape(8, P, P)
    w = a["L0_attn_b_W_qkv"]
    d["l0b_w"] = doubled_pairs([w[:, 0:1024], w[:, 1024:2048]], w[:, 2048:], 8)
    d["l0b_wo"] = np.concatenate([a["L0_attn_b_W_out"].reshape(16, 64, P).transpose(1, 0, 2)] * 2)

    stacks = {"w": [], "wo": [], "scales": [], "ln": [], "w1": [], "b1": [], "w2": [], "b2": []}
    hid = a["L0_ffn_w2"].shape[1]
    for n in range(2):
        w = a["L0_ffn_wqkv"][n]
        q, k, v = w[:, 0:512], w[:, 512:1024], w[:, 1024:]
        stacks["w"].append(by_pairs([q, swap_halves(q, 64), k, swap_halves(k, 64), v], 4))
        stacks["wo"].append(a["L0_ffn_wo"][n].reshape(4, P, P))
        qs, ks = a["L0_ffn_q_scale"][n], a["L0_ffn_k_scale"][n]
        stacks["scales"].append(np.stack([np.tile(s, 2) for s in (qs, swap_halves(qs, 64), ks, swap_halves(ks, 64))], 1))
        stacks["ln"].append(np.stack([a["L0_ffn_ln_g"][n], a["L0_ffn_ln_b"][n]], 1))
        w1 = np.zeros((P, 2, 3 * P), np.float32)
        w1[:, :, 0:hid] = a["L0_ffn_w1"][n].reshape(P, 2, hid)
        b1 = np.zeros((1, 2, 3 * P), np.float32)
        b1[:, :, 0:hid] = a["L0_ffn_b1"][n].reshape(1, 2, hid)
        w2 = np.zeros((3 * P, P), np.float32)
        w2[0:hid] = a["L0_ffn_w2"][n]
        stacks["w1"].append(w1.reshape(P, 6, P))
        stacks["b1"].append(b1.reshape(6, P).T)
        stacks["w2"].append(by_chunks(w2, 3))
        stacks["b2"].append(a["L0_ffn_b2"][n])
    for name, parts in stacks.items():
        d[f"l0f_{name}"] = np.stack(parts)

    def thirds(w):
        return [w[..., 0:128], w[..., 128:256], w[..., 256:384]]

    d["l1a_w"] = by_fours(thirds(a["L1_attn_a_w_qkv"]))
    q, k, v = thirds(a["L1_attn_a_b_qkv"])
    small_biases("l1a_b", [q, k], v)
    d["l1a_wo"], d["l1a_bo"] = a["L1_attn_a_w_proj"], a["L1_attn_a_b_proj"]
    q, k, v = thirds(a["L1_attn_b_Wqkv"])
    d["l1b_w"] = by_fours([q, swap_halves(q, 8), k, swap_halves(k, 8), v])
    q, k, v = thirds(a["L1_attn_b_bqkv"])
    small_biases("l1b_b", [q, swap_halves(q, 8), k, swap_halves(k, 8)], v)
    d["l1b_wo"], d["l1b_bo"] = a["L1_attn_b_Wo"], a["L1_attn_b_bo"]
    d["l1b_ln1"] = np.stack([a["L1_attn_b_ln1_g"], a["L1_attn_b_ln1_b"]], 1)
    d["l1b_ln2"] = np.stack([a["L1_attn_b_ln2_g"], a["L1_attn_b_ln2_b"]], 1)
    d["l1b_w1"], d["l1b_b1"] = a["L1_attn_b_W1"].reshape(P, 4, P), a["L1_attn_b_b1"].reshape(4, P).T
    d["l1b_w2"], d["l1b_b2"] = by_chunks(a["L1_attn_b_W2"], 4), a["L1_attn_b_b2"]

    dt = a["L1_ffn_W1"].dtype
    w = np.zeros((GATE_ROWS, P, 2, 64), dt)
    w[0:EXPERTS, :, 0], w[0:EXPERTS, :, 1] = a["L1_ffn_W1"], a["L1_ffn_W3"]
    w[EXPERTS, :, 0], w[EXPERTS, :, 1] = a["L1_ffn_sw1"].T, a["L1_ffn_sw3"].T
    d["moe_w"] = np.ascontiguousarray(w.reshape(GATE_ROWS // 2, 2, P, 2, 64).transpose(0, 2, 3, 1, 4)
                                      ).reshape(GATE_ROWS // 2, P, 2, P)
    w2 = np.zeros((GATE_ROWS, 64, P), dt)
    w2[0:EXPERTS], w2[EXPERTS] = a["L1_ffn_W2"], a["L1_ffn_sw2"].T
    d["moe_w2"] = w2.reshape(GATE_ROWS // 2, P, P)
    d["moe_gate"] = a["L1_ffn_gate_w"].T
    d["moe_bias"] = a["L1_ffn_bias"].reshape(EXPERTS)

    d["l2a_w"] = np.stack([a[f"L2_attn_a_W{s}"].T for s in "qkv"], 1)
    d["l2a_b"] = np.stack([a[f"L2_attn_a_b{s}"] for s in "qk"], 1)
    d["l2a_bv"] = a["L2_attn_a_bv"]
    d["l2b_w"] = by_fours([a[f"L2_attn_b_W{s}"] for s in "qkv"])
    small_biases("l2b_b", [a["L2_attn_b_bq"], a["L2_attn_b_bk"]], a["L2_attn_b_bv"])
    d["l2b_wo"], d["l2b_bo"] = a["L2_attn_b_Wo"], a["L2_attn_b_bo"]
    d["l2f_w1"], d["l2f_b1"] = a["L2_ffn_W1"].T.reshape(P, 4, P), a["L2_ffn_b1"].reshape(4, P).T
    d["l2f_w2"], d["l2f_b2"] = by_chunks(a["L2_ffn_W2"].T, 4), a["L2_ffn_b2"]
    d["l2f_scale"] = a["L2_ffn_scale"].reshape(1)

    d["l3a_k"], d["l3a_v"] = a["L3_attn_a_k"][0], a["L3_attn_a_v"][0]
    for s in "qkv":
        d[f"l3f_{s}_node"], d[f"l3f_{s}_nodeb"] = a[f"L3_ffn_{s}_node_w"].T, a[f"L3_ffn_{s}_node_b"].reshape(1, 15)
        d[f"l3f_{s}_w1"] = np.ascontiguousarray(a[f"L3_ffn_{s}_w1"].reshape(8, 2, P, 64).transpose(0, 2, 1, 3)
                                                ).reshape(8, P, 1, P)
        d[f"l3f_{s}_b1"] = a[f"L3_ffn_{s}_b1"].reshape(2, 4, P).transpose(0, 2, 1)
        d[f"l3f_{s}_w2"] = a[f"L3_ffn_{s}_w2"].reshape(8, P, P)
        d[f"l3f_{s}_b2"] = a[f"L3_ffn_{s}_b2"]
    for s in ("dq", "dkv", "uk", "uv"):
        d[f"l3b_{s}"] = a[f"L3_attn_b_W_{s}"]
    d["l3b_uqT"], d["l3b_woT"] = a["L3_attn_b_W_uq"].T, a["L3_attn_b_W_o"].T
    return d


def kernel(**inputs):
    import concourse.bacc as _bacc
    from concourse.bass_utils import run_bass_kernel_spmd as _run

    nc = _bacc.Bacc("TRN2", target_bir_lowering=False, num_devices=1)
    arrays, dram = {}, {}
    for name, value in {**layouts({k: np.asarray(v) for k, v in inputs.items()}), **constants()}.items():
        value = np.ascontiguousarray(value)
        arrays[f"in_{name}"] = value
        dram[name] = nc.dram_tensor(f"in_{name}", value.shape, mybir.dt.from_np(value.dtype), kind="ExternalInput").ap()
    dram["scratch_w"] = nc.dram_tensor("latent_weights", (4, P, 3, P), F32).ap()
    dram["out"] = nc.dram_tensor("out", (2, S, P), F32, kind="ExternalOutput").ap()
    network(nc, dram)
    return _run(nc, [arrays], core_ids=[0]).results[0]["out"]
```

```python
from contextlib import ExitStack, contextmanager

import numpy as np

import concourse.bass as bass
from concourse import mybir

F32 = mybir.dt.float32
BF16 = mybir.dt.bfloat16
ALU = mybir.AluOpType
ACT = mybir.ActivationFunctionType
AX_X = mybir.AxisListType.X

P = 128
S = 1024
NT = S // P
HALF = 512
NH = S // HALF
NEG = -1e30
EXPERTS, TOPK, CAPACITY = 32, 4, 128
GATE_ROWS = EXPERTS + 2
LEAVES = 16


QPH = HALF // P
ROWS, TOP = 96, 100


class Core:

    def __init__(self, nc, ctx, dram):
        self.nc, self.ctx, self.dram = nc, ctx, dram
        self.sems = {}

        def sb(name, shape, dt=F32):
            return ctx.enter_context(nc.sbuf_tensor(name, shape, dt))

        self.sb = sb
        self.X = sb("residual", [P, NT, P])
        self.Y = sb("normalised", [P, NT, P])
        self.H = sb("shifted", [P, NT, P])
        self.XT = sb("x_t", [P, S])
        self.QT, self.KT = sb("q_t", [P, S]), sb("k_t", [P, S])
        self.QB, self.KB = sb("q_t_bf16", [P, S], BF16), sb("k_t_bf16", [P, S], BF16)
        self.QS, self.KS = sb("q_pieces", [P, 4, S], BF16), sb("k_pieces", [P, 4, S], BF16)
        self.T1, self.T2 = sb("turned", [P, S]), sb("squares", [P, S])
        self.VA = sb("v_and_ones", [P, NT, 260])
        self.K3 = sb("k_third", [P, 2, S], BF16)
        self.onehot = sb("onehot", [P, 4])
        self.coef64 = sb("piece_coefs64", [P, 3])
        self.probs8 = sb("probs8_t", [P, 3, 4, HALF])
        self.rowmax = sb("row_max", [P, 2, 4, 4, 2])
        self.negmax8 = sb("neg_max8", [P, 2, 4, 4], BF16)
        self.out8 = sb("out8_t", [P, 2, HALF])
        self.rden8 = sb("rden8", [P, 2, 4, 4])
        self.wrows = self.probs8[:, 0, :, :].rearrange("p a (m n) -> p (a m) n", n=P)
        self.vbias = sb("v_bias", [P, P])
        self.bcols = sb("bias_columns", [P, 6])
        self.CTX, self.CT = sb("context", [P, NT, P]), sb("context_t", [P, S])
        self.HT = sb("hidden_t", [P, 4, S])
        self.rest = self.HT[:, 0:2, :]
        self.top = self.HT[:, 2, :].bitcast(BF16).rearrange("p (n s) -> p n s", n=2)
        self.mid = self.HT[:, 3, :].bitcast(BF16).rearrange("p (n s) -> p n s", n=2)
        self.stats, self.mv = sb("ln_stats", [P, NT, 6]), sb("ln_mean_var", [P, NT, 2])
        self.rstd = sb("ln_rstd", [P, NT, 2])
        self.W = sb("w_qkv", [P, 9, P])
        self.WO = sb("w_out", [P, P])
        self.W1, self.W2 = sb("w_up", [P, 6, P]), sb("w_down", [P, 4, P])
        self.node_bias = sb("node_bias", [P, LEAVES - 1])
        self.W1E, self.W2E = sb("w_up_eff", [P, 4, P]), sb("w_down_eff", [P, 4, P])
        self.gate_w = sb("gate_weights", [P, EXPERTS], BF16)
        self.SEL, self.selb = sb("pick_rows", [3 * GATE_ROWS, 4, P]), sb("pick_rows_bf16", [3 * GATE_ROWS, 4, P], BF16)
        self.gcols = sb("gain_bias", [P, 4])
        self.gates = sb("gates", [P, NT, GATE_ROWS])
        self.gates_rest = sb("gates_rest", [P, NT, GATE_ROWS])
        self.gate_pieces = sb("gate_pieces", [P, NT, 3 * GATE_ROWS], BF16)
        self.gatesT = sb("gates_t", [3 * GATE_ROWS, S], BF16)
        self.EW, self.EW2 = sb("w_pair_up", [P, 4, 1, P]), sb("w_pair_down", [P, 4, P])
        self.EWB = self.KS[:, 0, :].rearrange("p (i u n) -> p i u n", i=4, u=2)
        self.EW2B = self.KS[:, 1, 0:4 * P].rearrange("p (i n) -> p i n", i=4)
        self.small = sb("small", [P, 6, NT, EXPERTS])
        self.small8 = sb("top8", [P, NT, 8])
        self.gsum = sb("gate_sums", [P, 2, NT])
        self.ebias = sb("expert_bias", [P, EXPERTS])
        self.carry = [sb(f"expert_count_{n}", [1, EXPERTS]) for n in range(2)]
        self.probs = sb("probs_t", [P, 3, HALF])
        self.negmax = sb("neg_max", [P, 2, 4], BF16)
        self.negmax_row = sb("neg_max_row", [P, 2, HALF], BF16)
        self.rden = sb("rden", [P, 4, 1])
        self.odd = sb("odd_scaled", [P, 9])
        self.ident, self.identb = sb("ident", [P, P]), sb("ident_bf16", [P, P], BF16)
        self.masks = sb("masks", [P, 6, P], BF16)
        self.before = sb("before", [P, P])
        self.block1 = sb("block_ones", [P, P])
        self.pick8 = sb("pick8", [P, 8, P])
        self.ones = sb("ones", [P, HALF])
        self.first = sb("first_rows", [P, 3, P], BF16)
        self.rope64 = sb("rope64", [P, 2, S])
        self.rope8 = sb("rope8", [P, 2, S])
        self.xpos = sb("xpos", [P, 4, S])
        self.PS = ctx.enter_context(nc.psum_tensor("psum", [P, 8, HALF], F32))

    def banks(self, first, n=2):
        return self.PS[:, first:first + n, :].rearrange("p b n -> p (b n)")

    def tiles(self, first):
        return self.banks(first).rearrange("p (t d) -> p t d", d=P)

    @contextmanager
    def stage(self, *names):
        for n in names:
            if n not in self.sems:
                self.sems[n] = self.ctx.enter_context(self.nc.semaphore(n))
        sems = [self.sems[n] for n in names]
        with self.nc.Block() as block:
            yield [block] + sems
        for s in sems:
            self.nc.gpsimd.sem_clear(s)
        self.nc.all_engine_barrier()


def one(ap, i):
    v = ap[bass.ds(i, 1)]
    names = "abcd"[:len(v.shape) - 1]
    if len(names) == 1:
        return v
    return v.rearrange(f"z {' '.join(names)} -> (z {names[0]}) {' '.join(names[1:])}")



def load_constants(c):
    d = c.dram
    with c.stage("const_loaded", "const_set") as (block, loaded, const_set):
        todo = [(c.ident, d["c_ident"]), (c.before, d["c_before"]), (c.block1, d["c_block1"]),
                (c.pick8, d["c_pick8"]), (c.coef64, d["c_coef64"]), (c.rope64, d["c_rope64"]), (c.rope8, d["c_rope8"]), (c.xpos, d["c_xpos"])]

        @block.sync
        def _(sp):
            for dst, src in todo:
                sp.dma_start(dst[:], src).then_inc(loaded, 16)
            sp.dma_start(c.H[:, 0:6, :], d["c_masks"]).then_inc(loaded, 16)
            sp.dma_start(c.Y[:, 0:3, :], d["c_first"]).then_inc(loaded, 16)
            sp.dma_start(c.onehot[96:100, :], d["c_ident"][0:4, 0:4]).then_inc(loaded, 16)

        @block.vector
        def _(dve):
            dve.memset(c.ones[:, :], 1.0).then_inc(const_set, 1)
            dve.memset(c.negmax_row[:, :, :], 0.0).then_inc(const_set, 1)
            dve.memset(c.carry[0][:, :], 0.0).then_inc(const_set, 1)
            dve.memset(c.carry[1][:, :], 0.0).then_inc(const_set, 1)
            dve.wait_ge(loaded, 16 * (len(todo) + 3))
            dve.tensor_copy(c.identb[:, :], c.ident[:, :]).then_inc(const_set, 1)
            dve.tensor_copy(c.masks[:, :, :], c.H[:, 0:6, :]).then_inc(const_set, 1)
            dve.tensor_copy(c.first[:, :, :], c.Y[:, 0:3, :]).then_inc(const_set, 1)


def load_x(c, b):
    with c.stage("x_loaded") as (block, loaded):
        @block.sync
        def _(sp):
            sp.dma_start(c.X[:, :, :], one(c.dram["x"], b).rearrange("(t p) d -> p t d", p=P)).then_inc(loaded, 16)
            sp.wait_ge(loaded, 16)


def store_x(c, b):
    with c.stage("x_stored") as (block, stored):
        @block.sync
        def _(sp):
            sp.dma_start(one(c.dram["out"], b).rearrange("(t p) d -> p t d", p=P), c.X[:, :, :]).then_inc(stored, 16)
            sp.wait_ge(stored, 16)


def add_to(c, target, part):
    with c.stage("added") as (block, added):
        @block.vector
        def _(dve):
            dve.tensor_tensor(target[:, :, :], target[:, :, :], part, ALU.add).then_inc(added, 1)


def shift_tokens(c, src):
    with c.stage("shift_done", "shift_dma") as (block, done, moved):
        @block.vector
        def _(dve):
            dve.tensor_copy(c.H[:, :, 0:64], src[:, :, 0:64]).then_inc(done, 1)
            dve.memset(c.H[0:1, 0:1, 64:P], 0.0).then_inc(done, 1)

        @block.sync
        def _(sp):
            sp.dma_start(c.H[1:P, :, 64:P], src[0:P - 1, :, 64:P]).then_inc(moved, 16)
            sp.dma_start(c.H[0:1, 1:NT, 64:P], src[P - 1:P, 0:NT - 1, 64:P]).then_inc(moved, 16)
            sp.wait_ge(moved, 32)



def norm_and_turn(c, src, norm=None, gains=None, shift=False):
    with c.stage("ln_loaded", "ln_stats_done", "ln_aggr_done", "ln_root", "ln_rstd_done",
                 "ln_done", "turned_tiles", "turned_out") as \
            (block, loaded, stats_done, aggr_done, root, rstd_done, normed, turned, out_done):
        src_t = norm if norm is not None else src
        tiles = c.tiles(0)

        if gains is not None:
            @block.sync
            def _(sp):
                sp.dma_start(c.gcols[:, 0:2], gains).then_inc(loaded, 16)

        if norm is not None:
            @block.vector
            def _(dve):
                for t in range(NT):
                    dve.bn_stats(c.stats[:, t, :], src[:, t, :]).then_inc(stats_done, 1)
                for t in range(NT):
                    dve.wait_ge(stats_done, t + 1)
                    dve.bn_aggr(c.mv[:, t, :], c.stats[:, t, :]).then_inc(aggr_done, 1)
                dve.wait_ge(aggr_done, NT)
                dve.tensor_scalar(c.rstd[:, :, 0], c.mv[:, :, 1], 1e-5, None, ALU.add).then_inc(root, 1)
                dve.wait_ge(root, 2)
                dve.reciprocal(c.rstd[:, :, 1], c.rstd[:, :, 0]).then_inc(rstd_done, 1)
                dve.wait_ge(rstd_done, 1)
                for t in range(NT):
                    dve.tensor_scalar(norm[:, t, :], src[:, t, :], c.mv[:, t, 0:1], c.rstd[:, t, 1:2],
                                      ALU.subtract, ALU.mult).then_inc(normed, 1)

        @block.tensor
        def _(pe):
            for t in range(NT):
                if norm is not None:
                    pe.wait_ge(normed, t + 1)
                pe.transpose(tiles[:, t, :], src_t[:, t, :], c.ident[:, :]).then_inc(turned, 1)

        @block.scalar
        def _(act):
            if norm is not None:
                act.wait_ge(root, 1)
                act.activation(c.rstd[:, :, 0], c.rstd[:, :, 0], ACT.Sqrt).then_inc(root, 1)
            if gains is not None:
                act.wait_ge(loaded, 16)
            if shift:
                act.wait_ge(turned, NT)
                act.activation(c.XT[0:64, :], c.banks(0)[0:64, :], ACT.Copy).then_inc(out_done, 1)
                act.activation(c.XT[64:P, 1:S], c.banks(0)[64:P, 0:S - 1], ACT.Copy).then_inc(out_done, 1)
                act.activation(c.XT[64:P, 0:1], c.ones[64:P, 0:1], ACT.Copy, scale=0.0).then_inc(out_done, 1)
                return
            for h in range(NH):
                act.wait_ge(turned, (h + 1) * (NT // NH))
                part = c.XT[:, h * HALF:(h + 1) * HALF]
                if gains is None:
                    act.activation(part, c.banks(0)[:, h * HALF:(h + 1) * HALF], ACT.Copy).then_inc(out_done, 1)
                else:
                    act.activation(part, c.banks(0)[:, h * HALF:(h + 1) * HALF], ACT.Identity,
                                   bias=c.gcols[:, 1:2], scale=c.gcols[:, 0:1]).then_inc(out_done, 1)



class Heads:

    def __init__(self, dim, n, rows, scale, mode, keys=S):
        self.dim, self.n, self.rows, self.scale, self.mode = dim, n, rows, scale, mode
        self.key_tiles = keys // P

    def v(self, c, tile, h):
        w = self.dim + 1
        return c.VA[:, tile, h * w:(h + 1) * w]

    def sees(self, q):
        return {"full": (0, self.key_tiles), "causal": (0, q + 1), "window": (max(q - 1, 0), q + 1)}[self.mode]

    def mask(self, q, k, turned):
        if self.mode == "causal" and q == k:
            return int(turned)
        if self.mode == "window":
            return (2 if q == k else 4) + int(turned)
        return None


def clear_v(c):
    with c.stage("ones_set") as (block, ones_set):
        @block.vector
        def _(dve):
            dve.memset(c.VA[:, :, :], 1.0).then_inc(ones_set, 1)


def project(c, w, heads, bias=None, rope=None, xpos=None):
    turned = rope is not None or xpos is not None
    slots = 5 if turned else 3
    with c.stage("w_loaded", "projected", "rope_one", "rope_two", "rope_sum", "squared", "norm_summed",
                 "norm_root", "norm_clip", "norm_inv", "evacuated", "v_out", "b_loaded") as \
            (block, loaded, projected, one_done, two_done, summed, squared, norm_summed, norm_root,
             norm_clip, norm_inv, evacuated, v_out, b_loaded):
        outs = [(c.QT, c.QB), (c.KT, c.KB)]
        step = 2 if turned else 1
        w_v = slots - 1
        pitch = P // heads.n

        def v_to(h):
            at = h * (32 if heads.dim == 8 else heads.dim + 1)
            return c.VA[:, :, at:at + heads.dim]

        def v_from(h):
            return c.tiles(0)[:, :, h * pitch:h * pitch + heads.dim]


        @block.sync
        def _(sp):
            sp.dma_start(c.W[:, 0:slots, :], w).then_inc(loaded, 16)
            if bias is not None:
                cols, row = bias
                sp.dma_start(c.bcols[:, 0:slots - 1], cols).then_inc(b_loaded, 16)
                sp.dma_start(c.vbias[:, :], row.partition_broadcast(P)).then_inc(b_loaded, 16)

        @block.tensor
        def _(pe):
            pe.wait_ge(loaded, 16)
            for s in range(slots - 1):
                for h in range(NH):
                    out = c.PS[:, 2 * s + h, :]
                    mm = pe.matmul(out, c.W[:, s, :], c.XT[:, h * HALF:(h + 1) * HALF], start=True, stop=True)
                mm.then_inc(projected, 1)
            if xpos is not None:
                for n in range(2):
                    pe.wait_ge(squared, n + 1)
                    pe.wait_ge(summed, n + 1)
                    for h in range(NH):
                        mm = pe.matmul(c.PS[:, 4 * n + h, :], c.block1[:, :], c.T2[:, h * HALF:(h + 1) * HALF],
                                       start=True, stop=True)
                    mm.then_inc(norm_summed, 1)
                pe.wait_ge(norm_root, 1)
            else:
                pe.wait_ge(summed, 1)
            tiles = c.tiles(0)
            for t in range(NT):
                mm = pe.matmul(tiles[:, t, :], c.XT[:, t * P:(t + 1) * P], c.W[:, w_v, :], start=True, stop=True)
            mm.then_inc(projected, 1)

        @block.vector
        def _(dve):
            for n, (out, _) in enumerate(outs):
                dve.wait_ge(projected, step * (n + 1))
                straight = c.banks(2 * step * n)
                if n == 0 and bias is not None:
                    dve.wait_ge(b_loaded, 32)
                if not turned:
                    if bias is None:
                        dve.tensor_copy(out[:, :], straight).then_inc(summed, 1)
                    else:
                        dve.tensor_scalar(out[:, :], straight, c.bcols[:, n:n + 1], None, ALU.add).then_inc(summed, 1)
                    continue
                across = c.banks(2 * step * n + 2)
                if n:
                    dve.wait_ge(summed, n)
                if bias is not None:
                    dve.scalar_tensor_tensor(out[:, :], straight, c.bcols[:, 2 * n:2 * n + 1], rope[:, 0, :],
                                             ALU.add, ALU.mult).then_inc(one_done, 1)
                    dve.scalar_tensor_tensor(c.T1[:, :], across, c.bcols[:, 2 * n + 1:2 * n + 2], rope[:, 1, :],
                                             ALU.add, ALU.mult).then_inc(two_done, 1)
                elif xpos is None:
                    dve.tensor_tensor(out[:, :], straight, rope[:, 0, :], ALU.mult).then_inc(one_done, 1)
                    dve.tensor_tensor(c.T1[:, :], across, rope[:, 1, :], ALU.mult).then_inc(two_done, 1)
                else:
                    dve.scalar_tensor_tensor(out[:, :], straight, c.gcols[:, 2 * n:2 * n + 1], xpos[:, 2 * n, :],
                                             ALU.mult, ALU.mult).then_inc(one_done, 1)
                    dve.scalar_tensor_tensor(c.T1[:, :], across, c.gcols[:, 2 * n + 1:2 * n + 2],
                                             xpos[:, 2 * n + 1, :], ALU.mult, ALU.mult).then_inc(two_done, 1)
                dve.wait_ge(one_done, n + 1)
                dve.wait_ge(two_done, n + 1)
                dve.tensor_tensor(out[:, :], out[:, :], c.T1[:, :], ALU.add).then_inc(summed, 1)
                if xpos is not None:
                    dve.wait_ge(norm_root, n + 1)
                    dve.tensor_scalar(c.CT[:, :], c.CT[:, :], 1e-12, None, ALU.max).then_inc(norm_clip, 1)
                    dve.wait_ge(norm_clip, n + 1)
                    dve.reciprocal(c.CT[:, :], c.CT[:, :]).then_inc(norm_inv, 1)
                    dve.wait_ge(norm_inv, n + 1)
                    dve.wait_ge(summed, n + 1)
                    dve.tensor_tensor(out[:, :], out[:, :], c.CT[:, :], ALU.mult).then_inc(v_out, 1)

            if bias is not None:
                dve.wait_ge(projected, slots)
                for h in range(heads.n):
                    dve.tensor_tensor(v_to(h), v_from(h), c.vbias[:, None, pitch * h:pitch * h + heads.dim]
                                      .to_broadcast([P, NT, heads.dim]), ALU.add).then_inc(v_out, 1)

        @block.scalar
        def _(act):
            for n, (out, short) in enumerate(outs):
                act.wait_ge(projected, step * (n + 1))
                if xpos is not None:
                    act.wait_ge(one_done, n + 1)
                    if n:
                        act.wait_ge(norm_summed, n)
                        act.wait_ge(v_out, n)
                    act.activation(c.T2[:, :], c.banks(4 * n), ACT.Square).then_inc(squared, 1)
                    act.wait_ge(norm_summed, n + 1)
                    act.activation(c.CT[:, :], c.banks(4 * n), ACT.Sqrt).then_inc(norm_root, 1)
                    act.wait_ge(v_out, n + 1)
                    act.activation(short[:, :], out[:, :], ACT.Copy).then_inc(evacuated, 1)
                elif turned:
                    act.wait_ge(summed, n + 1)
                    if heads.dim > 8:
                        act.activation(short[:, :], out[:, :], ACT.Copy).then_inc(evacuated, 1)
                elif heads.dim > 8:
                    act.wait_ge(summed, n + 1)
                    act.activation(short[:, :], out[:, :], ACT.Copy).then_inc(evacuated, 1)
            act.wait_ge(projected, slots)
            for h in range(heads.n):
                if bias is None:
                    act.activation(v_to(h), v_from(h), ACT.Copy).then_inc(v_out, 1)


def attend(c, heads, out_at):
    units = [(h, half) for h in range(heads.n) for half in range(NH)]
    QPH = HALF // P
    pitch = P // heads.n
    work = []
    for u, (h, half) in enumerate(units):
        for k in range(heads.key_tiles):
            cols = [q - half * QPH for q in range(half * QPH, (half + 1) * QPH)
                    if heads.sees(q)[0] <= k < heads.sees(q)[1]]
            if cols:
                work.append((u, k, cols[0], cols[-1] + 1))
    first = [min(i for i, x in enumerate(work) if x[0] == u) for u in range(len(units))] + [len(work)]
    RING = QPH + 1
    first_index = {32: 0, 64: 1, 128: 2}[pitch]

    with c.stage("rows_ready", "rows_read", "scores_ready", "probs_ready", "pv_done",
                 "rden_done", "out_done") as \
            (block, rows_ready, rows_read, scores_ready, probs_ready, pv_done, rden_done, out_done):

        def rows(h):
            return slice(h * pitch, h * pitch + heads.rows)

        def o_at(q):
            w = heads.dim + 1
            return (6 + q // 2, (q % 2) * w) if heads.dim == P else (6, q * w)

        @block.tensor
        def _(pe):
            def row_scores(u, j):
                h, half = units[u]
                q = half * QPH + j
                use = u * RING + j
                lo, hi = heads.sees(q)
                if use >= 2:
                    pe.wait_ge(rows_read, use - 1)
                k = lo
                while k < hi:
                    n = 1
                    masked = heads.mask(q, k, False)
                    while (masked is None and k + n < hi and (k + n - lo) % QPH and
                           heads.mask(q, k + n, False) is None):
                        n += 1
                    col = (k - lo) % QPH * P
                    out = c.PS[:, 2 * (use % 2) + (k - lo) // QPH, col:col + n * P]
                    mm = pe.matmul(out, c.QB[rows(h), q * P:(q + 1) * P], c.KB[rows(h), k * P:(k + n) * P],
                                   start=True, stop=masked is None)
                    if masked is not None:
                        mm = pe.matmul(out, c.identb[:, :], c.masks[:, masked, :], start=False, stop=True)
                    k += n
                mm.then_inc(rows_ready, 1)

            def max_row(u):
                use = u * RING + QPH
                pe.wait_ge(rows_read, use)
                for j in range(QPH):
                    mm = pe.matmul(c.PS[0:1, 2 * (use % 2), j * P:(j + 1) * P], c.negmax[:, u % 2, j:j + 1],
                                   c.identb[:, :], start=True, stop=True)
                mm.then_inc(rows_ready, 1)

            def scores(n):
                u, k, lo, hi = work[n]
                h, half = units[u]
                if n >= 2:
                    pe.wait_ge(probs_ready, n - 1)
                if n == first[u]:
                    pe.wait_ge(rows_read, (u + 1) * RING)
                out = c.PS[:, 4 + n % 2, lo * P:hi * P]
                q0 = half * HALF
                pe.matmul(out, c.KT[rows(h), k * P:(k + 1) * P], c.QT[rows(h), q0 + lo * P:q0 + hi * P],
                          start=True, stop=False)
                for j in range(lo, hi):
                    masked = heads.mask(half * QPH + j, k, True)
                    if masked is not None:
                        pe.matmul(c.PS[:, 4 + n % 2, j * P:(j + 1) * P], c.identb[:, :], c.masks[:, masked, :],
                                  start=False, stop=False)
                mm = pe.matmul(out, c.first[rows(h), first_index, :], c.negmax_row[rows(h), u % 2, lo * P:hi * P], start=False, stop=True)
                mm.then_inc(scores_ready, 1)

            def weighted(n):
                u, k, lo, hi = work[n]
                h, half = units[u]
                pe.wait_ge(probs_ready, n + 1)
                if n == first[u] and u >= 1:
                    pe.wait_ge(out_done, u)
                for j in range(lo, hi):
                    bank, col = o_at(j)
                    opens = n == first[u] and (j == lo or (heads.dim == P and j % 2 == 0))
                    mm = pe.matmul(c.PS[:, bank, col:col + heads.dim + 1],
                                   c.probs[:, n % 3, j * P:(j + 1) * P], heads.v(c, k, h),
                                   start=opens, stop=k + 1 == heads.sees(half * QPH + j)[1], skip_group_check=True)
                mm.then_inc(pv_done, 1)

            for j in range(QPH):
                row_scores(0, j)
            max_row(0)
            for u in range(len(units)):
                ahead = list(range(QPH)) if u + 1 < len(units) else []
                for n in range(first[u], first[u + 1]):
                    scores(n)
                    if ahead and (n - first[u]) % 2 == 1:
                        row_scores(u + 1, ahead.pop(0))
                    if n > first[u]:
                        weighted(n - 1)
                while ahead:
                    row_scores(u + 1, ahead.pop(0))
                if u + 1 < len(units):
                    max_row(u + 1)
                weighted(first[u + 1] - 1)

        @block.scalar
        def _(act):
            for n, (u, k, lo, hi) in enumerate(work):
                act.wait_ge(scores_ready, n + 1)
                if n >= 3:
                    act.wait_ge(pv_done, n - 2)
                act.activation(c.probs[:, n % 3, lo * P:hi * P], c.PS[:, 4 + n % 2, lo * P:hi * P], ACT.Exp,
                               scale=heads.scale).then_inc(probs_ready, 1)

        @block.vector
        def _(dve):
            def maxima(u):
                h, half = units[u]
                for j in range(QPH):
                    use = u * RING + j
                    lo, hi = heads.sees(half * QPH + j)
                    dve.wait_ge(rows_ready, use + 1)
                    dve.tensor_reduce(c.negmax[:, u % 2, j:j + 1], c.banks(2 * (use % 2))[:, 0:(hi - lo) * P],
                                      AX_X, ALU.max, negate=True).then_inc(rows_read, 1)
                use = u * RING + QPH
                dve.wait_ge(rows_ready, use + 1)
                if u >= 2:
                    dve.wait_ge(scores_ready, first[u - 1])
                dve.wait_ge(rows_read, use)
                dve.tensor_copy(c.negmax_row[h * pitch:h * pitch + 1, u % 2, :], c.PS[0:1, 2 * (use % 2), :]).then_inc(rows_read, 1)

            def divide(u):
                h, half = units[u]
                d = heads.dim
                dve.wait_ge(pv_done, first[u + 1])
                if u:
                    dve.wait_ge(out_done, u)
                if d < P:
                    o = c.PS[:, 6, 0:QPH * (d + 1)].rearrange("p (q w) -> p q w", w=d + 1)
                else:
                    o = c.PS[:, 6:8, 0:2 * (d + 1)].rearrange("p b (q w) -> p b q w", w=d + 1)
                if d < P:
                    dve.reciprocal(c.rden[:, :, :], o[:, :, d:d + 1]).then_inc(rden_done, 1)
                    dve.wait_ge(rden_done, u + 1)
                    dve.tensor_tensor(out_at(h, half), o[:, :, 0:d], c.rden[:, :, :].to_broadcast([P, QPH, d]),
                                      ALU.mult).then_inc(out_done, 1)
                else:
                    for b in range(2):
                        dve.reciprocal(c.rden[:, 2 * b:2 * b + 2, :], o[:, b, :, d:d + 1]).then_inc(rden_done, 1)
                    dve.wait_ge(rden_done, 2 * (u + 1))
                    for b in range(2):
                        mm = dve.tensor_tensor(out_at(h, half)[:, 2 * b:2 * b + 2, :], o[:, b, :, 0:d],
                                               c.rden[:, 2 * b:2 * b + 2, :].to_broadcast([P, 2, d]), ALU.mult)
                    mm.then_inc(out_done, 1)

            maxima(0)
            for u in range(len(units)):
                if u + 1 < len(units):
                    maxima(u + 1)
                divide(u)


def project_out(c, target, w, bias=None):
    with c.stage("wo_loaded", "ctx_turned", "ctx_out", "y_ready", "y_added") as \
            (block, loaded, turned, ctx_out, y_ready, y_added):
        @block.sync
        def _(sp):
            sp.dma_start(c.WO[:, :], w).then_inc(loaded, 16)
            if bias is not None:
                sp.dma_start(c.vbias[:, :], bias.partition_broadcast(P)).then_inc(loaded, 16)

        @block.tensor
        def _(pe):
            for t in range(NT):
                pe.transpose(c.tiles(0)[:, t, :], c.CTX[:, t, :], c.ident[:, :]).then_inc(turned, 1)
            pe.wait_ge(loaded, 32 if bias is not None else 16)
            for t in range(NT):
                if t % (NT // NH) == 0:
                    pe.wait_ge(ctx_out, t // (NT // NH) + 1)
                pe.matmul(c.tiles(2)[:, t, :], c.CT[:, t * P:(t + 1) * P], c.WO[:, :],
                          start=True, stop=True).then_inc(y_ready, 1)

        @block.scalar
        def _(act):
            for h in range(NH):
                act.wait_ge(turned, (h + 1) * (NT // NH))
                act.activation(c.CT[:, h * HALF:(h + 1) * HALF], c.PS[:, h, :], ACT.Copy).then_inc(ctx_out, 1)

        @block.vector
        def _(dve):
            if bias is not None:
                dve.wait_ge(loaded, 32)
                dve.tensor_tensor(target[:, :, :], target[:, :, :], c.vbias[:, None, :].to_broadcast([P, NT, P]),
                                  ALU.add).then_inc(y_added, 1)
                dve.wait_ge(y_added, 1)
            for h in range(NH):
                dve.wait_ge(y_ready, (h + 1) * (NT // NH))
                t = slice(h * (NT // NH), (h + 1) * (NT // NH))
                dve.tensor_tensor(target[:, t, :], target[:, t, :], c.tiles(2)[:, t, :], ALU.add).then_inc(y_added, 1)


def head_norms(c, w, scales):
    n_heads = w.shape[-1] // 64
    with c.stage("w_loaded", "scales_loaded", "natural_ready", "square_done", "square_summed", "norm_root", "norm_clip", "norm_inv") as \
            (block, loaded, scales_loaded, natural, squared, summed, root, clipped, inverted):
        w_sb = c.HT[:, 0, :]
        squares = (c.HT[:, 1, :], c.HT[:, 2, :])
        norms = c.gates[:, :, 0:n_heads]

        @block.sync
        def _(sp):
            sp.dma_start(w_sb, w).then_inc(loaded, 16)
            sp.dma_start(c.gcols[:, :], scales).then_inc(scales_loaded, 16)
            sp.wait_ge(scales_loaded, 16)

        @block.tensor
        def _(pe):
            pe.wait_ge(loaded, 16)
            for t in range(NT):
                if t >= 4:
                    pe.wait_ge(squared, t - 3)
                for h in range(NH):
                    mm = pe.matmul(c.PS[:, 2 * (t % 4) + h, :], c.XT[:, t * P:(t + 1) * P],
                                   w_sb[:, h * HALF:(h + 1) * HALF], start=True, stop=True)
                mm.then_inc(natural, 1)

        @block.scalar
        def _(act):
            for t in range(NT):
                act.wait_ge(natural, t + 1)
                if t >= 2:
                    act.wait_ge(summed, t - 1)
                act.activation(squares[t % 2], c.banks(2 * (t % 4)), ACT.Square).then_inc(squared, 1)
            act.wait_ge(summed, NT)
            act.activation(norms, norms, ACT.Sqrt).then_inc(root, 1)

        @block.vector
        def _(dve):
            for t in range(NT):
                dve.wait_ge(squared, t + 1)
                dve.tensor_reduce(c.gates[:, t, 0:n_heads], squares[t % 2].rearrange("p (h d) -> p h d", d=64),
                                  AX_X, ALU.add).then_inc(summed, 1)
            dve.wait_ge(root, 1)
            dve.tensor_scalar(norms, norms, 1e-12, None, ALU.max).then_inc(clipped, 1)
            dve.wait_ge(clipped, 1)
            dve.reciprocal(norms, norms).then_inc(inverted, 1)
    turn_gates(c, n_heads, tokens=False)


class PairPrep:
    SEMS = ("w_loaded", "projected", "turn_one", "turn_two", "turn_done", "turn_sum", "top_done", "rest_done",
            "piece2_done", "q_done", "k_done", "v_ready", "v_out", "sel_cast", "norm_rows")
    PARTS = 8

    def __init__(self, c, w, sets, rope, xpos, sel, sems, alone=False):
        self.c, self.w, self.sets, self.rope, self.xpos, self.sel = c, w, sets, rope, xpos, sel
        self.alone = alone
        (self.w_loaded, self.projected, self.turn_one, self.turn_two, self.turn_done, self.turn_sum, self.top_done,
         self.rest_done, self.piece2_done, self.q_done, self.k_done, self.v_ready, self.v_out, self.sel_cast,
         self.norm_rows) = sems
        self.turned = rope is not None or xpos is not None
        self.per_item = 2 if self.turned else 1
        self.slots = 4 * self.per_item + 1
        self.sel_rows = None if sel is None else sel.shape[1]
        self.loads = 1 if sel is None else 2
        self.xs = (c.QT[:, 0:HALF], c.QT[:, HALF:S], c.KT[:, 0:HALF])
        self.tops = (c.QB[:, 0:HALF], c.QB[:, HALF:S])
        self.steps = [("part", t) for t in range(self.PARTS)]
        self.steps += [("flush", self.PARTS), ("values", 0), ("flush", self.PARTS + 1), ("values", 1)]

    def wait_pieces(self, engine, upto):
        of_q = sum(self.item(T)[2] == 0 for T in range(upto))
        if of_q:
            engine.wait_ge(self.q_done, of_q)
        if upto > of_q:
            engine.wait_ge(self.k_done, upto - of_q)

    def item(self, T):
        n = T % self.PARTS // 2
        return n, n // 2, n % 2, slice(T % 2 * HALF, (T % 2 + 1) * HALF)

    def bank(self, T):
        return (2 + 2 * (T % 2 if self.alone else 0)) if self.turned else 2 + T % 2

    def load(self, sp, pair):
        c = self.c
        sp.dma_start(c.W[:, 0:self.slots, :], one(self.w, pair)).then_inc(self.w_loaded, 16)
        if self.sel is not None:
            sp.dma_start(c.SEL[0:self.sel_rows, :, :], one(self.sel, pair)).then_inc(self.w_loaded, 16)

    def tensor(self, pe, s, kind, t, loaded):
        c, T = self.c, self.PARTS * s + t
        if kind == "part":
            n, h, side, cols = self.item(T)
            if t == 0:
                if loaded:
                    pe.wait_ge(self.w_loaded, 16 * loaded)
                if s:
                    pe.wait_ge(self.v_out, 2 * s)
            elif self.turned and not (self.alone and t == 1):
                before = T - int(self.alone)
                pe.wait_ge(self.turn_one, before)
                pe.wait_ge(self.turn_two, before)
            if not self.turned and t >= 2:
                pe.wait_ge(self.rest_done, T - 1)
            for x in range(self.per_item):
                mm = pe.matmul(c.PS[:, self.bank(T) + x, :], c.W[:, self.per_item * n + x, :], c.XT[:, cols],
                               start=True, stop=True)
            mm.then_inc(self.projected, 1)
            if self.xpos is not None:
                pe.wait_ge(self.sel_cast, s + 1)
                if T:
                    pe.wait_ge(self.turn_sum, T)
                pe.matmul(c.PS[:, 1, :], c.selb[0:self.sel_rows, n, :], c.gatesT[0:self.sel_rows, cols],
                          start=True, stop=True).then_inc(self.norm_rows, 1)
        elif kind == "values":
            last = self.PARTS * (s + 1)
            pe.wait_ge(self.turn_sum if self.turned else self.rest_done, last)
            for x in range(4):
                mm = pe.matmul(c.PS[:, 2 + t, x * P:(x + 1) * P], c.XT[:, (4 * t + x) * P:(4 * t + x + 1) * P],
                               c.W[:, self.slots - 1, :], start=True, stop=True)
            mm.then_inc(self.v_ready, 1)

    def scalar(self, act, s, kind, t):
        c, T, last = self.c, self.PARTS * s + t, self.PARTS * (s + 1)
        q_pieces, k_pieces = self.sets[s][0:2]
        if kind == "part":
            n, h, side, cols = self.item(T)
            act.wait_ge(self.turn_sum if self.turned else self.projected, T + 1)
            source = self.xs[T % 3] if self.turned else c.PS[:, self.bank(T), :]
            if side == 0:
                if T >= 2:
                    act.wait_ge(self.rest_done, T - 1)
                act.activation(self.tops[T % 2], source, ACT.Copy, scale=c.coef64[:, 0:1]).then_inc(self.top_done, 1)
            else:
                act.activation(k_pieces[0][:, h, cols], source, ACT.Copy).then_inc(self.top_done, 1)
        if kind == "part" or (kind == "flush" and T == last):
            if t:
                R = T - 1
                n, h, side, cols = self.item(R)
                act.wait_ge(self.rest_done, R + 1)
                dst = q_pieces[0] if side == 0 else k_pieces[1]
                act.activation(dst[:, h, cols], self.xs[R % 3], ACT.Copy).then_inc(self.piece2_done, 1)
        if kind == "values":
            act.wait_ge(self.v_ready, 2 * s + t + 1)
            act.activation(self.values(s)[:, 4 * t:4 * t + 4].rearrange("p t (h w) -> p t h w", h=2)[:, :, :, 0:64],
                           c.PS[:, 2 + t, :].rearrange("p (t h w) -> p t h w", h=2, w=64), ACT.Copy
                           ).then_inc(self.v_out, 1)

    def values(self, s):
        at = 130 * self.sets[s][2]
        return self.c.VA[:, :, at:at + 130]

    def vector(self, dve, s, kind, t, loaded):
        c, T = self.c, self.PARTS * s + t
        q_pieces, k_pieces = self.sets[s][0:2]
        first, last = self.PARTS * s, self.PARTS * (s + 1)

        def rest(R):
            if not first <= R < last:
                return
            n, h, side, cols = self.item(R)
            x = self.xs[R % 3]
            source = x if self.turned else c.PS[:, self.bank(R), :]
            dve.wait_ge(self.top_done, R + 1)
            if not self.turned and R >= 3:
                self.wait_pieces(dve, R - 2)
            if side == 0:
                dve.tensor_tensor(x, source, self.tops[R % 2], ALU.subtract).then_inc(self.rest_done, 1)
            else:
                dve.scalar_tensor_tensor(x, k_pieces[0][:, h, cols], c.coef64[:, 2:3], source,
                                         ALU.mult, ALU.add).then_inc(self.rest_done, 1)

        if kind == "part" and t == 0 and self.sel is not None:
            if loaded:
                dve.wait_ge(self.w_loaded, 16 * loaded)
            if s:
                dve.wait_ge(self.norm_rows, first)
            dve.tensor_copy(c.selb[0:self.sel_rows, :, :], c.SEL[0:self.sel_rows, :, :]).then_inc(self.sel_cast, 1)
        if kind == "part" and self.turned:
            n, h, side, cols = self.item(T)
            x, straight, across = self.xs[T % 3], c.PS[:, self.bank(T), :], c.PS[:, self.bank(T) + 1, :]
            dve.wait_ge(self.projected, T + 1)
            if T >= 3:
                self.wait_pieces(dve, T - 2)
            if self.xpos is None:
                dve.tensor_tensor(x, straight, self.rope[:, 0, cols], ALU.mult).then_inc(self.turn_one, 1)
                if T:
                    dve.wait_ge(self.turn_sum, T)
                dve.tensor_tensor(c.T1[:, 0:HALF], across, self.rope[:, 1, cols], ALU.mult).then_inc(self.turn_two, 1)
                rest(T - 1)
                dve.wait_ge(self.turn_one, T + 1)
                dve.wait_ge(self.turn_two, T + 1)
                dve.tensor_tensor(x, x, c.T1[:, 0:HALF], ALU.add).then_inc(self.turn_sum, 1)
            else:
                dve.scalar_tensor_tensor(x, straight, c.gcols[:, 2 * side:2 * side + 1], self.xpos[:, 2 * side, cols],
                                         ALU.mult, ALU.mult).then_inc(self.turn_one, 1)
                if T:
                    dve.wait_ge(self.turn_done, T)
                dve.scalar_tensor_tensor(c.T1[:, 0:HALF], across, c.gcols[:, 2 * side + 1:2 * side + 2],
                                         self.xpos[:, 2 * side + 1, cols], ALU.mult, ALU.mult
                                         ).then_inc(self.turn_two, 1)
                rest(T - 1)
                dve.wait_ge(self.turn_one, T + 1)
                dve.wait_ge(self.turn_two, T + 1)
                dve.tensor_tensor(x, x, c.T1[:, 0:HALF], ALU.add).then_inc(self.turn_done, 1)
                dve.wait_ge(self.turn_done, T + 1)
                dve.wait_ge(self.norm_rows, T + 1)
                dve.tensor_tensor(x, x, c.PS[:, 1, :], ALU.mult).then_inc(self.turn_sum, 1)
        elif kind == "part" or kind == "flush":
            rest(T - 1)
        if (kind == "part" or kind == "flush") and first <= T - 2 < last and self.item(T - 2)[2] == 0:
            n, h, side, cols = self.item(T - 2)
            dve.wait_ge(self.piece2_done, T - 1)
            dve.scalar_tensor_tensor(q_pieces[1][:, h, cols], q_pieces[0][:, h, cols], c.coef64[:, 1:2],
                                     self.xs[(T - 2) % 3], ALU.mult, ALU.add).then_inc(self.q_done, 1)

    def gpsimd(self, pool, s, kind, t):
        R, k_pieces = self.PARTS * s + t - 2, self.sets[s][1]
        if kind in ("part", "flush") and self.PARTS * s <= R < self.PARTS * (s + 1):
            n, h, side, cols = self.item(R)
            if side == 1:
                pool.wait_ge(self.piece2_done, R + 1)
                pool.tensor_tensor(k_pieces[2][:, h, cols], self.xs[R % 3], k_pieces[1][:, h, cols],
                                   ALU.subtract).then_inc(self.k_done, 1)


class PairMaxima:

    def __init__(self, c, heads, units, sets):
        self.c, self.heads, self.units, self.sets = c, heads, units, sets
        self.banks = 1 if heads.mode == "window" else 2
        self.uses = uses = []
        for x, (u, p, half, h) in enumerate(units):
            for j in range(QPH):
                lo, hi = heads.sees(half * QPH + j)
                if heads.mode != "window":
                    uses += [(x, j, k, min(QPH, hi - k), (k - lo) // QPH) for k in range(lo, hi, QPH)]
                elif j % 2 == 0:
                    uses.append((x, j, None, None, 0))
            uses.append((x, None, None, None, None))
        self.last = [max(i for i, use in enumerate(uses) if use[0] == x) for x in range(len(units))]
        self.chunks = [max(use[4] or 0 for use in uses if use[0] == x) + 1 for x in range(len(units))]

    def of(self, x):
        return list(range(self.last[x - 1] + 1 if x else 0, self.last[x]))

    def scores(self, pe, i, rows_ready, rows_read):
        c, heads = self.c, self.heads
        x, j, k, count, _ = self.uses[i]
        u, p, half, h = self.units[x]
        q_pieces, k_pieces = self.sets[p][0:2]
        q = half * QPH + j
        if i >= self.banks:
            pe.wait_ge(rows_read, i + 1 - self.banks)
        if heads.mode == "window":
            for n, tile in enumerate((q, q + 1)):
                for m, k in enumerate((max(tile - 1, 0), tile)):
                    out = c.PS[:, i % self.banks, (2 * n + m) * P:(2 * n + m + 1) * P]
                    pe.matmul(out, q_pieces[0][:, h, tile * P:(tile + 1) * P],
                              k_pieces[0][:, h, k * P:(k + 1) * P], start=True, stop=False)
                    mm = pe.matmul(out, c.identb[:, :], c.masks[:, heads.mask(tile, k, False), :],
                                   start=False, stop=True)
            mm.then_inc(rows_ready, 1)
            return
        done = 0
        while done < count:
            masked = heads.mask(q, k + done, False)
            n = 1
            while masked is None and done + n < count and heads.mask(q, k + done + n, False) is None:
                n += 1
            out = c.PS[:, i % self.banks, done * P:(done + n) * P]
            mm = pe.matmul(out, q_pieces[0][:, h, q * P:(q + 1) * P],
                           k_pieces[0][:, h, (k + done) * P:(k + done + n) * P], start=True, stop=masked is None)
            if masked is not None:
                mm = pe.matmul(out, c.identb[:, :], c.masks[:, masked, :], start=False, stop=True)
            done += n
        mm.then_inc(rows_ready, 1)

    def turn(self, pe, x, rows_ready, maxima_done):
        c, i, u = self.c, self.last[x], self.units[x][0]
        pe.wait_ge(maxima_done, x + 1)
        for j in range(QPH):
            mm = pe.matmul(c.PS[0:1, i % self.banks, j * P:(j + 1) * P], c.negmax[:, u % 2, j:j + 1], c.identb[:, :],
                           start=True, stop=True)
        mm.then_inc(rows_ready, 1)

    def reduce(self, dve, i, rows_ready, rows_read):
        c = self.c
        x, j, _, count, chunk = self.uses[i]
        dve.wait_ge(rows_ready, i + 1)
        if self.heads.mode == "window":
            dve.tensor_reduce(c.rowmax[:, self.units[x][0] % 2, 0, j:j + 2, 0], c.PS[:, i % self.banks, :].rearrange(
                "p (j k) -> p j k", j=2), AX_X, ALU.max).then_inc(rows_read, 1)
            return
        dve.tensor_reduce(c.rowmax[:, self.units[x][0] % 2, 0, j, chunk:chunk + 1], c.PS[:, i % self.banks, 0:count * P],
                          AX_X, ALU.max).then_inc(rows_read, 1)

    def combine(self, dve, x, rows_read, maxima_done):
        c, u = self.c, self.units[x][0]
        dve.wait_ge(rows_read, self.last[x])
        dve.tensor_reduce(c.negmax[:, u % 2, :], c.rowmax[:, u % 2, 0, :, 0:self.chunks[x]], AX_X, ALU.max,
                          negate=True).then_inc(maxima_done, 1)

    def keep_row(self, dve, x, rows_ready, rows_read):
        c, i, u = self.c, self.last[x], self.units[x][0]
        dve.wait_ge(rows_ready, i + 1)
        dve.tensor_copy(c.negmax_row[0:1, u % 2, :], c.PS[0:1, i % self.banks, :]).then_inc(rows_read, 1)


def pair_sets(c, order):
    second = c.HT[:, :, :].rearrange("p a s -> p (a s)").bitcast(BF16).rearrange("p (x s) -> p x s", s=S)
    second_k3 = c.small[:, :, :, :].rearrange("p a t e -> p (a t e)").bitcast(BF16)[:, 0:2 * S].rearrange(
        "p (x s) -> p x s", s=S)
    both = (((c.QS[:, 0:2, :], c.QS[:, 2:4, :]), (c.KS[:, 0:2, :], c.KS[:, 2:4, :], c.K3), 0),
            ((second[:, 0:2], second[:, 2:4]), (second[:, 4:6], second[:, 6:8], second_k3), 1))
    return [both[n] for n in order]


def first_pair(c, heads, w, rope, xpos, sel):
    maxima = PairMaxima(c, heads, [(0, 0, 0, 0)], pair_sets(c, (0,)))
    with c.stage("ones_set", "rows_ready", "rows_read", "maxima_done", *PairPrep.SEMS) as \
            (block, ones_set, rows_ready, rows_read, maxima_done, *prep_sems):
        prep = PairPrep(c, w, pair_sets(c, (0,)), rope, xpos, sel, prep_sems, alone=True)

        @block.sync
        def _(sp):
            prep.load(sp, 0)
            sp.wait_ge(prep.v_ready, 2)
            if sel is not None:
                sp.wait_ge(prep.sel_cast, 1)
            prep.load(sp, 1)
            sp.wait_ge(prep.w_loaded, 2 * 16 * prep.loads)

        @block.tensor
        def _(pe):
            for kind, t in prep.steps:
                prep.tensor(pe, 0, kind, t, prep.loads)
            prep.wait_pieces(pe, prep.PARTS)
            for i in maxima.of(0):
                maxima.scores(pe, i, rows_ready, rows_read)
            maxima.turn(pe, 0, rows_ready, maxima_done)

        @block.scalar
        def _(act):
            for kind, t in prep.steps:
                if kind == "values":
                    act.wait_ge(ones_set, 1)
                prep.scalar(act, 0, kind, t)

        @block.gpsimd
        def _(pool):
            for kind, t in prep.steps:
                prep.gpsimd(pool, 0, kind, t)

        @block.vector
        def _(dve):
            dve.memset(c.VA[:, :, :], 1.0).then_inc(ones_set, 1)
            for kind, t in prep.steps:
                prep.vector(dve, 0, kind, t, prep.loads)
            for i in maxima.of(0):
                maxima.reduce(dve, i, rows_ready, rows_read)
            maxima.combine(dve, 0, rows_read, maxima_done)
            maxima.keep_row(dve, 0, rows_ready, rows_read)


def attend_pairs(c, heads, start, n, more, w, rope=None, xpos=None, sel=None, target=None, wo=None):
    units = [(p, half, h) for p in range(n) for half in range(NH) for h in range(2)]
    U = len(units)
    n_prepared = n if more else n - 1
    rows_mode = target is None
    sets = pair_sets(c, [p % 2 for p in range(n + 1)])
    maxima = PairMaxima(c, heads, [(u, *units[u]) for u in range(1, U)] + [(U, n, 0, 0)] * more, sets)
    work = []
    for u, (p, half, h) in enumerate(units):
        for k in range(heads.key_tiles):
            cols = [j for j in range(QPH) if heads.sees(half * QPH + j)[0] <= k < heads.sees(half * QPH + j)[1]]
            if cols:
                work.append((u, k, cols[0], cols[-1] + 1))
    first = [min(i for i, x in enumerate(work) if x[0] == u) for u in range(U)] + [len(work)]
    PER_ROW = 1024 // 64
    row_w = c.wrows
    by_place = c.CT[:, :].rearrange("p (m r) -> p r m", m=PER_ROW)

    with c.stage("rows_ready", "rows_read", "maxima_done", "scores_ready", "probs_ready", "pv_done",
                 "rden_done", "out_done", "ctx_turned", "ctx_out", "y_ready", "y_added", "wo_loaded",
                 *PairPrep.SEMS) as \
            (block, rows_ready, rows_read, maxima_done, scores_ready, probs_ready, pv_done,
             rden_done, out_done, ctx_turned, ctx_out, y_ready, y_added, wo_loaded, *prep_sems):
        prep = PairPrep(c, w, sets[1:], rope, xpos, sel, prep_sems)

        order = []
        reduced = 0

        def take_rows(upto):
            nonlocal reduced
            while reduced < upto:
                if maxima.uses[reduced][1] is not None:
                    order.append(("reduce", reduced))
                reduced += 1

        for u in range(U):
            count = first[u + 1] - first[u]
            if u % 4 == 0:
                pair, prep_place, projected, turned, shortened = u // 4, 0, 0, 0, 0
                steps = prep.steps if pair < n_prepared else []
                prep_places = 2 * (first[u + 3] - first[u]) + first[u + 4] - first[u + 3]
            rows, found, row_place = maxima.of(u) if u + 1 < U or more else [], 0, 0
            row_start = count if u % 4 == 3 else 0
            row_places = max(2 * count - row_start - 3, 2)
            for step in range(first[u], first[u + 1]):
                at = step - first[u]
                order.append(("scores", step))
                for place in range(2):
                    if rows:
                        take_rows(rows[0] + found)
                    if rows and 2 * at + place >= row_start:
                        row_place += 1
                        if row_place <= row_places:
                            while found < row_place * len(rows) // row_places:
                                take_rows(rows[found] + 1 - maxima.banks)
                                order.append(("row_scores", rows[found]))
                                found += 1
                            if row_place == row_places:
                                take_rows(rows[-1] + 1)
                                order.append(("combine", u))
                        if row_place == row_places + 2:
                            order.append(("turn_maxima", u))
                    while turned < projected:
                        order.append(("turn", (pair, *steps[turned])))
                        turned += 1
                    if place == 0 and step > first[u]:
                        order.append(("weighted", step - 1))
                    prep_place += 1
                    while prep_place <= prep_places and projected < prep_place * len(steps) // prep_places:
                        while turned < projected:
                            order.append(("turn", (pair, *steps[turned])))
                            turned += 1
                        while shortened < turned:
                            order.append(("shorten", (pair, *steps[shortened])))
                            shortened += 1
                        order.append(("project", (pair, *steps[projected])))
                        projected += 1
                    if prep_place == prep_places:
                        for kind, upto in (("turn", turned), ("shorten", shortened)):
                            order += [(kind, (pair, *step)) for step in steps[upto:]]
                        turned = shortened = len(steps)
                if u >= 2 and u % 2 == 0 and at == 1:
                    order.append(("turn_context", u // 2 - 1))
                if u >= 2 and u % 2 == 0 and at == 2:
                    order.append(("project_context", u // 2 - 1))
                if u >= 2 and u % 2 == 0 and at == 3:
                    order.append(("add_out", u // 2 - 1))
            order.append(("weighted", first[u + 1] - 1))
            order.append(("divide", u))
        order += [("turn_context", U // 2 - 1), ("project_context", U // 2 - 1), ("add_out", U // 2 - 1)]

        @block.sync
        def _(sp):
            if not rows_mode:
                for p in range(n):
                    sp.dma_start(c.W1E[:, p, :], one(wo, start + p)).then_inc(wo_loaded, 16)
            n_loads = n if more else n - 2
            for s in range(n_loads):
                sp.wait_ge(prep.v_ready, 2 * (s + 1))
                if sel is not None:
                    sp.wait_ge(prep.sel_cast, s + 1)
                prep.load(sp, start + 2 + s)
            sp.wait_ge(prep.w_loaded, 16 * prep.loads * n_loads)

        @block.tensor
        def _(pe):
            def scores(n):
                u, k, lo, hi = work[n]
                p, half, h = units[u]
                q_pieces, k_pieces = sets[p][0:2]
                if n >= 2:
                    pe.wait_ge(probs_ready, n - 1)
                if n == first[u] and u:
                    pe.wait_ge(rows_read, maxima.last[u - 1] + 1)
                out = c.PS[:, 4 + n % 2, lo * P:hi * P]
                q0 = half * HALF
                for i, (qp, kp) in enumerate(((0, 0), (1, 1), (0, 2))):
                    pe.matmul(out, k_pieces[kp][:, h, k * P:(k + 1) * P],
                              q_pieces[qp][:, h, q0 + lo * P:q0 + hi * P], start=i == 0, stop=False)
                for j in range(lo, hi):
                    masked = heads.mask(half * QPH + j, k, True)
                    if masked is not None:
                        pe.matmul(c.PS[:, 4 + n % 2, j * P:(j + 1) * P], c.identb[:, :], c.masks[:, masked, :],
                                  start=False, stop=False)
                mm = pe.matmul(out, c.first[:, 2, :], c.negmax_row[:, u % 2, lo * P:hi * P], start=False, stop=True)
                mm.then_inc(scores_ready, 1)

            def weighted(n):
                u, k, lo, hi = work[n]
                p, half, h = units[u]
                pe.wait_ge(probs_ready, n + 1)
                if n == first[u] and u >= 1:
                    pe.wait_ge(out_done, u)
                at = 130 * (p % 2) + 65 * h
                v = c.VA[:, k, at:at + 65]
                for j in range(lo, hi):
                    mm = pe.matmul(c.PS[:, 6, j * 65:(j + 1) * 65], c.probs[:, n % 3, j * P:(j + 1) * P], v,
                                   start=n == first[u] and j == lo,
                                   stop=k + 1 == heads.sees(half * QPH + j)[1], skip_group_check=True)
                mm.then_inc(pv_done, 1)

            def turn_context(e):
                pe.wait_ge(out_done, 2 * (e + 1))
                if e:
                    pe.wait_ge(y_added, e)
                for j in range(QPH):
                    mm = pe.transpose(c.PS[:, 7, j * P:(j + 1) * P], c.CTX[:, e % 2 * QPH + j, :], c.ident[:, :])
                mm.then_inc(ctx_turned, 1)

            def project_context(e):
                p, half = e // 2, e % 2
                pe.wait_ge(ctx_out, e + 1)
                if rows_mode:
                    n = 32
                    for h in range(2):
                        on = slice(64 * h, 64 * h + 64)
                        at = 64 * h + n * half
                        for m in range(PER_ROW):
                            mm = pe.matmul(c.PS[at:at + n, 7, 0:P], c.CT[on, 64 * m + n * half:64 * m + n * half + n],
                                           row_w[on, m, :], start=m == 0, stop=m == PER_ROW - 1)
                    mm.then_inc(y_ready, 1)
                    return
                pe.wait_ge(wo_loaded, 16 * len(units) // 4)
                for j in range(QPH):
                    t = half * QPH + j
                    mm = pe.matmul(c.PS[:, 7, j * P:(j + 1) * P], c.CT[:, t * P:(t + 1) * P], c.W1E[:, p, :],
                                   start=True, stop=True)
                mm.then_inc(y_ready, 1)

            for kind, x in order:
                if kind == "scores":
                    scores(x)
                elif kind == "row_scores":
                    for p in range(n_prepared):
                        if x == maxima.of(4 * p + 3)[0]:
                            prep.wait_pieces(pe, (p + 1) * prep.PARTS)
                    maxima.scores(pe, x, rows_ready, rows_read)
                elif kind == "turn_maxima":
                    maxima.turn(pe, x, rows_ready, maxima_done)
                elif kind == "weighted":
                    u = work[x][0]
                    if x == first[u] and u % 4 == 0 and u:
                        pe.wait_ge(prep.v_out, 2 * (u // 4))
                    weighted(x)
                elif kind == "project":
                    prep.tensor(pe, *x, prep.loads * x[0])
                elif kind == "turn_context":
                    turn_context(x)
                elif kind == "project_context":
                    project_context(x)

        @block.scalar
        def _(act):
            def probs(n):
                u, k, lo, hi = work[n]
                act.wait_ge(scores_ready, n + 1)
                if n >= 3:
                    act.wait_ge(pv_done, n - 2)
                act.activation(c.probs[:, n % 3, lo * P:hi * P], c.PS[:, 4 + n % 2, lo * P:hi * P], ACT.Exp,
                               scale=heads.scale).then_inc(probs_ready, 1)

            def context_out(e):
                half = e % 2
                act.wait_ge(ctx_turned, e + 1)
                if e >= 2:
                    act.wait_ge(y_ready, e - 1)
                if rows_mode:
                    act.activation(by_place[:, 32 * half:32 * half + 32, :],
                                   c.PS[:, 7, :].rearrange("p (r m) -> p r m", m=PER_ROW), ACT.Copy).then_inc(ctx_out, 1)
                else:
                    act.activation(c.CT[:, half * HALF:(half + 1) * HALF], c.PS[:, 7, :], ACT.Copy).then_inc(ctx_out, 1)

            for kind, x in order:
                if kind == "scores":
                    probs(x)
                elif kind == "shorten":
                    if x[1:] == ("values", 0) and x[0]:
                        act.wait_ge(pv_done, first[4 * x[0]])
                    prep.scalar(act, *x)
                elif kind == "turn_context":
                    context_out(x)

        @block.gpsimd
        def _(pool):
            for kind, x in order:
                if kind == "turn":
                    prep.gpsimd(pool, *x)

        @block.vector
        def _(dve):
            def divide(u):
                p, half, h = units[u]
                dve.wait_ge(pv_done, first[u + 1])
                if u:
                    dve.wait_ge(out_done, u)
                if u >= 4:
                    dve.wait_ge(ctx_turned, u // 2 - 1)
                o = c.PS[:, 6, 0:QPH * 65].rearrange("p (q w) -> p q w", w=65)
                dve.reciprocal(c.rden[:, :, :], o[:, :, 64:65]).then_inc(rden_done, 1)
                dve.wait_ge(rden_done, u + 1)
                dve.tensor_tensor(c.CTX[:, half * QPH:(half + 1) * QPH, 64 * h:64 * h + 64], o[:, :, 0:64],
                                  c.rden[:, :, :].to_broadcast([P, QPH, 64]), ALU.mult).then_inc(out_done, 1)

            def add_out(e):
                p, half = e // 2, e % 2
                dve.wait_ge(y_ready, e + 1)
                if rows_mode:
                    for h in range(2):
                        at = 64 * h + 32 * half
                        tile = c.X[at:at + 32, bass.ds(start + p, 1), :].rearrange("p z d -> p (z d)")
                        ins = dve.tensor_tensor(tile, tile, c.PS[at:at + 32, 7, 0:P], ALU.add)
                    ins.then_inc(y_added, 1)
                    return
                if e >= 2:
                    dve.wait_ge(y_added, e - 1)
                part = target[:, half * QPH:(half + 1) * QPH, :]
                dve.tensor_tensor(part, part, c.PS[:, 7, :].rearrange("p (t d) -> p t d", d=P), ALU.add
                                  ).then_inc(y_added, 1)

            for kind, x in order:
                if kind == "reduce":
                    maxima.reduce(dve, x, rows_ready, rows_read)
                elif kind == "combine":
                    maxima.combine(dve, x, rows_read, maxima_done)
                elif kind == "turn_maxima":
                    maxima.keep_row(dve, x, rows_ready, rows_read)
                elif kind == "turn":
                    prep.vector(dve, *x, prep.loads * x[0])
                elif kind == "divide":
                    divide(x)
                elif kind == "add_out":
                    add_out(x)


def attention64(c, target, w, wo, n_pairs, mode, scale, rope=None, xpos=None, sel=None):
    heads = Heads(64, 2, 64, scale, mode)
    first_pair(c, heads, w, rope, xpos, sel)
    if n_pairs <= 4:
        attend_pairs(c, heads, 0, n_pairs, False, w, rope=rope, xpos=xpos, sel=sel, target=target, wo=wo)
        return
    with c.nc.Fori(0, n_pairs // 4) as four:
        attend_pairs(c, heads, 4 * four, 4, True, w, rope=rope, xpos=xpos, sel=sel, target=target, wo=wo)


def attention8(c, w, bias, mode, rope=None):
    heads = Heads(8, 4, 32, 8.0 ** -0.5, mode)
    project8(c, w, bias, rope)
    first_maxima(c, heads)
    with c.nc.Fori(0, 2) as two:
        attend_two_groups(c, heads, two)


def q_k_sets(c):
    second = c.HT[:, :, :].rearrange("p a s -> p (a s)").bitcast(BF16).rearrange("p (x j s) -> p x j s", x=2, j=4)
    return (c.QS, c.KS), (second[:, 0], second[:, 1])


def load_group(c, sp, place, head, loaded):
    q_rows, k_rows = place
    for a in range(3):
        q_piece = c.dram["q_pieces"][a][bass.ds(head, 4)].rearrange("j d s -> d j s")
        for n in range(3):
            at = 24 * a + 8 * n
            sp.dma_start(q_rows[at:at + 8, :, :], q_piece).then_inc(loaded, 16)
        k_pieces = c.dram["k_pieces"][bass.ds(head, 4)].rearrange("j c d s -> (c d) j s")
        sp.dma_start(k_rows[24 * a:24 * a + 24, :, :], k_pieces).then_inc(loaded, 16)
    return 12


def project8(c, w, bias, rope):
    turned = rope is not None
    per_side = 2 if turned else 1
    slots = 2 * per_side + 1
    v_bank = 0 if turned else 4
    (q_rows, k_rows), (q_rows2, k_rows2) = q_k_sets(c)
    pieces = c.probs8[:, 0:2, :, :].rearrange("p a h s -> p (a h s)").bitcast(BF16).rearrange(
        "p (x n s) -> p x n s", x=2, n=4)
    with c.stage("w_loaded", "b_loaded", "projected", "turn_one", "turn_two", "whole", "top_done", "rest_done",
                 "mid_done", "pieces_done", "v_out", "stored", "cleared", "cleared2", "ones_set", "first_loaded") as \
            (block, w_loaded, b_loaded, projected, turn_one, turn_two, whole, top_done, rest_done, mid_done,
             pieces_done, v_out, stored, cleared, cleared2, ones_set, first_loaded):
        sides = (c.QT, c.KT)

        @block.sync
        def _(sp):
            if w is not None:
                sp.dma_start(c.W[:, 0:slots, :], w).then_inc(w_loaded, 16)
            if bias is not None:
                sp.dma_start(c.bcols[:, 0:slots - 1], bias[0]).then_inc(b_loaded, 16)
                sp.dma_start(c.vbias[:, :], bias[1].partition_broadcast(P)).then_inc(b_loaded, 16)
            for side in range(2):
                for n in range(3):
                    if n == 0:
                        sp.wait_ge(top_done, side + 1)
                    if n == 1:
                        sp.wait_ge(mid_done, side + 1)
                    if n == 2:
                        sp.wait_ge(pieces_done, side + 1)
                    dst = c.dram["k_pieces"][:, n] if side else c.dram["q_pieces"][n]
                    sp.dma_start(dst, pieces[:, side, n, :]).then_inc(stored, 16)
            sp.wait_ge(stored, 6 * 16)
            sp.wait_ge(cleared, 2)
            n = load_group(c, sp, (q_rows, k_rows), 0, first_loaded)
            sp.wait_ge(first_loaded, 16 * n)

        @block.tensor
        def _(pe):
            if w is not None:
                pe.wait_ge(w_loaded, 16)
            for s in range(slots - 1):
                for h in range(NH):
                    mm = pe.matmul(c.PS[:, 2 * s + h, :], c.W[:, s, :], c.XT[:, h * HALF:(h + 1) * HALF],
                                   start=True, stop=True)
                mm.then_inc(projected, 1)
            if turned:
                pe.wait_ge(turn_one, 1)
            for t in range(NT):
                mm = pe.matmul(c.tiles(v_bank)[:, t, :], c.XT[:, t * P:(t + 1) * P], c.W[:, slots - 1, :],
                               start=True, stop=True)
            mm.then_inc(projected, 1)

        @block.vector
        def _(dve):
            dve.memset(c.VA[:, :, 0:168], 1.0).then_inc(ones_set, 1)
            dve.memset(q_rows[64:P, :, :], 0.0).then_inc(cleared, 1)
            dve.memset(k_rows[64:P, :, :], 0.0).then_inc(cleared, 1)
            if bias is not None:
                dve.wait_ge(b_loaded, 32)
            for side in range(2):
                out = sides[side][:, :]
                dve.wait_ge(projected, per_side * (side + 1))
                straight = c.banks(2 * per_side * side)
                if turned:
                    across = c.banks(2 * per_side * side + 2)
                    dve.scalar_tensor_tensor(out, straight, c.bcols[:, 2 * side:2 * side + 1], rope[:, 0, :],
                                             ALU.add, ALU.mult).then_inc(turn_one, 1)
                    if side:
                        dve.wait_ge(whole, side)
                    dve.scalar_tensor_tensor(c.T1[:, :], across, c.bcols[:, 2 * side + 1:2 * side + 2],
                                             rope[:, 1, :], ALU.add, ALU.mult).then_inc(turn_two, 1)
                    dve.wait_ge(turn_one, side + 1)
                    dve.wait_ge(turn_two, side + 1)
                    dve.tensor_tensor(out, out, c.T1[:, :], ALU.add).then_inc(whole, 1)
                elif bias is not None:
                    dve.tensor_scalar(out, straight, c.bcols[:, side:side + 1], None, ALU.add).then_inc(whole, 1)
                else:
                    dve.tensor_copy(out, straight).then_inc(whole, 1)
            for side in range(2):
                out = sides[side][:, :]
                dve.wait_ge(top_done, side + 1)
                dve.tensor_tensor(out, out, pieces[:, side, 0, :], ALU.subtract).then_inc(rest_done, 1)
                dve.wait_ge(mid_done, side + 1)
                dve.tensor_tensor(pieces[:, side, 2, :], out, pieces[:, side, 1, :], ALU.subtract
                                  ).then_inc(pieces_done, 1)
            dve.wait_ge(projected, slots)
            dve.wait_ge(ones_set, 1)
            v = c.VA[:, :, 0:144].rearrange("p t (h w) -> p t h w", w=9)[:, :, :, 0:8]
            for t in range(NT):
                v_from = c.tiles(v_bank)[:, t, :].rearrange("p (h e) -> p h e", e=8)
                if bias is None:
                    dve.tensor_copy(v[:, t], v_from).then_inc(v_out, 1)
                else:
                    dve.tensor_tensor(v[:, t], v_from, c.vbias[:, :].rearrange("p (h e) -> p h e", e=8), ALU.add
                                      ).then_inc(v_out, 1)

        @block.scalar
        def _(act):
            for rows in (q_rows2, k_rows2):
                act.activation(rows[64:P, :, :].rearrange("p j (h s) -> p (j h) s", h=NH),
                               c.ones[64:P, None, :].to_broadcast([64, 4 * NH, HALF]), ACT.Copy, scale=0.0
                               ).then_inc(cleared2, 1)
            for side in range(2):
                out = sides[side][:, :]
                act.wait_ge(whole, side + 1)
                act.activation(pieces[:, side, 0, :], out, ACT.Copy).then_inc(top_done, 1)
            for side in range(2):
                out = sides[side][:, :]
                act.wait_ge(rest_done, side + 1)
                act.activation(pieces[:, side, 1, :], out, ACT.Copy).then_inc(mid_done, 1)
            act.wait_ge(cleared, 2)
            act.wait_ge(cleared2, 2)
            for rows in (k_rows, k_rows2):
                act.activation(rows[96:100, :, :], c.onehot[96:100, :, None].to_broadcast([4, 4, S]), ACT.Copy
                               ).then_inc(cleared2, 1)


class RowMaxima:

    def __init__(self, c, heads, units, sets):
        self.c, self.heads, self.units, self.sets = c, heads, units, sets
        self.uses = uses = []
        for x, (u, gg, half) in enumerate(units):
            for h in range(4):
                for j in range(QPH):
                    lo, hi = heads.sees(half * QPH + j)
                    uses += [(x, h, j, k, min(QPH, hi - k)) for k in range(lo, hi, QPH)]
            uses.append((x, None, None, None, None))
        self.last = [max(i for i, use in enumerate(uses) if use[0] == x) for x in range(len(units))]
        self.chunks = [max(use[3] or 0 for use in uses if use[0] == x) // QPH + 1 for x in range(len(units))]

    def of(self, x):
        return list(range(self.last[x - 1] + 1 if x else 0, self.last[x]))

    def scores(self, pe, i, rows_ready, rows_read):
        c, heads = self.c, self.heads
        x, h, j, k, n = self.uses[i]
        u, gg, half = self.units[x]
        q_rows, k_rows = self.sets[gg]
        q = half * QPH + j
        if i >= 2:
            pe.wait_ge(rows_read, i - 1)
        bank = 6 + i % 2
        plain = n - 1 if heads.mask(q, k + n - 1, False) is not None else n
        if plain:
            mm = pe.matmul(c.PS[:, bank, 0:plain * P], q_rows[0:ROWS, h, q * P:(q + 1) * P],
                           k_rows[0:ROWS, h, k * P:(k + plain) * P], start=True, stop=True)
        if plain < n:
            out = c.PS[:, bank, plain * P:n * P]
            pe.matmul(out, q_rows[0:ROWS, h, q * P:(q + 1) * P],
                      k_rows[0:ROWS, h, (k + plain) * P:(k + n) * P], start=True, stop=False)
            mm = pe.matmul(out, c.identb[:, :], c.masks[:, heads.mask(q, k + n - 1, False), :],
                           start=False, stop=True)
        mm.then_inc(rows_ready, 1)

    def turn(self, pe, x, rows_ready, maxima_done):
        c, i, u = self.c, self.last[x], self.units[x][0]
        pe.wait_ge(maxima_done, x + 1)
        for j in range(QPH):
            mm = pe.matmul(c.PS[ROWS:TOP, 6 + i % 2, j * P:(j + 1) * P], c.negmax8[:, u % 2, :, j],
                           c.identb[:, :], start=True, stop=True)
        mm.then_inc(rows_ready, 1)

    def reduce(self, dve, x, rows_ready, rows_read, maxima_done):
        c = self.c
        u, gg, half = self.units[x]
        for i in self.of(x):
            _, h, j, k, n = self.uses[i]
            dve.wait_ge(rows_ready, i + 1)
            dve.tensor_reduce(c.rowmax[:, u % 2, h, j, k // QPH:k // QPH + 1], c.PS[:, 6 + i % 2, 0:n * P],
                              AX_X, ALU.max).then_inc(rows_read, 1)
        i = self.last[x]
        dve.wait_ge(rows_read, i)
        dve.tensor_reduce(c.negmax8[:, u % 2, :, :], c.rowmax[:, u % 2, :, :, 0:self.chunks[x]], AX_X, ALU.max,
                          negate=True).then_inc(maxima_done, 1)
        dve.wait_ge(rows_ready, i + 1)
        dve.tensor_copy(self.sets[gg][0][ROWS:TOP, :, half * HALF:(half + 1) * HALF],
                        c.PS[ROWS:TOP, 6 + i % 2, :][:, None, :].to_broadcast([TOP - ROWS, 4, HALF])
                        ).then_inc(rows_read, 1)


def first_maxima(c, heads):
    maxima = RowMaxima(c, heads, [(0, 0, 0)], q_k_sets(c))
    with c.stage("rows_ready", "rows_read", "maxima_done") as (block, rows_ready, rows_read, maxima_done):
        @block.tensor
        def _(pe):
            for i in maxima.of(0):
                maxima.scores(pe, i, rows_ready, rows_read)
            maxima.turn(pe, 0, rows_ready, maxima_done)

        @block.vector
        def _(dve):
            maxima.reduce(dve, 0, rows_ready, rows_read, maxima_done)


def attend_two_groups(c, heads, two):
    sets = q_k_sets(c)
    units = [(0, 0), (0, 1), (1, 1), (1, 0)]
    U = len(units)
    maxima = RowMaxima(c, heads, [(u, *units[u]) for u in range(1, U)] + [(U, 0, 0)], sets)
    work = []
    for u, (gg, half) in enumerate(units):
        for k in range(heads.key_tiles):
            cols = [j for j in range(QPH) if heads.sees(half * QPH + j)[0] <= k < heads.sees(half * QPH + j)[1]]
            if cols:
                work.append((u, k, cols[0], cols[-1] + 1))
    first = [min(i for i, x in enumerate(work) if x[0] == u) for u in range(U)] + [len(work)]
    group_v = [b[:, 0:NT * 60].rearrange("p (t w) -> p t w", w=60) for b in (c.T1, c.T2)]

    with c.stage("second_loaded", "first_loaded", "v_copied", "rows_ready", "rows_read", "maxima_done",
                 "scores_ready", "probs_ready", "pv_done", "o_out", "o_turned", "rden_done", "out_done") as \
            (block, second_loaded, first_loaded, v_copied, rows_ready, rows_read, maxima_done,
             scores_ready, probs_ready, pv_done, o_out, o_turned, rden_done, out_done):

        @block.sync
        def _(sp):
            load_group(c, sp, sets[1], 8 * two + 4, second_loaded)
            sp.wait_ge(scores_ready, 2 * first[2])
            n = load_group(c, sp, sets[0], 8 - 8 * two, first_loaded)
            sp.wait_ge(first_loaded, 16 * n)

        @block.tensor
        def _(pe):
            def scores(n, pair):
                u, k, lo, hi = work[n]
                gg, half = units[u]
                q_rows, k_rows = sets[gg]
                m = 2 * n + pair
                if m >= 2:
                    pe.wait_ge(probs_ready, m - 1)
                if n == first[u] and pair == 0 and u:
                    pe.wait_ge(rows_read, maxima.last[u - 1] + 1)
                for hh in range(2):
                    h = 2 * pair + hh
                    bank = 2 * (m % 2) + hh
                    mm = pe.matmul(c.PS[:, bank, lo * P:hi * P], k_rows[0:TOP, h, k * P:(k + 1) * P],
                                   q_rows[0:TOP, h, half * HALF + lo * P:half * HALF + hi * P], start=True, stop=True)
                    for j in range(lo, hi):
                        masked = heads.mask(half * QPH + j, k, True)
                        if masked is not None:
                            mm = pe.matmul(c.PS[:, bank, j * P:(j + 1) * P], c.identb[:, :], c.masks[:, masked, :],
                                           start=False, stop=True, skip_group_check=True)
                mm.then_inc(scores_ready, 1)

            def weighted(n, pair):
                u, k, lo, hi = work[n]
                gg, half = units[u]
                pe.wait_ge(probs_ready, 2 * n + pair + 1)
                if n == 0 and pair == 0:
                    pe.wait_ge(v_copied, 2)
                if n == first[u] and pair == 0 and u >= 2:
                    pe.wait_ge(out_done, u - 1)
                for h in (2 * pair, 2 * pair + 1):
                    mm = pe.matmul(c.PS[32 * h:32 * h + 32, 4 + u % 2, lo * P:hi * P],
                                   group_v[gg][:, k, 9 * h:9 * h + 32],
                                   c.probs8[:, n % 3, h, lo * P:hi * P], start=n == first[u], stop=True,
                                   skip_group_check=True)
                if pair:
                    mm.then_inc(pv_done, 1)

            def turn_out(u):
                pe.wait_ge(o_out, u + 1)
                for j in range(QPH):
                    mm = pe.transpose(c.PS[:, 4 + u % 2, j * P:(j + 1) * P], c.out8[:, u % 2, j * P:(j + 1) * P],
                                      c.ident[:, :])
                mm.then_inc(o_turned, 1)

            for u in range(U):
                count = first[u + 1] - first[u]
                ahead = maxima.of(u)
                slots_left = 4 * count - 3
                turned = False

                def next_maxima():
                    nonlocal slots_left, turned
                    if ahead:
                        for _ in range(-(-len(ahead) // max(slots_left, 1))):
                            i = ahead.pop(0)
                            if u == 1 and i == maxima.of(1)[0]:
                                pe.wait_ge(second_loaded, 12 * 16)
                            if u == U - 1 and i == maxima.of(U - 1)[0]:
                                pe.wait_ge(first_loaded, 12 * 16)
                            maxima.scores(pe, i, rows_ready, rows_read)
                    elif not turned:
                        maxima.turn(pe, u, rows_ready, maxima_done)
                        turned = True
                    slots_left -= 1

                for n in range(first[u], first[u + 1]):
                    for pair in range(2):
                        scores(n, pair)
                        next_maxima()
                        if n > first[u]:
                            weighted(n - 1, pair)
                        next_maxima()
                    if u and n == first[u] + 1:
                        turn_out(u - 1)
                weighted(first[u + 1] - 1, 0)
                weighted(first[u + 1] - 1, 1)
            turn_out(U - 1)

        @block.scalar
        def _(act):
            for gg in range(2):
                v = c.VA[:, :, bass.ds(72 * two + 36 * gg, 60)]
                act.activation(group_v[gg], v, ACT.Copy).then_inc(v_copied, 1)
            for n, (u, k, lo, hi) in enumerate(work):
                for pair in range(2):
                    m = 2 * n + pair
                    act.wait_ge(scores_ready, m + 1)
                    if n >= 3:
                        act.wait_ge(pv_done, n - 2)
                    act.activation(c.probs8[:, n % 3, 2 * pair:2 * pair + 2, lo * P:hi * P],
                                   c.PS[:, 2 * (m % 2):2 * (m % 2) + 2, lo * P:hi * P], ACT.Exp,
                                   scale=heads.scale).then_inc(probs_ready, 1)
                if u and n == first[u]:
                    act.wait_ge(pv_done, first[u])
                    if u >= 3:
                        act.wait_ge(o_turned, u - 2)
                    act.activation(c.out8[:, (u - 1) % 2, :], c.PS[:, 4 + (u - 1) % 2, :], ACT.Copy
                                   ).then_inc(o_out, 1)
            act.wait_ge(pv_done, len(work))
            act.wait_ge(o_turned, U - 2)
            act.activation(c.out8[:, (U - 1) % 2, :], c.PS[:, 4 + (U - 1) % 2, :], ACT.Copy).then_inc(o_out, 1)

        @block.vector
        def _(dve):
            def divide(u):
                gg, half = units[u]
                dve.wait_ge(o_turned, u + 1)
                if u:
                    dve.wait_ge(out_done, u)
                o = c.PS[:, 4 + u % 2, :].rearrange("p (q h w) -> p q h w", q=QPH, h=4)
                dve.reciprocal(c.rden8[:, u % 2, :, :], o[:, :, :, 8]).then_inc(rden_done, 1)
                dve.wait_ge(rden_done, u + 1)
                out = c.CTX[:, QPH * half:QPH * (half + 1), bass.ds(two * 64 + 32 * gg, 32)].rearrange(
                    "p q (h e) -> p q h e", h=4)
                dve.tensor_tensor(out, o[:, :, :, 0:8], c.rden8[:, u % 2, :, :, None].to_broadcast([P, QPH, 4, 8]),
                                  ALU.mult).then_inc(out_done, 1)

            for u in range(U):
                maxima.reduce(dve, u, rows_ready, rows_read, maxima_done)
                if u:
                    divide(u - 1)
            divide(U - 1)



def mlp(c, target, w1, b1, w2, b2, chunks, gated, batch_weights=False):
    with c.stage("mlp_loaded", "mlp_b_loaded", "up_done", "gelu_done", "hidden_done", "down_done", "mlp_added") as \
            (block, loaded, b_loaded, up, gelu, hidden, down, added):
        n_up = chunks * (2 if gated else 1)
        steps = [(k, h) for k in range(chunks) for h in range(NH)]
        W1, W2 = (c.W1E, c.W2E) if batch_weights else (c.W1, c.W2)

        @block.sync
        def _(sp):
            if not batch_weights:
                sp.dma_start(W1[:, 0:n_up, :], w1).then_inc(loaded, 16)
                sp.dma_start(W2[:, 0:chunks, :], w2).then_inc(loaded, 16)
            sp.dma_start(c.bcols[:, 0:n_up], b1).then_inc(b_loaded, 16)
            sp.dma_start(c.vbias[:, :], b2.partition_broadcast(P)).then_inc(b_loaded, 16)

        @block.tensor
        def _(pe):
            if not batch_weights:
                pe.wait_ge(loaded, 32)
            for n, (k, h) in enumerate(steps):
                if n >= 3:
                    pe.wait_ge(hidden if gated else gelu, n - 2)
                for g in range(2 if gated else 1):
                    mm = pe.matmul(c.PS[:, 2 * (n % 3) + g, :], W1[:, k + g * chunks, :],
                                   c.XT[:, h * HALF:(h + 1) * HALF], start=True, stop=True)
                mm.then_inc(up, 1)
            pe.wait_ge(hidden if gated else gelu, len(steps))
            for t in range(NT):
                for k in range(chunks):
                    mm = pe.matmul(c.tiles(6)[:, t, :], c.HT[:, k, t * P:(t + 1) * P], W2[:, k, :],
                                   start=k == 0, stop=k == chunks - 1)
                mm.then_inc(down, 1)

        @block.scalar
        def _(act):
            act.wait_ge(b_loaded, 32)
            for n, (k, h) in enumerate(steps):
                act.wait_ge(up, n + 1)
                gate = k + chunks * int(gated)
                act.activation(c.HT[:, k, h * HALF:(h + 1) * HALF], c.PS[:, 2 * (n % 3) + int(gated), :],
                               ACT.Gelu, bias=c.bcols[:, gate:gate + 1]).then_inc(gelu, 1)

        @block.vector
        def _(dve):
            dve.wait_ge(b_loaded, 32)
            dve.tensor_tensor(target[:, :, :], target[:, :, :], c.vbias[:, None, :].to_broadcast([P, NT, P]),
                              ALU.add).then_inc(added, 1)
            if gated:
                for n, (k, h) in enumerate(steps):
                    dve.wait_ge(gelu, n + 1)
                    part = c.HT[:, k, h * HALF:(h + 1) * HALF]
                    dve.scalar_tensor_tensor(part, c.PS[:, 2 * (n % 3), :], c.bcols[:, k:k + 1], part,
                                             ALU.add, ALU.mult).then_inc(hidden, 1)
            dve.wait_ge(added, 1)
            for h in range(NH):
                dve.wait_ge(down, (h + 1) * (NT // NH))
                t = slice(h * (NT // NH), (h + 1) * (NT // NH))
                dve.tensor_tensor(target[:, t, :], target[:, t, :], c.tiles(6)[:, t, :], ALU.add).then_inc(added, 1)


def experts(c, w, w2, sel, rows, n_pairs, bias=None, add_tokens=None, add_turned=None):
    routed = bias is None
    ups = 2 if routed else 1
    steps = [(i, h) for i in range(n_pairs) for h in range(NH)]
    sel_bf = c.selb
    with c.stage("pair_loaded", "sel_loaded", "w2_loaded", "bias_loaded", "sel_cast", "w2_cast", "pair_up", "pair_act", "pair_gated",
                 "pair_hidden", "pair_down", "pair_added") as \
            (block, loaded, sel_loaded, w2_loaded, bias_loaded, sel_cast, w2_cast, up, acted, gated, hidden, down, added):
        @block.sync
        def _(sp):
            sp.dma_start((c.EWB if routed else c.EW)[:, 0:n_pairs, 0:ups, :], w).then_inc(loaded, 16)
            sp.dma_start(c.SEL[0:rows, 0:n_pairs, :], sel).then_inc(sel_loaded, 16)
            sp.dma_start((c.EW2B if routed else c.EW2)[:, 0:n_pairs, :], w2).then_inc(w2_loaded, 16)
            if not routed:
                sp.dma_start(c.bcols[:, 0:n_pairs], bias).then_inc(bias_loaded, 16)

        @block.tensor
        def _(pe):
            def ups_of(n):
                i, h = steps[n]
                cols = slice(h * HALF, (h + 1) * HALF)
                if n == 0:
                    pe.wait_ge(loaded, 16)
                if n >= 2:
                    pe.wait_ge(hidden, n - 1)
                for u in range(ups):
                    out = c.PS[:, 3 * (n % 2) + u, :]
                    if routed:
                        for piece in range(3):
                            pe.matmul(out, c.EWB[:, i, u, :], c.QS[:, piece, cols], start=piece == 0, stop=piece == 2)
                    else:
                        pe.matmul(out, c.EW[:, i, u, :], c.XT[:, cols], start=True, stop=True)
                if n == 0:
                    pe.wait_ge(sel_cast, 1)
                pe.matmul(c.PS[:, 3 * (n % 2) + 2, :], sel_bf[0:rows, i, :], c.gatesT[0:rows, cols],
                          start=True, stop=True).then_inc(up, 1)

            def down_of(n):
                i, h = steps[n]
                if n == 0:
                    pe.wait_ge(w2_cast if routed else w2_loaded, 1 if routed else 16)
                pe.wait_ge(hidden, n + 1)
                if add_tokens is not None:
                    for t in range(h * (NT // NH), (h + 1) * (NT // NH)):
                        mm = pe.matmul(c.tiles(6)[:, t, :], c.HT[:, i % 2, t * P:(t + 1) * P], c.EW2[:, i, :],
                                       start=i == 0 and t % (NT // NH) == 0, stop=i == n_pairs - 1,
                                       skip_group_check=True)
                else:
                    mm = pe.matmul(c.PS[:, 6 + h, :], c.EW2[:, i, :], c.HT[:, i % 2, h * HALF:(h + 1) * HALF],
                                   start=i == 0, stop=i == n_pairs - 1)
                mm.then_inc(down, 1)

            for n in range(len(steps)):
                ups_of(n)
                if n:
                    down_of(n - 1)
            down_of(len(steps) - 1)

        @block.scalar
        def _(act):
            if not routed:
                act.wait_ge(bias_loaded, 16)
            for n, (i, h) in enumerate(steps):
                act.wait_ge(up, n + 1)
                if n >= 4:
                    act.wait_ge(down, n - 3)
                part = c.HT[:, i % 2, h * HALF:(h + 1) * HALF]
                if routed:
                    act.activation(part, c.PS[:, 3 * (n % 2), :], ACT.Silu).then_inc(acted, 1)
                else:
                    act.activation(part, c.PS[:, 3 * (n % 2), :], ACT.Relu, bias=c.bcols[:, i:i + 1]).then_inc(acted, 1)

        @block.vector
        def _(dve):
            dve.wait_ge(sel_loaded, 16)
            dve.tensor_copy(sel_bf[0:rows, 0:n_pairs, :], c.SEL[0:rows, 0:n_pairs, :]).then_inc(sel_cast, 1)
            if routed:
                dve.wait_ge(w2_loaded, 16)
                dve.tensor_copy(c.EW2[:, 0:n_pairs, :], c.EW2B[:, 0:n_pairs, :]).then_inc(w2_cast, 1)
            for n, (i, h) in enumerate(steps):
                part = c.HT[:, i % 2, h * HALF:(h + 1) * HALF]
                dve.wait_ge(acted, n + 1)
                if routed:
                    dve.tensor_tensor(part, part, c.PS[:, 3 * (n % 2) + 1, :], ALU.mult).then_inc(gated, 1)
                    dve.wait_ge(gated, n + 1)
                dve.tensor_tensor(part, part, c.PS[:, 3 * (n % 2) + 2, :], ALU.mult).then_inc(hidden, 1)
            for h in range(NH):
                dve.wait_ge(down, len(steps) - NH + h + 1)
                if add_tokens is not None:
                    t = slice(h * (NT // NH), (h + 1) * (NT // NH))
                    dve.tensor_tensor(add_tokens[:, t, :], add_tokens[:, t, :], c.tiles(6)[:, t, :],
                                      ALU.add).then_inc(added, 1)
                else:
                    cols = slice(h * HALF, (h + 1) * HALF)
                    dve.tensor_tensor(add_turned[:, cols], add_turned[:, cols], c.PS[:, 6 + h, :],
                                      ALU.add).then_inc(added, 1)


def some(ap, i, n):
    v = ap[bass.ds(i * n, n)]
    names = "abcd"[:len(v.shape) - 1]
    return v.rearrange(f"z {' '.join(names)} -> {names[0]} z {' '.join(names[1:])}")


def turn_gates(c, rows, exact=False, tokens=True):
    n = 1 if exact else 3
    with c.stage("gate_piece", "gates_turned", "gates_out", "x_piece") as (block, piece, turned, out_done, x_piece):
        out = c.banks(0).bitcast(BF16)

        @block.vector
        def _(dve):
            at = 0

            def next_step(instruction):
                nonlocal at
                instruction.then_inc(piece, 1)
                at += 1
                dve.wait_ge(piece, at)

            g, r = c.gates[:, :, 0:rows], c.gates_rest[:, :, 0:rows]
            pieces = [c.gate_pieces[:, :, i * rows:(i + 1) * rows] for i in range(n)]
            next_step(dve.tensor_copy(pieces[0], g))
            if not exact:
                next_step(dve.tensor_tensor(r, g, pieces[0], ALU.subtract))
                next_step(dve.tensor_copy(pieces[1], r))
                next_step(dve.tensor_tensor(pieces[2], r, pieces[1], ALU.subtract))
            if not exact and tokens:
                x1, x2, x3 = (c.QS[:, i, :] for i in range(3))
                rest = c.HT[:, 0, :]
                dve.tensor_copy(x1, c.XT[:, :]).then_inc(x_piece, 1)
                dve.wait_ge(x_piece, 1)
                dve.tensor_tensor(rest, c.XT[:, :], x1, ALU.subtract).then_inc(x_piece, 1)
                dve.wait_ge(x_piece, 2)
                dve.tensor_copy(x2, rest).then_inc(x_piece, 1)
                dve.wait_ge(x_piece, 3)
                dve.tensor_tensor(x3, rest, x2, ALU.subtract).then_inc(x_piece, 1)

        @block.tensor
        def _(pe):
            pe.wait_ge(piece, 1 if exact else 4)
            for t in range(NT):
                pe.transpose(out[0:n * rows, t * P:(t + 1) * P], c.gate_pieces[:, t, 0:n * rows],
                             c.identb[:, :]).then_inc(turned, 1)

        @block.scalar
        def _(act):
            act.wait_ge(turned, NT)
            act.activation(c.gatesT[0:n * rows, :], out[0:n * rows, 0:S], ACT.Copy).then_inc(out_done, 1)


def route_experts(c, n):
    d = c.dram
    carry = c.carry[n]
    score, biased, left, chosen, weight, room = (c.small[:, k] for k in range(6))
    with c.stage("gw_loaded", "gw_cast", "logits_done", "sigmoid_done", "route_step", "counted",
                 "carry_ready", "carry_done") as \
            (block, loaded, cast_done, logits, sigm, step, counted, carry_ready, carry_done):
        @block.sync
        def _(sp):
            sp.dma_start(c.gate_w[:, :], d["moe_gate"]).then_inc(loaded, 16)
            sp.dma_start(c.ebias[:, :], d["moe_bias"].partition_broadcast(P)).then_inc(loaded, 16)

        @block.gpsimd
        def _(pool):
            pool.wait_ge(loaded, 32)
            pool.tensor_copy(c.W1[:, 0, 0:EXPERTS], c.gate_w[:, :]).then_inc(cast_done, 1)

        @block.tensor
        def _(pe):
            pe.wait_ge(cast_done, 1)
            for t in range(NT):
                mm = pe.matmul(c.PS[:, 0, t * EXPERTS:(t + 1) * EXPERTS], c.XT[:, t * P:(t + 1) * P],
                               c.W1[:, 0, 0:EXPERTS], start=True, stop=True)
            mm.then_inc(logits, 1)
            pe.wait_ge(step, NT + 2 + NT + 1)
            for t in range(NT):
                out = c.PS[:, 1, t * EXPERTS:(t + 1) * EXPERTS]
                pe.matmul(out, c.ones[0:1, 0:P], carry[:, :], start=True, stop=False)
                for s in range(t):
                    pe.matmul(out, c.ones[:, 0:P], chosen[:, s, :], start=False, stop=False)
                pe.matmul(out, c.before[:, :], chosen[:, t, :], start=False, stop=True).then_inc(counted, 1)
            out = c.PS[0:1, 2, 0:EXPERTS]
            pe.matmul(out, c.ones[0:1, 0:1], carry[:, :], start=True, stop=False)
            for s in range(NT):
                mm = pe.matmul(out, c.ones[:, 0:1], chosen[:, s, :], start=False, stop=s == NT - 1)
            mm.then_inc(carry_ready, 1)

        @block.scalar
        def _(act):
            act.wait_ge(logits, 1)
            act.activation(score, c.PS[:, 0, 0:NT * EXPERTS].rearrange("p (t e) -> p t e", e=EXPERTS),
                           ACT.Sigmoid).then_inc(sigm, 1)

        @block.vector
        def _(dve):
            at = 0

            def next_step(instruction):
                nonlocal at
                instruction.then_inc(step, 1)
                at += 1

            dve.wait_ge(sigm, 1)
            dve.wait_ge(loaded, 32)
            next_step(dve.tensor_tensor(biased, score, c.ebias[:, None, :].to_broadcast([P, NT, EXPERTS]), ALU.add))
            dve.wait_ge(step, at)
            for t in range(NT):
                next_step(dve.max(c.small8[:, t, :], biased[:, t, :]))
            dve.wait_ge(step, at)
            next_step(dve.memset(c.small8[:, :, TOPK:8], 3e38))
            dve.wait_ge(step, at)
            for t in range(NT):
                next_step(dve.match_replace(left[:, t, :], c.small8[:, t, :], biased[:, t, :], -3e38))
            dve.wait_ge(step, at)
            next_step(dve.tensor_tensor(chosen, left, biased, ALU.not_equal))
            dve.wait_ge(step, at)
            next_step(dve.tensor_tensor(weight, score, chosen, ALU.mult))
            dve.wait_ge(step, at)
            next_step(dve.tensor_reduce(c.gsum[:, 0, :], weight, AX_X, ALU.add))
            dve.wait_ge(step, at)
            next_step(dve.tensor_scalar(c.gsum[:, 0, :], c.gsum[:, 0, :], 1e-12, None, ALU.max))
            dve.wait_ge(step, at)
            next_step(dve.reciprocal(c.gsum[:, 1, :], c.gsum[:, 0, :]))
            dve.wait_ge(step, at)
            next_step(dve.tensor_tensor(weight, weight, c.gsum[:, 1, :, None].to_broadcast([P, NT, EXPERTS]), ALU.mult))
            dve.wait_ge(counted, NT)
            next_step(dve.tensor_scalar(room, c.PS[:, 1, 0:NT * EXPERTS].rearrange("p (t e) -> p t e", e=EXPERTS),
                                        float(CAPACITY), None, ALU.is_lt))
            dve.wait_ge(step, at)
            next_step(dve.tensor_tensor(c.gates[:, :, 0:EXPERTS], weight, room, ALU.mult))
            next_step(dve.memset(c.gates[:, :, EXPERTS:EXPERTS + 1], 1.0))
            next_step(dve.memset(c.gates[:, :, EXPERTS + 1:EXPERTS + 2], 0.0))
            dve.wait_ge(carry_ready, 1)
            dve.tensor_copy(carry[:, :], c.PS[0:1, 2, 0:EXPERTS]).then_inc(carry_done, 1)
    turn_gates(c, GATE_ROWS)


def route_leaves(c, node_w, node_b):
    yes, no = c.small[:, 0, :, 0:LEAVES], c.small[:, 1, :, 0:LEAVES]
    with c.stage("nodes_loaded", "nodes_done", "tree_step") as (block, loaded, nodes, step):
        @block.sync
        def _(sp):
            sp.dma_start(c.W1[:, 0, 0:LEAVES - 1], node_w).then_inc(loaded, 16)
            sp.dma_start(c.node_bias[:, :], node_b.partition_broadcast(P)).then_inc(loaded, 16)

        @block.tensor
        def _(pe):
            pe.wait_ge(loaded, 32)
            for t in range(NT):
                out = c.PS[:, 0, t * LEAVES:t * LEAVES + LEAVES - 1]
                mm = pe.matmul(out, c.XT[:, t * P:(t + 1) * P], c.W1[:, 0, 0:LEAVES - 1], start=True, stop=True)
            mm.then_inc(nodes, 1)

        @block.vector
        def _(dve):
            at = 0

            def next_step(instruction):
                nonlocal at
                instruction.then_inc(step, 1)
                at += 1

            dve.wait_ge(nodes, 1)
            score = c.PS[:, 0, 0:NT * LEAVES].rearrange("p (t e) -> p t e", e=LEAVES)[:, :, 0:LEAVES - 1]
            dve.wait_ge(loaded, 32)
            next_step(dve.tensor_tensor(yes[:, :, 0:LEAVES - 1], score,
                                        c.node_bias[:, None, :].to_broadcast([P, NT, LEAVES - 1]), ALU.add))
            dve.wait_ge(step, at)
            next_step(dve.tensor_scalar(yes[:, :, 0:LEAVES - 1], yes[:, :, 0:LEAVES - 1], 0.0, None, ALU.is_ge))
            dve.wait_ge(step, at)
            next_step(dve.tensor_scalar(no[:, :, 0:LEAVES - 1], yes[:, :, 0:LEAVES - 1], -1.0, 1.0, ALU.mult, ALU.add))
            dve.wait_ge(step, at)
            path = c.small[:, 2, :, 0:2]
            next_step(dve.tensor_copy(path[:, :, 0:1], no[:, :, 0:1]))
            next_step(dve.tensor_copy(path[:, :, 1:2], yes[:, :, 0:1]))
            n, k = 2, 3
            while n < LEAVES:
                dve.wait_ge(step, at)
                wide = c.small[:, k, :, 0:2 * n] if 2 * n < LEAVES else c.gates[:, :, 0:LEAVES]
                split = wide.rearrange("p t (i s) -> p t i s", s=2)
                next_step(dve.tensor_tensor(split[:, :, :, 0], path, no[:, :, n - 1:2 * n - 1], ALU.mult))
                next_step(dve.tensor_tensor(split[:, :, :, 1], path, yes[:, :, n - 1:2 * n - 1], ALU.mult))
                path, n, k = wide, 2 * n, k + 1
    turn_gates(c, LEAVES, exact=True)


def leaf_bias(c, b2, turned=None, tokens=None):
    with c.stage("b2_loaded", "gates_wide", "b2_done", "b2_out") as (block, loaded, wide, done, out_done):
        b2s = c.SEL[0:LEAVES, 0, :]

        @block.sync
        def _(sp):
            sp.dma_start(b2s, b2).then_inc(loaded, 16)

        @block.tensor
        def _(pe):
            pe.wait_ge(loaded, 16)
            pe.wait_ge(wide, 1)
            if turned is not None:
                for h in range(NH):
                    mm = pe.matmul(c.PS[:, h, :], b2s, c.T1[0:LEAVES, h * HALF:(h + 1) * HALF], start=True, stop=True)
            else:
                for t in range(NT):
                    mm = pe.matmul(c.tiles(0)[:, t, :], c.T1[0:LEAVES, t * P:(t + 1) * P], b2s, start=True, stop=True)
            mm.then_inc(done, 1)

        @block.vector
        def _(dve):
            dve.tensor_copy(c.T1[0:LEAVES, :], c.gatesT[0:LEAVES, :]).then_inc(wide, 1)

        @block.scalar
        def _(act):
            act.wait_ge(done, 1)
            if turned is not None:
                act.activation(turned[:, :], c.banks(0), ACT.Copy).then_inc(out_done, 1)
            else:
                act.activation(tokens, c.tiles(0), ACT.Copy).then_inc(out_done, 1)


def shorten_q_k(c, keys=S):
    with c.stage("short_q", "short_k") as (block, short_q, short_k):
        @block.scalar
        def _(act):
            act.activation(c.QB[:, :], c.QT[:, :], ACT.Copy).then_inc(short_q, 1)

        @block.vector
        def _(dve):
            dve.tensor_copy(c.KB[:, 0:keys], c.KT[:, 0:keys]).then_inc(short_k, 1)


def whole_out(c):
    return lambda h, half: c.CTX[:, 4 * half:4 * half + 4, :]



def local_transformer(c):
    d = c.dram
    norm_and_turn(c, c.X, norm=c.Y)
    for layer in range(2):
        norm_and_turn(c, c.Y, shift=True)
        head_norms(c, d["l0f_wqk"][layer], d["l0f_scales"][layer])
        attention64(c, c.Y, d["l0f_w"][layer], d["l0f_wo"][layer], 4, "window", 8.0, xpos=c.xpos, sel=d["c_sel48"])
        shift_tokens(c, c.Y)
        norm_and_turn(c, c.H, norm=c.CTX, gains=d["l0f_ln"][layer])
        mlp(c, c.Y, d["l0f_w1"][layer], d["l0f_b1"][layer], d["l0f_w2"][layer], d["l0f_b2"][layer], 3, True)
    add_to(c, c.X, c.Y[:, :, :])


def mixture(c, n):
    d = c.dram
    norm_and_turn(c, c.X, norm=c.Y)
    route_experts(c, n)
    rows = 3 * GATE_ROWS
    with c.nc.Fori(0, EXPERTS // 8) as i:
        experts(c, some(d["moe_w"], i, 4), some(d["moe_w2"], i, 4), some(d["c_sel34"], i, 4), rows, 4, add_tokens=c.X)
    shared = GATE_ROWS // 2 - 1
    experts(c, some(d["moe_w"], shared, 1), some(d["moe_w2"], shared, 1), some(d["c_sel34"], shared, 1), rows, 1,
            add_tokens=c.X)


def transformer_block(c):
    d = c.dram
    norm_and_turn(c, c.X, norm=c.Y)
    norm_and_turn(c, c.Y, norm=c.H, gains=d["l1b_ln1"])
    attention8(c, d["l1b_w"], (d["l1b_b"], d["l1b_bv"]), "causal", rope=c.rope8)
    project_out(c, c.Y, d["l1b_wo"], d["l1b_bo"])
    norm_and_turn(c, c.Y, norm=c.H, gains=d["l1b_ln2"])
    mlp(c, c.Y, d["l1b_w1"], d["l1b_b1"], d["l1b_w2"], d["l1b_b2"], 4, False)
    add_to(c, c.X, c.Y[:, :, :])


def adapted_mlp(c):
    d = c.dram
    norm_and_turn(c, c.X, norm=c.Y)
    with c.stage("lora_loaded", "lora_scaled", "lora_rows", "lora_sum") as (block, loaded, scaled, rows, summed):
        @block.sync
        def _(sp):
            sp.dma_start(c.W1[:, 0:4, :], d["l2f_w1"]).then_inc(loaded, 16)
            sp.dma_start(c.W2[:, :, :], d["l2f_w2"]).then_inc(loaded, 16)
            sp.dma_start(c.odd[:, 8:9], d["l2f_scale"].partition_broadcast(P)).then_inc(loaded, 16)

        @block.tensor
        def _(pe):
            for j in range(8):
                pe.matmul(c.tiles(0)[:, j, :], c.pick8[:, j, :], c.Y[:, 0, :], start=True, stop=True).then_inc(rows, 1)

        @block.vector
        def _(dve):
            dve.wait_ge(loaded, 48)
            dve.tensor_scalar(c.odd[:, 0:8], c.XT[:, 2:18:2], c.odd[:, 8:9], None, ALU.mult).then_inc(scaled, 1)
            dve.wait_ge(scaled, 1)
            dve.wait_ge(rows, 8)
            for j in range(4):
                dve.scalar_tensor_tensor(c.W1E[:, j, :], c.tiles(0)[:, j, :], c.odd[:, j:j + 1], c.W1[:, j, :],
                                         ALU.mult, ALU.add).then_inc(summed, 1)
            for j in range(4):
                for r in range(4):
                    dve.scalar_tensor_tensor(c.W2E[:, r, 32 * j:32 * j + 32],
                                             c.tiles(0)[:, 4 + j, r:P:4], c.odd[:, 4 + j:5 + j],
                                             c.W2[:, r, 32 * j:32 * j + 32],
                                             ALU.mult, ALU.add).then_inc(summed, 1)
    mlp(c, c.X, None, d["l2f_b1"], None, d["l2f_b2"], 4, False, batch_weights=True)


def single_head(c):
    heads = Heads(P, 1, P, P ** -0.5, "causal")
    norm_and_turn(c, c.X, norm=c.Y)
    clear_v(c)
    project(c, c.dram["l2a_w"], heads, bias=(c.dram["l2a_b"], c.dram["l2a_bv"]))
    attend(c, heads, whole_out(c))
    add_to(c, c.X, c.CTX[:, :, :])


def cross_attention(c):
    d = c.dram
    keys = 512
    heads = Heads(P, 1, P, 1.0, "full", keys=keys)
    norm_and_turn(c, c.X, norm=c.Y)
    clear_v(c)
    with c.stage("kv_loaded", "v_in", "k_scaled", "k_turned", "k_out") as (block, loaded, v_in, k_scaled, turned, k_out):
        @block.sync
        def _(sp):
            sp.dma_start(c.W1[:, 0:4, :], d["l3a_k"].rearrange("(t p) d -> p t d", p=P)).then_inc(loaded, 16)
            sp.dma_start(c.VA[:, 0:4, 0:P], d["l3a_v"].rearrange("(t p) d -> p t d", p=P)).then_inc(v_in, 16)
            sp.wait_ge(v_in, 16)

        @block.vector
        def _(dve):
            dve.wait_ge(loaded, 16)
            for t in range(4):
                dve.tensor_scalar(c.W1E[:, t, :], c.W1[:, t, :], c.XT[:, 256 * t:256 * t + 1], None,
                                  ALU.mult).then_inc(k_scaled, 1)

        @block.tensor
        def _(pe):
            for t in range(4):
                pe.wait_ge(k_scaled, t + 1)
                pe.transpose(c.PS[:, 0, t * P:(t + 1) * P], c.W1E[:, t, :], c.ident[:, :]).then_inc(turned, 1)

        @block.scalar
        def _(act):
            act.activation(c.QT[:, :], c.XT[:, :], ACT.Copy).then_inc(k_out, 1)
            act.wait_ge(turned, 4)
            act.activation(c.KT[:, 0:keys], c.PS[:, 0, :], ACT.Copy).then_inc(k_out, 1)
    shorten_q_k(c, keys)
    attend(c, heads, whole_out(c))
    add_to(c, c.X, c.CTX[:, :, :])


def tree_attention(c):
    d = c.dram
    heads = Heads(P, 1, P, P ** -0.5, "full")
    norm_and_turn(c, c.X, norm=c.Y)
    clear_v(c)
    for name, turned in (("q", c.QT), ("k", c.KT), ("v", None)):
        tokens = None if turned is not None else c.VA[:, :, 0:P]
        route_leaves(c, d[f"l3f_{name}_node"], d[f"l3f_{name}_nodeb"])
        leaf_bias(c, d[f"l3f_{name}_b2"], turned, tokens)
        with c.nc.Fori(0, LEAVES // 8) as i:
            experts(c, some(d[f"l3f_{name}_w1"], i, 4), some(d[f"l3f_{name}_w2"], i, 4), some(d["c_sel16"], i, 4), LEAVES,
                    4, bias=one(d[f"l3f_{name}_b1"], i), add_tokens=tokens, add_turned=turned)
    shorten_q_k(c)
    attend(c, heads, whole_out(c))
    add_to(c, c.X, c.CTX[:, :, :])


def latent_attention(c):
    d = c.dram
    norm_and_turn(c, c.X, norm=c.Y)
    with c.stage("lat_loaded", "lat_mm", "lat_out") as (block, loaded, mm_done, out_done):
        dq, uqT, dkv = (c.W1[0:64, s, :] for s in (0, 1, 3))
        uk, uv = c.W1[:, 2, 0:64], c.W1[:, 4, 0:64]
        woT = c.W1[:, 5, :]
        aT, keT, veT = c.W2[:, 0, :], c.W2[0:64, 1, :], c.W2[0:64, 2, :]

        @block.sync
        def _(sp):
            for dst, src in ((dq, "dq"), (uqT, "uqT"), (dkv, "dkv"), (uk, "uk"), (uv, "uv"), (woT, "woT")):
                sp.dma_start(dst, d[f"l3b_{src}"]).then_inc(loaded, 16)

        @block.tensor
        def _(pe):
            pe.wait_ge(loaded, 96)
            pe.matmul(c.PS[:, 0, 0:P], uqT, dq, start=True, stop=True).then_inc(mm_done, 1)
            pe.matmul(c.PS[0:64, 1, 0:P], uv, woT, start=True, stop=True).then_inc(mm_done, 1)
            pe.matmul(c.PS[:, 2, 0:P], dq, uqT, start=True, stop=True).then_inc(mm_done, 1)
            pe.wait_ge(out_done, 1)
            pe.matmul(c.PS[0:64, 3, 0:P], uk, aT, start=True, stop=True).then_inc(mm_done, 1)
            pe.wait_ge(out_done, 3)
            pe.matmul(c.PS[:, 4, 0:P], dkv, keT, start=True, stop=True).then_inc(mm_done, 1)
            pe.matmul(c.PS[:, 5, 0:P], dkv, veT, start=True, stop=True).then_inc(mm_done, 1)

        @block.vector
        def _(dve):
            dve.wait_ge(mm_done, 1)
            dve.tensor_copy(aT, c.PS[:, 0, 0:P]).then_inc(out_done, 1)
            dve.wait_ge(mm_done, 2)
            dve.tensor_copy(veT, c.PS[0:64, 1, 0:P]).then_inc(out_done, 1)
            dve.wait_ge(mm_done, 4)
            dve.tensor_copy(keT, c.PS[0:64, 3, 0:P]).then_inc(out_done, 1)
            dve.wait_ge(mm_done, 6)
            for s, bank in enumerate((2, 4, 5)):
                dve.tensor_copy(c.W[:, s, :], c.PS[:, bank, 0:P]).then_inc(out_done, 1)
    attention8(c, None, None, "causal")
    add_to(c, c.X, c.CTX[:, :, :])


def network(nc, dram):
    with ExitStack() as ctx:
        c = Core(nc, ctx, dram)
        d = dram
        load_constants(c)

        def gqa():
            norm_and_turn(c, c.X, norm=c.Y)
            attention64(c, c.X, d["l0a_w"], d["l0a_wo"], 8, "causal", 0.125, rope=c.rope64)

        def mha():
            norm_and_turn(c, c.X, norm=c.Y)
            with c.stage("wo_loaded") as (block, loaded):
                @block.sync
                def _(sp):
                    sp.dma_start(c.wrows, d["l0b_wo"]).then_inc(loaded, 16)
                    sp.wait_ge(loaded, 16)
            attention64(c, None, d["l0b_w"], None, 8, "full", 0.125)

        def small_full():
            norm_and_turn(c, c.X, norm=c.Y)
            attention8(c, d["l1a_w"], (d["l1a_b"], d["l1a_bv"]), "full")
            project_out(c, c.X, d["l1a_wo"], d["l1a_bo"])

        def small_causal():
            norm_and_turn(c, c.X, norm=c.Y)
            attention8(c, d["l2b_w"], (d["l2b_b"], d["l2b_bv"]), "causal")
            project_out(c, c.X, d["l2b_wo"], d["l2b_bo"])

        layers = [gqa, lambda: local_transformer(c), mha, lambda: local_transformer(c),
                  small_full, lambda: mixture(c, 0), lambda: transformer_block(c), lambda: mixture(c, 1),
                  lambda: single_head(c), lambda: adapted_mlp(c), small_causal, lambda: adapted_mlp(c),
                  lambda: cross_attention(c), lambda: tree_attention(c), lambda: latent_attention(c),
                  lambda: tree_attention(c)]
        with nc.Fori(0, 2) as b:
            load_x(c, b)
            for layer in layers:
                layer()
            store_x(c, b)



def constants():
    f = np.float32
    i = np.arange(P)
    q, k = i[:, None], i[None, :]
    causal = np.where(k > q, f(NEG), f(0))
    old = np.where(q + P - k > 64, f(NEG), f(0))
    near = np.where((k > q) | (q - k > 64), f(NEG), f(0))
    out = {"c_ident": np.eye(P, dtype=f), "c_before": (q < k).astype(f),
           "c_block1": (q // 64 == k // 64).astype(f)}
    out["c_masks"] = np.stack([causal, causal.T, near, near.T, old, old.T], 1).astype(f)
    out["c_first"] = np.zeros((P, 3, P), f)
    for n, pitch in enumerate((32, 64, 128)):
        out["c_first"][::pitch, n] = 1
    pick = np.zeros((P, 8, P), f)
    for j in range(8):
        pick[1 + 2 * j, j, :] = 1
    out["c_pick8"] = pick
    out["c_coef64"] = np.stack([i >= 64, -(i >= 64).astype(f), -(i < 64).astype(f)], 1).astype(f)
    t = np.arange(S, dtype=f)

    def frequencies(dim):
        return (f(1) / np.power(f(10000), np.arange(0, dim, 2, dtype=f) / f(dim))).astype(f)

    fr = t[None, :] * frequencies(64)[:, None]
    cos, sin = np.cos(fr), np.sin(fr)
    out["c_rope64"] = np.stack([np.tile(cos, (4, 1)), np.concatenate([-sin, sin] * 2)], 1).astype(f)
    base = ((np.arange(0, 64, 2, dtype=f) + f(0.4 * 64)) / f(1.4 * 64)).astype(f)
    power = ((t - f(S // 2)) / f(32)).astype(f)
    scale = np.power(base[:, None], power[None, :]).astype(f)
    out["c_xpos"] = np.stack([np.tile(cos * scale, (4, 1)), np.concatenate([-sin * scale, sin * scale] * 2),
                              np.tile(cos / scale, (4, 1)), np.concatenate([-sin / scale, sin / scale] * 2)],
                             1).astype(f)
    fr8 = t[None, :] * frequencies(8)[:, None]
    rope8 = np.zeros((16, 8, 2, S), f)
    rope8[:, :, 0] = np.tile(np.cos(fr8), (2, 1))
    rope8[:, :, 1] = np.concatenate([-np.sin(fr8), np.sin(fr8)])
    out["c_rope8"] = rope8.reshape(P, 2, S)
    sel = np.zeros((6, 3, 16, 4, P), f)
    for pair in range(4):
        for item in range(4):
            sel[pair, :, 8 * (item % 2) + 2 * pair + item // 2, item] = 1
    out["c_sel48"] = sel.reshape(6, 48, 4, P)
    for name, rows in (("c_sel34", GATE_ROWS), ("c_sel16", LEAVES)):
        pieces = 3 if rows == GATE_ROWS else 1
        sel = np.zeros((rows // 2, pieces, rows, P), f)
        for n in range(rows // 2):
            sel[n, :, 2 * n, 0:64] = 1
            sel[n, :, 2 * n + 1, 64:P] = 1
        out[name] = sel.reshape(rows // 2, pieces * rows, P)
    return out


def swap_halves(w, dim):
    lead = w.shape[:-1]
    v = w.reshape(*lead, -1, 2, dim // 2)
    return v[..., ::-1, :].reshape(w.shape)


def by_pairs(parts, n_pairs):
    return np.ascontiguousarray(np.stack([w.reshape(w.shape[0], n_pairs, P) for w in parts], 2).transpose(1, 0, 2, 3))


def doubled_pairs(parts, v, n_pairs):
    out = np.zeros((n_pairs, P, 2 * len(parts) + 1, P), v.dtype)
    sides = out[:, :, 0:-1].reshape(n_pairs, P, 2, len(parts), 2, 64)
    for s, w in enumerate(parts):
        sides[:, :, :, s] = w.reshape(P, n_pairs, 2, 1, 64).transpose(1, 0, 2, 3, 4)
    out[:, :, 0:-1] = sides.reshape(n_pairs, P, 2 * len(parts), P)
    out[:, :, -1] = v.reshape(P, n_pairs, P).transpose(1, 0, 2)
    return np.concatenate([out, np.zeros_like(out[0:2])])


def by_chunks(w, n):
    return np.ascontiguousarray(w.reshape(n, P, w.shape[-1]).transpose(1, 0, 2))


def layouts(a):
    d = {"x": a["L0_attn_a_x"]}

    def small_biases(name, q_k, v):
        d[name], d[name + "v"] = np.stack(q_k, 1), v

    def doubled(w):
        return np.broadcast_to(w.reshape(P, 4, 1, 64), (P, 4, 4, 64)).reshape(P, 1024)

    q, k, v = a["L0_attn_a_wq"], doubled(a["L0_attn_a_wk"]), doubled(a["L0_attn_a_wv"])
    d["l0a_w"] = doubled_pairs([q, swap_halves(q, 64), k, swap_halves(k, 64)], v, 8)
    d["l0a_wo"] = a["L0_attn_a_wo"].reshape(8, P, P)
    w = a["L0_attn_b_W_qkv"]
    d["l0b_w"] = doubled_pairs([w[:, 0:1024], w[:, 1024:2048]], w[:, 2048:], 8)
    d["l0b_wo"] = np.concatenate([a["L0_attn_b_W_out"].reshape(16, 64, P).transpose(1, 0, 2)] * 2)

    stacks = {"w": [], "wqk": [], "wo": [], "scales": [], "ln": [], "w1": [], "b1": [], "w2": [], "b2": []}
    hid = a["L0_ffn_w2"].shape[1]
    for n in range(2):
        w = a["L0_ffn_wqkv"][n]
        q, k, v = w[:, 0:512], w[:, 512:1024], w[:, 1024:]
        stacks["w"].append(doubled_pairs([q, swap_halves(q, 64), k, swap_halves(k, 64)], v, 4))
        stacks["wqk"].append(w[:, 0:1024])
        stacks["wo"].append(a["L0_ffn_wo"][n].reshape(4, P, P))
        qs, ks = a["L0_ffn_q_scale"][n], a["L0_ffn_k_scale"][n]
        stacks["scales"].append(np.stack([np.tile(s, 2) for s in (qs, swap_halves(qs, 64), ks, swap_halves(ks, 64))], 1))
        stacks["ln"].append(np.stack([a["L0_ffn_ln_g"][n], a["L0_ffn_ln_b"][n]], 1))
        w1 = np.zeros((P, 2, 3 * P), np.float32)
        w1[:, :, 0:hid] = a["L0_ffn_w1"][n].reshape(P, 2, hid)
        b1 = np.zeros((1, 2, 3 * P), np.float32)
        b1[:, :, 0:hid] = a["L0_ffn_b1"][n].reshape(1, 2, hid)
        w2 = np.zeros((3 * P, P), np.float32)
        w2[0:hid] = a["L0_ffn_w2"][n]
        stacks["w1"].append(w1.reshape(P, 6, P))
        stacks["b1"].append(b1.reshape(6, P).T)
        stacks["w2"].append(by_chunks(w2, 3))
        stacks["b2"].append(a["L0_ffn_b2"][n])
    for name, parts in stacks.items():
        d[f"l0f_{name}"] = np.stack(parts)

    def thirds(w):
        return [w[..., 0:128], w[..., 128:256], w[..., 256:384]]

    d["l1a_w"] = np.stack(thirds(a["L1_attn_a_w_qkv"]), 1)
    q, k, v = thirds(a["L1_attn_a_b_qkv"])
    small_biases("l1a_b", [q, k], v)
    d["l1a_wo"], d["l1a_bo"] = a["L1_attn_a_w_proj"], a["L1_attn_a_b_proj"]
    q, k, v = thirds(a["L1_attn_b_Wqkv"])
    d["l1b_w"] = np.stack([q, swap_halves(q, 8), k, swap_halves(k, 8), v], 1)
    q, k, v = thirds(a["L1_attn_b_bqkv"])
    small_biases("l1b_b", [q, swap_halves(q, 8), k, swap_halves(k, 8)], v)
    d["l1b_wo"], d["l1b_bo"] = a["L1_attn_b_Wo"], a["L1_attn_b_bo"]
    d["l1b_ln1"] = np.stack([a["L1_attn_b_ln1_g"], a["L1_attn_b_ln1_b"]], 1)
    d["l1b_ln2"] = np.stack([a["L1_attn_b_ln2_g"], a["L1_attn_b_ln2_b"]], 1)
    d["l1b_w1"], d["l1b_b1"] = a["L1_attn_b_W1"].reshape(P, 4, P), a["L1_attn_b_b1"].reshape(4, P).T
    d["l1b_w2"], d["l1b_b2"] = by_chunks(a["L1_attn_b_W2"], 4), a["L1_attn_b_b2"]

    dt = a["L1_ffn_W1"].dtype
    w = np.zeros((GATE_ROWS, P, 2, 64), dt)
    w[0:EXPERTS, :, 0], w[0:EXPERTS, :, 1] = a["L1_ffn_W1"], a["L1_ffn_W3"]
    w[EXPERTS, :, 0], w[EXPERTS, :, 1] = a["L1_ffn_sw1"].T, a["L1_ffn_sw3"].T
    d["moe_w"] = np.ascontiguousarray(w.reshape(GATE_ROWS // 2, 2, P, 2, 64).transpose(0, 2, 3, 1, 4)
                                      ).reshape(GATE_ROWS // 2, P, 2, P)
    w2 = np.zeros((GATE_ROWS, 64, P), dt)
    w2[0:EXPERTS], w2[EXPERTS] = a["L1_ffn_W2"], a["L1_ffn_sw2"].T
    d["moe_w2"] = w2.reshape(GATE_ROWS // 2, P, P)
    d["moe_gate"] = a["L1_ffn_gate_w"].T
    d["moe_bias"] = a["L1_ffn_bias"].reshape(EXPERTS)

    d["l2a_w"] = np.stack([a[f"L2_attn_a_W{s}"].T for s in "qkv"], 1)
    d["l2a_b"] = np.stack([a[f"L2_attn_a_b{s}"] for s in "qk"], 1)
    d["l2a_bv"] = a["L2_attn_a_bv"]
    d["l2b_w"] = np.stack([a[f"L2_attn_b_W{s}"] for s in "qkv"], 1)
    small_biases("l2b_b", [a["L2_attn_b_bq"], a["L2_attn_b_bk"]], a["L2_attn_b_bv"])
    d["l2b_wo"], d["l2b_bo"] = a["L2_attn_b_Wo"], a["L2_attn_b_bo"]
    d["l2f_w1"], d["l2f_b1"] = a["L2_ffn_W1"].T.reshape(P, 4, P), a["L2_ffn_b1"].reshape(4, P).T
    d["l2f_w2"], d["l2f_b2"] = by_chunks(a["L2_ffn_W2"].T, 4), a["L2_ffn_b2"]
    d["l2f_scale"] = a["L2_ffn_scale"].reshape(1)

    d["l3a_k"], d["l3a_v"] = a["L3_attn_a_k"][0], a["L3_attn_a_v"][0]
    for s in "qkv":
        d[f"l3f_{s}_node"], d[f"l3f_{s}_nodeb"] = a[f"L3_ffn_{s}_node_w"].T, a[f"L3_ffn_{s}_node_b"]
        d[f"l3f_{s}_w1"] = np.ascontiguousarray(a[f"L3_ffn_{s}_w1"].reshape(8, 2, P, 64).transpose(0, 2, 1, 3)
                                                ).reshape(8, P, 1, P)
        d[f"l3f_{s}_b1"] = a[f"L3_ffn_{s}_b1"].reshape(2, 4, P).transpose(0, 2, 1)
        d[f"l3f_{s}_w2"] = a[f"L3_ffn_{s}_w2"].reshape(8, P, P)
        d[f"l3f_{s}_b2"] = a[f"L3_ffn_{s}_b2"]
    for s in ("dq", "dkv", "uk", "uv"):
        d[f"l3b_{s}"] = a[f"L3_attn_b_W_{s}"]
    d["l3b_uqT"], d["l3b_woT"] = a["L3_attn_b_W_uq"].T, a["L3_attn_b_W_o"].T
    return d


def kernel(**inputs):
    import concourse.bacc as _bacc
    from concourse.bass_utils import run_bass_kernel_spmd as _run

    nc = _bacc.Bacc("TRN2", target_bir_lowering=False, num_devices=1)
    arrays, dram = {}, {}
    for name, value in {**layouts({k: np.asarray(v) for k, v in inputs.items()}), **constants()}.items():
        value = np.ascontiguousarray(value)
        arrays[f"in_{name}"] = value
        dram[name] = nc.dram_tensor(f"in_{name}", value.shape, mybir.dt.from_np(value.dtype), kind="ExternalInput").ap()
    dram["q_pieces"] = nc.dram_tensor("q_pieces_by_piece", (3, 16, 8, S), BF16).ap()
    dram["k_pieces"] = nc.dram_tensor("k_pieces_by_head", (16, 3, 8, S), BF16).ap()
    dram["out"] = nc.dram_tensor("out", (2, S, P), F32, kind="ExternalOutput").ap()
    network(nc, dram)
    return _run(nc, [arrays], core_ids=[0]).results[0]["out"]
```
